# Optimizing a Trainium2 kernel written in Bass

```python
import numpy as np
import jax
import jax.numpy as jnp

def _softmax(x, axis=-1):
    return jax.nn.softmax(x, axis=axis)

def _gelu(x):
    return jax.nn.gelu(x, approximate=True)

def _silu(x):
    return jax.nn.silu(x)

def _sigmoid(x):
    return jax.nn.sigmoid(x)

def _layernorm(x, axis=-1, eps=1e-05):
    m = jnp.mean(x, axis=axis, keepdims=True)
    v = jnp.var(x, axis=axis, keepdims=True)
    return (x - m) / jnp.sqrt(v + eps)

def _scatter_add(tgt, idx, src, axis=0):
    return tgt.at[idx].add(src)

def _segment_sum(src, seg, n):
    return jax.ops.segment_sum(src, seg, n)
kernel_name = 'mk_decoder_preln_d1_seqx_r4_4b78f9'

def setup_inputs(seed: int=0):
    np.random.seed(seed)
    _w = jnp.asarray

    def _rec_inputs():
        import jax
        import jax.numpy as jnp
        _rk = jax.random.key(seed)
        x = 7.22e-05 + 1 * jax.random.normal(jax.random.fold_in(_rk, 1), (4, 512, 512), jnp.float32)
        _lenS = 512 - jax.random.randint(jax.random.fold_in(_rk, 7), (4,), 0, max(1, 512 // 4) + 1, jnp.int32)
        _lenS2 = 512 - jax.random.randint(jax.random.fold_in(_rk, 8), (4,), 0, max(1, 512 // 4) + 1, jnp.int32)
        _ctx_1024P = jax.random.normal(jax.random.fold_in(_rk, 11), (4, 16, 256), jnp.float32)
        _ctx_1024c = jax.random.dirichlet(jax.random.fold_in(_rk, 511), 0.3 * jnp.ones((16,), jnp.float32), (4, 512))
        _ctx_1024t = jnp.einsum('bsk,bkd->bsd', _ctx_1024c, _ctx_1024P)
        _ctx_1024t = _ctx_1024t * jax.lax.rsqrt(jnp.mean(jnp.square(_ctx_1024t)) + 1e-12) * 0.953939
        ctx_1024 = 2.81802e-05 + 1.00001 * (_ctx_1024t + 0.3 * jax.random.normal(jax.random.fold_in(_rk, 611), (4, 512, 256), jnp.float32))
        return (x, ctx_1024)
    x, ctx_1024 = _rec_inputs()

    def _L0_attn_setup():
        import jax, jax.numpy as jnp
        import numpy as np
        EMBED_DIM = 512
        NUM_HEADS = 16
        BLOCK_SIZE = 128

        def _flash_attention_v2(q, k, v, block_size, scale):
            B, H, S, D = q.shape
            nb = S // block_size
            qb = q.reshape(B, H, nb, block_size, D)
            kb = k.reshape(B, H, nb, block_size, D).transpose(2, 0, 1, 3, 4)
            vb = v.reshape(B, H, nb, block_size, D).transpose(2, 0, 1, 3, 4)
            out0 = jnp.zeros_like(qb)
            l0 = jnp.zeros((B, H, nb, block_size, 1), dtype=q.dtype)
            m0 = jnp.full((B, H, nb, block_size, 1), -jnp.inf, dtype=q.dtype)

            def step(carry, kv):
                out, l, m = carry
                k_j, v_j = kv
                s = jnp.einsum('bhnqd,bhkd->bhnqk', qb, k_j) * scale
                m_ij = jnp.max(s, axis=-1, keepdims=True)
                p = jnp.exp(s - m_ij)
                l_ij = jnp.sum(p, axis=-1, keepdims=True)
                m_new = jnp.maximum(m, m_ij)
                alpha = jnp.exp(m - m_new)
                beta = jnp.exp(m_ij - m_new)
                l_new = alpha * l + beta * l_ij
                pv = jnp.einsum('bhnqk,bhkd->bhnqd', p, v_j)
                out_new = alpha * l / l_new * out + beta * l_ij / l_new * pv
                return ((out_new, l_new, m_new), None)
            (out, _, _), _ = jax.lax.scan(step, (out0, l0, m0), (kb, vb))
            return out.reshape(B, H, S, D)
        key = jax.random.key(seed)
        k1, k2, k3 = jax.random.split(key, 3)
        B, S, E = (2, 1024, EMBED_DIM)
        x = jax.random.normal(k1, (B, S, E), dtype=jnp.float32)
        w_qkv = jax.random.normal(k2, (3 * E, E), dtype=jnp.float32) * 0.02
        w_out = jax.random.normal(k3, (E, E), dtype=jnp.float32) * 0.02
        b_out = jnp.zeros((E,), dtype=jnp.float32)
        return {'x': x, 'w_qkv': w_qkv, 'w_out': w_out, 'b_out': b_out}
    _L0_attn_all = _L0_attn_setup()
    _L0_attn_in = {k: v for k, v in _L0_attn_all.items() if k in ('w_qkv', 'w_out', 'b_out')}
    del _L0_attn_all

    def _L0_xattn_setup():
        import jax, jax.numpy as jnp
        import numpy as np
        key = jax.random.key(seed)
        ks = jax.random.split(key, 6)
        B, L, N, C, D = (8, 128, 512, 256, 128)
        return {'teacher_logits': jax.random.normal(ks[0], (B, L, N), dtype=jnp.float32), 'teacher_features': jax.random.normal(ks[1], (B, N, C), dtype=jnp.float32), 'Wq': jax.random.normal(ks[2], (D, C), dtype=jnp.float32) * (1.0 / np.sqrt(C)), 'bq': jnp.zeros((D,), dtype=jnp.float32), 'Wk': jax.random.normal(ks[3], (D, C), dtype=jnp.float32) * (1.0 / np.sqrt(C)), 'bk': jnp.zeros((D,), dtype=jnp.float32)}
    _L0_xattn_all = _L0_xattn_setup()
    _L0_xattn_in = {k: v for k, v in _L0_xattn_all.items() if k in ('Wq', 'bq', 'Wk', 'bk')}
    del _L0_xattn_all

    def _L0_ffn_setup():
        import jax, jax.numpy as jnp
        import numpy as np
        import math
        GOLDEN_CENTER = 1.0 / math.e
        GOLDEN_LOWER = 0.5 - math.log(4.0 / 3.0)
        GOLDEN_UPPER = 0.5
        B, T, D = (4, 256, 512)
        E = 8
        F = 2048 // (E // 2)
        R = 64
        NL = 2

        def _router_weights(x, Wr, temperature):
            logits = jnp.einsum('btd,de->bte', x, Wr)
            inhibition = jax.nn.sigmoid(logits / temperature)
            in_zone = (inhibition >= GOLDEN_LOWER) & (inhibition <= GOLDEN_UPPER)
            distance = jnp.abs(inhibition - GOLDEN_CENTER)
            w = jnp.exp(-distance / 0.1) * in_zone.astype(x.dtype)
            wsum = w.sum(axis=-1, keepdims=True)
            no_expert = wsum < 1e-08
            fb = jnp.exp(-distance / 0.3)
            _, top2 = jax.lax.top_k(fb, 2)
            fb_mask = jax.nn.one_hot(top2, E, dtype=x.dtype).sum(axis=-2)
            fb_w = fb * fb_mask
            fb_w = fb_w / jnp.clip(fb_w.sum(axis=-1, keepdims=True), 1e-08)
            w = jnp.where(no_expert, fb_w, w)
            return w / jnp.clip(w.sum(axis=-1, keepdims=True), 1e-08)
        key = jax.random.key(seed)
        ks = jax.random.split(key, 13)
        s = 0.02
        x = jax.random.normal(ks[0], (B, T, D), dtype=jnp.float32)
        Wg = jax.random.normal(ks[1], (E, D, F), dtype=jnp.float32) * s
        Wu = jax.random.normal(ks[2], (E, D, F), dtype=jnp.float32) * s
        Wd = jax.random.normal(ks[3], (E, F, D), dtype=jnp.float32) * s
        Ga = jax.random.normal(ks[4], (NL, D, R), dtype=jnp.float32) * s
        Gb = jax.random.normal(ks[5], (NL, R, F), dtype=jnp.float32) * s
        Ua = jax.random.normal(ks[6], (NL, D, R), dtype=jnp.float32) * s
        Ub = jax.random.normal(ks[7], (NL, R, F), dtype=jnp.float32) * s
        Da = jax.random.normal(ks[8], (NL, F, R), dtype=jnp.float32) * s
        Db = jax.random.normal(ks[9], (NL, R, D), dtype=jnp.float32) * s
        Wr = jax.random.normal(ks[10], (D, E), dtype=jnp.float32) * s
        temperature = jnp.ones((1,), dtype=jnp.float32)
        return {'x': x, 'Wg': Wg, 'Wu': Wu, 'Wd': Wd, 'Ga': Ga, 'Gb': Gb, 'Ua': Ua, 'Ub': Ub, 'Da': Da, 'Db': Db, 'Wr': Wr, 'temperature': temperature}
    _L0_ffn_all = _L0_ffn_setup()
    _L0_ffn_in = {k: v for k, v in _L0_ffn_all.items() if k in ('Wg', 'Wu', 'Wd', 'Ga', 'Gb', 'Ua', 'Ub', 'Da', 'Db', 'Wr', 'temperature')}
    del _L0_ffn_all
    return {'x': x, 'ctx_1024': ctx_1024, 'L0_attn_w_qkv': _L0_attn_in['w_qkv'], 'L0_attn_w_out': _L0_attn_in['w_out'], 'L0_attn_b_out': _L0_attn_in['b_out'], 'L0_xattn_Wq': _L0_xattn_in['Wq'], 'L0_xattn_bq': _L0_xattn_in['bq'], 'L0_xattn_Wk': _L0_xattn_in['Wk'], 'L0_xattn_bk': _L0_xattn_in['bk'], 'L0_ffn_Wg': _L0_ffn_in['Wg'], 'L0_ffn_Wu': _L0_ffn_in['Wu'], 'L0_ffn_Wd': _L0_ffn_in['Wd'], 'L0_ffn_Ga': _L0_ffn_in['Ga'], 'L0_ffn_Gb': _L0_ffn_in['Gb'], 'L0_ffn_Ua': _L0_ffn_in['Ua'], 'L0_ffn_Ub': _L0_ffn_in['Ub'], 'L0_ffn_Da': _L0_ffn_in['Da'], 'L0_ffn_Db': _L0_ffn_in['Db'], 'L0_ffn_Wr': _L0_ffn_in['Wr'], 'L0_ffn_temperature': _L0_ffn_in['temperature']}

def reference(x, ctx_1024, L0_attn_w_qkv, L0_attn_w_out, L0_attn_b_out, L0_xattn_Wq, L0_xattn_bq, L0_xattn_Wk, L0_xattn_bk, L0_ffn_Wg, L0_ffn_Wu, L0_ffn_Wd, L0_ffn_Ga, L0_ffn_Gb, L0_ffn_Ua, L0_ffn_Ub, L0_ffn_Da, L0_ffn_Db, L0_ffn_Wr, L0_ffn_temperature):
    import jax
    import jax.numpy as jnp

    def _L0_attn_ref(x, w_qkv, w_out, b_out):
        import jax, jax.numpy as jnp
        import numpy as np
        EMBED_DIM = 512
        NUM_HEADS = 16
        BLOCK_SIZE = 128

        def _flash_attention_v2(q, k, v, block_size, scale):
            B, H, S, D = q.shape
            nb = S // block_size
            qb = q.reshape(B, H, nb, block_size, D)
            kb = k.reshape(B, H, nb, block_size, D).transpose(2, 0, 1, 3, 4)
            vb = v.reshape(B, H, nb, block_size, D).transpose(2, 0, 1, 3, 4)
            out0 = jnp.zeros_like(qb)
            l0 = jnp.zeros((B, H, nb, block_size, 1), dtype=q.dtype)
            m0 = jnp.full((B, H, nb, block_size, 1), -jnp.inf, dtype=q.dtype)

            def step(carry, kv):
                out, l, m = carry
                k_j, v_j = kv
                s = jnp.einsum('bhnqd,bhkd->bhnqk', qb, k_j) * scale
                m_ij = jnp.max(s, axis=-1, keepdims=True)
                p = jnp.exp(s - m_ij)
                l_ij = jnp.sum(p, axis=-1, keepdims=True)
                m_new = jnp.maximum(m, m_ij)
                alpha = jnp.exp(m - m_new)
                beta = jnp.exp(m_ij - m_new)
                l_new = alpha * l + beta * l_ij
                pv = jnp.einsum('bhnqk,bhkd->bhnqd', p, v_j)
                out_new = alpha * l / l_new * out + beta * l_ij / l_new * pv
                return ((out_new, l_new, m_new), None)
            (out, _, _), _ = jax.lax.scan(step, (out0, l0, m0), (kb, vb))
            return out.reshape(B, H, S, D)
        B, S, E = x.shape
        H = NUM_HEADS
        D = E // H
        scale = 1.0 / np.sqrt(D).astype(np.float32)
        qkv = (x @ w_qkv.T).reshape(B, S, 3, H, D)
        q, k, v = jnp.moveaxis(qkv, 2, 0)
        q = q.transpose(0, 2, 1, 3)
        k = k.transpose(0, 2, 1, 3)
        v = v.transpose(0, 2, 1, 3)
        out = _flash_attention_v2(q, k, v, BLOCK_SIZE, scale)
        out = out.transpose(0, 2, 1, 3).reshape(B, S, E)
        return out @ w_out.T + b_out

    def _L0_xattn_ref(teacher_logits, teacher_features, Wq, bq, Wk, bk):
        import jax, jax.numpy as jnp
        import numpy as np
        query = jnp.einsum('bnc,dc->bnd', teacher_features, Wq) + bq
        key = jnp.einsum('bnc,dc->bnd', teacher_features, Wk) + bk
        energy = jnp.einsum('bnd,bmd->bnm', query, key)
        attention = jax.nn.softmax(energy, axis=-1)
        x_m = jnp.einsum('bln,bmn->blm', teacher_logits, attention)
        return x_m

    def _L0_ffn_ref(x, Wg, Wu, Wd, Ga, Gb, Ua, Ub, Da, Db, Wr, temperature):
        import jax, jax.numpy as jnp
        import numpy as np
        import math
        GOLDEN_CENTER = 1.0 / math.e
        GOLDEN_LOWER = 0.5 - math.log(4.0 / 3.0)
        GOLDEN_UPPER = 0.5
        B, T, D = (4, 256, 512)
        E = 8
        F = 2048 // (E // 2)
        R = 64
        NL = 2

        def _router_weights(x, Wr, temperature):
            logits = jnp.einsum('btd,de->bte', x, Wr)
            inhibition = jax.nn.sigmoid(logits / temperature)
            in_zone = (inhibition >= GOLDEN_LOWER) & (inhibition <= GOLDEN_UPPER)
            distance = jnp.abs(inhibition - GOLDEN_CENTER)
            w = jnp.exp(-distance / 0.1) * in_zone.astype(x.dtype)
            wsum = w.sum(axis=-1, keepdims=True)
            no_expert = wsum < 1e-08
            fb = jnp.exp(-distance / 0.3)
            _, top2 = jax.lax.top_k(fb, 2)
            fb_mask = jax.nn.one_hot(top2, E, dtype=x.dtype).sum(axis=-2)
            fb_w = fb * fb_mask
            fb_w = fb_w / jnp.clip(fb_w.sum(axis=-1, keepdims=True), 1e-08)
            w = jnp.where(no_expert, fb_w, w)
            return w / jnp.clip(w.sum(axis=-1, keepdims=True), 1e-08)
        weights = _router_weights(x, Wr, temperature)
        gate = jnp.einsum('btd,edf->ebtf', x, Wg)
        up = jnp.einsum('btd,edf->ebtf', x, Wu)
        gate = gate.at[:NL].add(jnp.einsum('btd,edr,erf->ebtf', x, Ga, Gb))
        up = up.at[:NL].add(jnp.einsum('btd,edr,erf->ebtf', x, Ua, Ub))
        mid = jax.nn.silu(gate) * up
        out = jnp.einsum('ebtf,efd->ebtd', mid, Wd)
        out = out.at[:NL].add(jnp.einsum('ebtf,efr,erd->ebtd', mid[:NL], Da, Db))
        return jnp.einsum('bte,ebtd->btd', weights, out)
    x = x + _L0_attn_ref(_layernorm(x, axis=-1), L0_attn_w_qkv, L0_attn_w_out, L0_attn_b_out)
    x = x + _L0_xattn_ref(_layernorm(x, axis=-1), ctx_1024, L0_xattn_Wq, L0_xattn_bq, L0_xattn_Wk, L0_xattn_bk)
    x = x + _L0_ffn_ref(_layernorm(x, axis=-1), L0_ffn_Wg, L0_ffn_Wu, L0_ffn_Wd, L0_ffn_Ga, L0_ffn_Gb, L0_ffn_Ua, L0_ffn_Ub, L0_ffn_Da, L0_ffn_Db, L0_ffn_Wr, L0_ffn_temperature)
    return x

_drawn_inputs = setup_inputs


def setup_inputs(seed=0):
    import zlib

    import numpy as np

    out = dict(_drawn_inputs(seed))
    spreads = {'L0_attn_b_out': (0.0, 0.1), 'L0_xattn_bq': (0.0, 0.1), 'L0_xattn_bk': (0.0, 0.8)}
    factors = {'L0_ffn_Wg': 3.129,
     'L0_ffn_Wu': 3.11,
     'L0_ffn_Wd': 3.074,
     'L0_ffn_Ga': 8.0,
     'L0_ffn_Gb': 8.0,
     'L0_ffn_Ua': 8.0,
     'L0_ffn_Ub': 8.0,
     'L0_ffn_Da': 8.0,
     'L0_ffn_Db': 8.0,
     'L0_ffn_Wr': 3.927}
    for name, (base, spread) in spreads.items():
        noise = np.random.default_rng([zlib.crc32(name.encode()), seed]).standard_normal(out[name].shape)
        drawn = base * np.exp(spread * noise) if base else spread * noise
        out[name] = jnp.asarray(drawn.astype(out[name].dtype))
    for name, factor in factors.items():
        out[name] = (out[name] * factor).astype(out[name].dtype)
    return out
```

```python
import math
from contextlib import ExitStack

import numpy as np

import concourse.bass as bass
from concourse import mybir

F32 = mybir.dt.float32
F32R = mybir.dt.float32r
I32 = mybir.dt.int32
U32 = mybir.dt.uint32
ALU = mybir.AluOpType
ACT = mybir.ActivationFunctionType
AX = mybir.AxisListType

P = 128
B, S, D = 4, 512, 512
KB = D // P
TB = S // P
NT = B * TB
H, HD = 16, 32
HG = P // HD
NG = H // HG
NPAIR = H // 2
C = 256
CB = C // P
NE, FF, NL, R = 8, 512, 2, 64
FH = FF // 2
FB = FH // P
CREDIT = 1
LN_EPS = 1e-5
ATT_SCALE = 1.0 / math.sqrt(HD)
GOLDEN_CENTER = 1.0 / math.e
GOLDEN_LOWER = 0.5 - math.log(4.0 / 3.0)
GOLDEN_UPPER = 0.5

SLOTS = 3
STACK = 3 * HD
SHIFT = 2 * TB
PRING = 4
LAG = 2
VW = HD + 1
NSTEP = H * TB
NEWTON = 4


def matmul3(pe, out, w_hi, w_lo, x_hi, x_lo, first, last):
    pe.matmul(out, w_hi, x_hi, start=first, stop=False)
    pe.matmul(out, w_hi, x_lo, start=False, stop=False)
    return pe.matmul(out, w_lo, x_hi, start=False, stop=last)


def moments(dve, stats, mean, var, tmp, chain):
    even, odd, sq_even, sq_odd = (stats[:, :, i] for i in (1, 4, 2, 5))
    chain.then(dve.tensor_tensor(mean, even, odd, ALU.add))
    chain.then(dve.tensor_scalar(mean, mean, 0.5, None, ALU.mult))
    chain.then(dve.tensor_tensor(tmp, even, odd, ALU.subtract))
    chain.then(dve.scalar_tensor_tensor(out=tmp, in0=tmp, scalar=0.25, in1=tmp, op0=ALU.mult, op1=ALU.mult))
    chain.then(dve.tensor_tensor(var, sq_even, sq_odd, ALU.add))
    chain.then(dve.scalar_tensor_tensor(out=var, in0=var, scalar=1.0 / D, in1=tmp, op0=ALU.mult, op1=ALU.add))


def rsqrt_steps(dve, var, y, tmp, chain):
    chain.then(dve.tensor_scalar(var, var, LN_EPS, None, ALU.add))
    chain.then(dve.tensor_scalar(tmp.bitcast(U32), var.bitcast(U32), 1, None, ALU.logical_shift_right))
    chain.then(dve.tensor_scalar(y.bitcast(I32), tmp.bitcast(I32), -1.0, float(0x5F3759DF), ALU.mult, ALU.add))
    for _ in range(NEWTON):
        chain.then(dve.scalar_tensor_tensor(out=tmp, in0=y, scalar=-0.5, in1=y, op0=ALU.mult, op1=ALU.mult))
        chain.then(dve.tensor_tensor(tmp, tmp, var, ALU.mult))
        chain.then(dve.scalar_tensor_tensor(out=y, in0=tmp, scalar=1.5, in1=y, op0=ALU.add, op1=ALU.mult))


class Chain:

    def __init__(self, eng, sem, base=0):
        self.eng, self.sem, self.base, self.n = eng, sem, base, 0

    def then(self, instruction):
        self.n += 1
        instruction.then_inc(self.sem, 1)
        self.eng.wait_ge(self.sem, self.base + self.n)


def build(nc, x, ctxT, w_qkvT, w_outT, b_out, wqT, bq, wkT, bk, Wg, Wu, Wd, GaT, Gb, UaT, Ub, DaT, Db, Wr,
          temperature, ident_in, out, stop=3):
    xt = x.rearrange("b (t p) d -> p (b t) d", p=P)
    outt = out.rearrange("b (t p) d -> p (b t) d", p=P)
    w_fix = nc.dram_tensor("w_fix", [NL, 3, D, FF], F32, kind="Internal").ap()
    with ExitStack() as whole:
        xres = whole.enter_context(nc.sbuf_tensor("xres", [P, NT, D], F32))
        ident = whole.enter_context(nc.sbuf_tensor("ident", [P, P], F32))
        bank = [whole.enter_context(nc.psum_tensor(f"bank{i}", [P, 512], F32)) for i in range(8)]
        self_attention(nc, xres, ident, bank, xt, w_qkvT, w_outT, b_out, ident_in)
        if stop >= 2:
            cross_attention(nc, xres, ident, bank, ctxT, wqT, bq, wkT, bk, Wg, Wu, Wd, GaT, Gb, UaT, Ub, DaT, Db, w_fix)
        if stop >= 3:
            experts(nc, xres, ident, bank, Wg, Wu, Wd, w_fix, Wr, temperature)
        with nc.semaphore("out_stored") as out_stored, nc.Block() as block:
            @block.sync
            def _(sp):
                for b in range(B):
                    sp.dma_start(outt[:, b * TB:(b + 1) * TB, :], xres[:, b * TB:(b + 1) * TB, :]).then_inc(out_stored, 16)
                sp.wait_ge(out_stored, 16 * B)


def self_attention(nc, xres, ident, bank, xt, w_qkvT, w_outT, b_out, ident_in):
    with ExitStack() as ctx:
        def sb(name, shape, dt=F32):
            return ctx.enter_context(nc.sbuf_tensor("a_" + name, shape, dt))

        def sem(name):
            return ctx.enter_context(nc.semaphore("a_" + name))

        w_hi, w_lo = sb("w_hi", [P, KB, 3 * D], F32R), sb("w_lo", [P, KB, 3 * D], F32R)
        wo_hi, wo_lo = sb("wo_hi", [P, KB, D], F32R), sb("wo_lo", [P, KB, D], F32R)
        xT_hi, xT_lo = sb("xT_hi", [P, KB, S], F32R), sb("xT_lo", [P, KB, S], F32R)
        q_stack, k_stack = sb("q_stack", [P, SLOTS, 2, S], F32R), sb("k_stack", [P, SLOTS, 2, S], F32R)
        qk_hi, qk_lo = sb("qk_hi", [P, 2, S], F32R), sb("qk_lo", [P, 2, S], F32R)
        v_ones = sb("v_ones", [P, TB, H, VW])
        work = sb("work", [P, PRING, S])
        pv = sb("pv", [P, 2, TB, TB, VW])
        weighed = sb("weighed", [P, TB, TB, HD])
        half_sum, o_sum = sb("half_sum", [P, 2, TB, HD]), sb("o_sum", [P, TB, HD])
        l_part = sb("l_part", [P, TB, TB])
        l_sum, l_rec = sb("l_sum", [P, TB, 1]), sb("l_rec", [P, 2, TB, 1])
        o_group = sb("o_group", [P, TB, P])
        OT_hi, OT_lo = sb("OT_hi", [P, NG, S], F32R), sb("OT_lo", [P, NG, S], F32R)
        bo = sb("bo", [P, D])
        stats, mean = sb("stats", [P, TB, 6]), sb("mean", [P, TB])
        var, rstd, tmp = sb("var", [P, TB]), sb("rstd", [P, TB]), sb("tmp", [P, TB])
        row_max, gap, neg_shift, gain = (sb(n, [P, 2, TB, 2 * TB]) for n in ("row_max", "gap", "neg_shift", "gain"))
        whole_max = sb("whole_max", [P, 2 * TB])
        shift_rows = sb("shift_rows", [TB * 2 * TB, 2, P], F32R)
        block_one = sb("block_one", [P, TB])

        x_in, w_raw, wo_raw, small_in = sem("x_in"), sem("w_raw"), sem("wo_raw"), sem("small_in")
        w_hi_made, w_lo_made, wo_hi_made, wo_lo_made = sem("w_hi_made"), sem("w_lo_made"), sem("wo_hi_made"), sem("wo_lo_made")
        ones_set = sem("ones_set")
        stats_made, ln_chain, xn_ready, xT_psum, xT_hi_made, xT_lo_made = (
            sem("stats_made"), sem("ln_chain"), sem("xn_ready"), sem("xT_psum"), sem("xT_hi_made"), sem("xT_lo_made"))
        qk_psum, qk_hi_made, qk_lo_made = sem("qk_psum"), sem("qk_hi_made"), sem("qk_lo_made")
        v_psum, v_made = sem("v_psum"), sem("v_made")
        stack_in = [sem(f"stack_in{i}") for i in range(SLOTS)]
        s_psum, max_made, whole_made, gap_made, shift_made, gain_made = (
            sem("s_psum"), sem("max_made"), sem("whole_made"), sem("gap_made"), sem("shift_made"), sem("gain_made"))
        shiftT_psum, shift_hi_made, shift_rows_made = sem("shiftT_psum"), sem("shift_hi_made"), sem("shift_rows_made")
        shift_in = [sem(f"shift_in{i}") for i in range(2)]
        st_psum, exp_made, pv_psum, pv_made = sem("st_psum"), sem("exp_made"), sem("pv_psum"), sem("pv_made")
        l_part_made, l_sum_made, l_rec_made, combine_chain = (
            sem("l_part_made"), sem("l_sum_made"), sem("l_rec_made"), sem("combine_chain"))
        OT_psum, OT_hi_made, OT_lo_made, y_psum, bias_added, x1_made = (
            sem("OT_psum"), sem("OT_hi_made"), sem("OT_lo_made"), sem("y_psum"), sem("bias_added"), sem("x1_made"))

        NCH = KB * 3
        slot_pairs = [len(range(s, NPAIR, SLOTS)) for s in range(SLOTS)]

        def staged(i):
            return xres[:, TB + i, :]

        def stacks_ready(b, p):
            return (b * slot_pairs[p % SLOTS] + p // SLOTS + 1) * 192

        def shift_ready(b, p):
            return (b * (NPAIR // 2) + p // 2 + 1) * 16 * SHIFT

        def o_done(b, h):
            return (b * H + h + 1) * 4

        LAST = NSTEP + 8

        block = ctx.enter_context(nc.Block())

        @block.sync
        def _(sp):
            sp.dma_start(ident[:, :], ident_in).then_inc(small_in, 16)
            sp.dma_start(bo[:, :], b_out.rearrange("(a d) -> a d", a=1).broadcast_to([P, D])).then_inc(small_in, 16)
            for part in range(2):
                r0 = STACK + part * TB
                sp.dma_start(block_one[r0:r0 + TB, :], ident_in[0:TB, 0:TB]).then_inc(small_in, 16)
            sp.dma_start(xres[:, 0:TB, :], xt[:, 0:TB, :]).then_inc(x_in, 16)
            for k in range(KB):
                if k:
                    sp.wait_ge(w_raw, 16 * k)
                sp.dma_start(xres[:, TB + 3 * k:TB + 3 * k + 3, :],
                             w_qkvT[k * P:(k + 1) * P, :].rearrange("p (c n) -> p c n", n=D)).then_inc(w_raw, 16)
            sp.wait_ge(w_lo_made, NCH)
            sp.dma_start(xres[:, TB:2 * TB, :], w_outT.rearrange("(k p) n -> p k n", p=P)).then_inc(wo_raw, 16)
            sp.wait_ge(wo_lo_made, KB)
            sp.wait_ge(x_in, 16)
            sp.dma_start(xres[:, TB:NT, :], xt[:, TB:NT, :]).then_inc(x_in, 16)
            with sp.Fori(0, B) as b:
                def load_stacks(p):
                    s, g, r0 = p % SLOTS, p // 2, (p % 2) * 2 * HD
                    split = sp.to_reg(b * 2 * NG + 2 * g + 2)
                    slot_free = sp.to_reg(b * NSTEP + (p - SLOTS + 1) * 2 * TB) if p >= SLOTS else None
                    sp.wait_ge(qk_lo_made, split)
                    if p >= SLOTS:
                        sp.wait_ge(st_psum, slot_free)
                    for which, stack, parts in ((0, q_stack, (qk_hi, qk_hi, qk_lo)), (1, k_stack, (qk_hi, qk_lo, qk_hi))):
                        for r, part in enumerate(parts):
                            for hh in range(2):
                                sp.dma_start(stack[r * HD:(r + 1) * HD, s, hh, :].bitcast(F32),
                                             part[r0 + hh * HD:r0 + (hh + 1) * HD, which, :].bitcast(F32)).then_inc(stack_in[s], 16)

                def load_shift(p):
                    sp.wait_ge(shift_rows_made, b * NPAIR + p + 1)
                    for part in range(2):
                        for kb in range(TB):
                            r0 = STACK + part * TB + kb
                            sp.dma_start(q_stack[r0:r0 + 1, p % SLOTS, :, :].bitcast(F32).rearrange("o h (t q) -> o (h t) q", q=P),
                                         shift_rows[kb * 2 * TB:(kb + 1) * 2 * TB, part, :].bitcast(F32)).then_inc(shift_in[p % 2], 16)

                load_stacks(0)
                load_stacks(1)
                load_shift(0)
                for p in range(NPAIR):
                    if p + 2 < NPAIR:
                        load_stacks(p + 2)
                    if p + 1 < NPAIR:
                        load_shift(p + 1)

        @block.gpsimd
        def _(pool):
            pool.memset(v_ones[:, :, :, HD:VW], 1.0).then_inc(ones_set, 1)
            for i in range(NCH):
                pool.wait_ge(w_hi_made, i + 1)
                k, c = divmod(i, 3)
                pool.tensor_tensor(w_lo[:, k, c * D:(c + 1) * D], staged(i), w_hi[:, k, c * D:(c + 1) * D].bitcast(F32),
                                   ALU.subtract).then_inc(w_lo_made, 1)
            for k in range(KB):
                pool.wait_ge(wo_hi_made, k + 1)
                pool.tensor_tensor(wo_lo[:, k, :], xres[:, TB + k, :], wo_hi[:, k, :].bitcast(F32), ALU.subtract)\
                    .then_inc(wo_lo_made, 1)
            pool.wait_ge(small_in, 64)
            with pool.Fori(0, B) as b:
                for j in range(TB):
                    pool.wait_ge(xn_ready, b * TB + j + 1)
                    xj = xres[:, bass.ds(b * TB + j, 1), :].rearrange("p o d -> p (o d)")
                    pool.tensor_tensor(xj, xj, bo[:, :], ALU.add).then_inc(bias_added, 1)
                for h in range(H):
                    chain = Chain(pool, combine_chain, (b * H + h) * 4)
                    pool.wait_ge(pv_made, b * NSTEP + TB * (h + 1))
                    chain.then(pool.tensor_tensor(weighed[:, :, :, :], pv[:, h % 2, :, :, 0:HD],
                                                  pv[:, h % 2, :, :, HD:VW].broadcast_to([P, TB, TB, HD]), ALU.mult))
                    chain.then(pool.tensor_tensor(half_sum[:, :, :, :], weighed[:, 0:2, :, :], weighed[:, 2:4, :, :], ALU.add))
                    chain.then(pool.tensor_tensor(o_sum[:, :, :], half_sum[:, 0, :, :], half_sum[:, 1, :, :], ALU.add))
                    pool.wait_ge(l_rec_made, b * H + h + 1)
                    if h % HG == 0 and h:
                        pool.wait_ge(OT_psum, b * NG + h // HG)
                    chain.then(pool.tensor_tensor(o_group[:, :, (h % HG) * HD:(h % HG + 1) * HD], o_sum[:, :, :],
                                                  l_rec[:, h % 2, :, :].broadcast_to([P, TB, HD]), ALU.mult))

        @block.scalar
        def _(act):
            for i in range(NCH):
                k, c = divmod(i, 3)
                act.wait_ge(w_raw, 16 * (k + 1))
                act.activation(w_hi[:, k, c * D:(c + 1) * D], staged(i), ACT.Copy).then_inc(w_hi_made, 1)
            for k in range(KB):
                act.wait_ge(wo_raw, 16)
                act.activation(wo_hi[:, k, :], xres[:, TB + k, :], ACT.Copy).then_inc(wo_hi_made, 1)
            with act.Fori(0, B) as b:
                for j in range(TB):
                    act.wait_ge(xT_psum, b * TB + j + 1)
                    act.activation(xT_hi[:, :, j * P:(j + 1) * P], bank[j][:, :].rearrange("p (k t) -> p k t", k=KB), ACT.Copy)\
                        .then_inc(xT_hi_made, 1)

                def qk_high(i):
                    act.wait_ge(qk_psum, b * 2 * NG + i + 1)
                    if i >= 2:
                        for p in (i // 2 * 2 - 2, i // 2 * 2 - 1):
                            act.wait_ge(stack_in[p % SLOTS], stacks_ready(b, p))
                    act.activation(qk_hi[:, i % 2, :], bank[7][:, :], ACT.Copy).then_inc(qk_hi_made, 1)

                qk_high(0)
                qk_high(1)
                for t in range(TB):
                    act.wait_ge(v_psum, b * TB + t + 1)
                    act.activation(v_ones[:, t, :, 0:HD], bank[t][:, :].rearrange("p (h d) -> p h d", h=H), ACT.Copy)\
                        .then_inc(v_made, 1)

                def gains(p):
                    act.wait_ge(gap_made, b * NPAIR + p + 1)
                    if p >= 2:
                        act.wait_ge(l_part_made, b * H + 2 * (p - 1))
                    act.activation(gain[:, p % 2, :, :], gap[:, p % 2, :, :], ACT.Exp, scale=0.5 * ATT_SCALE).then_inc(gain_made, 1)

                gains(0)
                for n in range(LAST):
                    p, t = divmod(n, 2 * TB)
                    if n < NSTEP:
                        act.wait_ge(st_psum, b * NSTEP + n + 1)
                        if n >= PRING:
                            act.wait_ge(pv_psum, b * NSTEP + n - PRING + 1)
                        act.activation(work[:, n % PRING, :], bank[2 + n % 2][:, :], ACT.Exp, scale=ATT_SCALE).then_inc(exp_made, 1)
                        if p % 2 == 0 and p // 2 + 1 < NG and t in (2, 5):
                            qk_high(p + 2 + (t == 5))
                        if t == 5 and p + 1 < NPAIR:
                            gains(p + 1)
                    m = n - 3
                    if 0 <= m < NSTEP:
                        h, kb = divmod(m, TB)
                        act.wait_ge(pv_psum, b * NSTEP + m + 1)
                        if kb == 0 and h >= 2:
                            act.wait_ge(combine_chain, o_done(b, h - 2))
                            act.wait_ge(l_part_made, b * H + h - 1)
                        act.activation(pv[:, h % 2, kb, :, :], bank[4 + m % 2][:, 0:TB * VW].rearrange("p (t w) -> p t w", w=VW), ACT.Copy)\
                            .then_inc(pv_made, 1)
                    g = (n - 22) // 16
                    if n >= 22 and (n - 22) % 16 == 0 and g < NG:
                        act.wait_ge(OT_psum, b * NG + g + 1)
                        act.activation(OT_hi[:, g, :], bank[6][:, :], ACT.Copy).then_inc(OT_hi_made, 1)

        def xT_low(dve, b, j):
            dve.wait_ge(xT_hi_made, b * TB + j + 1)
            dve.tensor_tensor(xT_lo[:, :, j * P:(j + 1) * P], bank[j][:, :].rearrange("p (k t) -> p k t", k=KB),
                              xT_hi[:, :, j * P:(j + 1) * P].bitcast(F32), ALU.subtract).then_inc(xT_lo_made, 1)

        @block.vector
        def _(dve):
            dve.wait_ge(small_in, 64)
            dve.tensor_copy(k_stack[STACK:STACK + SHIFT, :, :, :].rearrange("r s h (k n) -> r (s h) k n", k=TB),
                            block_one[STACK:STACK + SHIFT, :].rearrange("r (a k b) -> r a k b", a=1, b=1)
                            .broadcast_to([SHIFT, SLOTS * 2, TB, P])).then_inc(ones_set, 1)
            dve.sem_inc(x1_made, CREDIT)
            with dve.Fori(0, B) as b:
                dve.wait_ge(x_in, 16 + ((b + 3) >> 2) * 16)
                chain = Chain(dve, ln_chain, b * (TB + 9 + 3 * NEWTON))

                def row(j):
                    return xres[:, bass.ds(b * TB + j, 1), :].rearrange("p o d -> p (o d)")

                for j in range(TB):
                    chain.then(dve.bn_stats(stats[:, j, :], row(j)))
                moments(dve, stats, mean[:, :], var[:, :], tmp[:, :], chain)
                rsqrt_steps(dve, var[:, :], rstd[:, :], tmp[:, :], chain)
                for j in range(TB):
                    if j >= 2:
                        dve.wait_ge(xT_psum, b * TB + j - 1)
                    dve.tensor_scalar(work[:, j % 2, :], row(j), mean[:, j:j + 1], rstd[:, j:j + 1], ALU.subtract, ALU.mult)\
                        .then_inc(xn_ready, 1)
                    if j >= 1:
                        xT_low(dve, b, j - 1)
                xT_low(dve, b, TB - 1)

                def qk_low(i):
                    dve.wait_ge(qk_hi_made, b * 2 * NG + i + 1)
                    dve.tensor_tensor(qk_lo[:, i % 2, :], bank[7][:, :], qk_hi[:, i % 2, :].bitcast(F32), ALU.subtract)\
                        .then_inc(qk_lo_made, 1)

                def tile_max(n):
                    dve.wait_ge(s_psum, b * NSTEP + n + 1)
                    p, t = divmod(n, 2 * TB)
                    dve.reduce_max(row_max[:, p % 2, :, t:t + 1], bank[n % 2][:, :].rearrange("q (k n) -> q k n", k=TB), AX.X)\
                        .then_inc(max_made, 1)

                def shifts(p):
                    i = b * NPAIR + p + 1
                    dve.wait_ge(max_made, b * NSTEP + (p + 1) * 2 * TB)
                    dve.tensor_reduce(whole_max[:, :], row_max[:, p % 2, :, :].rearrange("q k x -> q x k"), AX.X, ALU.max)\
                        .then_inc(whole_made, 1)
                    dve.wait_ge(whole_made, i)
                    if p >= 2:
                        dve.wait_ge(gain_made, i - 2)
                    dve.tensor_tensor(gap[:, p % 2, :, :], row_max[:, p % 2, :, :],
                                      whole_max[:, :].rearrange("q (o x) -> q o x", o=1).broadcast_to([P, TB, 2 * TB]), ALU.subtract)\
                        .then_inc(gap_made, 1)
                    dve.wait_ge(gap_made, i)
                    dve.scalar_tensor_tensor(out=neg_shift[:, p % 2, :, :], in0=gap[:, p % 2, :, :], scalar=0.5,
                                             in1=row_max[:, p % 2, :, :], op0=ALU.mult, op1=ALU.subtract).then_inc(shift_made, 1)

                def split_shifts(p):
                    dve.wait_ge(shiftT_psum, b * NPAIR + p + 1)
                    if p >= 1:
                        dve.wait_ge(shift_in[(p - 1) % 2], shift_ready(b, p - 1))
                    rows = bank[6][0:TB * 2 * TB, 0:P]
                    dve.tensor_copy(shift_rows[:, 0, :], rows).then_inc(shift_hi_made, 1)
                    dve.wait_ge(shift_hi_made, b * NPAIR + p + 1)
                    dve.tensor_tensor(shift_rows[:, 1, :], rows, shift_rows[:, 0, :].bitcast(F32), ALU.subtract)\
                        .then_inc(shift_rows_made, 1)

                qk_low(0)
                qk_low(1)
                for t in range(2 * TB):
                    tile_max(t)
                shifts(0)
                split_shifts(0)
                for n in range(LAST):
                    p, t = divmod(n, 2 * TB)
                    if n < NSTEP and t < TB and p + 1 < NPAIR:
                        tile_max((p + 1) * 2 * TB + 2 * t)
                        tile_max((p + 1) * 2 * TB + 2 * t + 1)
                        if t == TB - 1:
                            shifts(p + 1)
                    if n < NSTEP and p % 2 == 0 and p // 2 + 1 < NG and t in (2, 5):
                        qk_low(p + 2 + (t == 5))
                    if n < NSTEP and t == TB and p + 1 < NPAIR:
                        split_shifts(p + 1)
                    h = (n - 7) // TB
                    if n >= 7 and (n - 7) % TB == 0 and h < H:
                        i = b * H + h + 1
                        hh = h % 2
                        dve.wait_ge(pv_made, b * NSTEP + TB * (h + 1))
                        dve.wait_ge(gain_made, b * NPAIR + h // 2 + 1)
                        dve.tensor_tensor(l_part[:, :, :], pv[:, h % 2, :, :, HD:VW].rearrange("p k t o -> p k (t o)"),
                                          gain[:, h // 2 % 2, :, hh * TB:(hh + 1) * TB], ALU.mult).then_inc(l_part_made, 1)
                        dve.wait_ge(l_part_made, i)
                        dve.tensor_reduce(l_sum[:, :, 0], l_part[:, :, :].rearrange("p k t -> p t k"), AX.X, ALU.add)\
                            .then_inc(l_sum_made, 1)
                        dve.wait_ge(l_sum_made, i)
                        if h >= 2:
                            dve.wait_ge(combine_chain, o_done(b, h - 2))
                        dve.reciprocal(l_rec[:, h % 2, :, :], l_sum[:, :, :]).then_inc(l_rec_made, 1)
                    g = (n - 23) // 16
                    if n >= 23 and (n - 23) % 16 == 0 and g < NG:
                        dve.wait_ge(OT_hi_made, b * NG + g + 1)
                        dve.tensor_tensor(OT_lo[:, g, :], bank[6][:, :], OT_hi[:, g, :].bitcast(F32), ALU.subtract)\
                            .then_inc(OT_lo_made, 1)
                dve.wait_ge(bias_added, b * TB + TB)
                for j in range(TB):
                    dve.wait_ge(y_psum, b * TB + j + 1)
                    dve.tensor_tensor(row(j), bank[j][:, :], row(j), ALU.add).then_inc(x1_made, 1)

        @block.tensor
        def _(pe):
            pe.wait_ge(small_in, 64)
            with pe.Fori(0, B) as b:
                pe.wait_ge(x1_made, b * TB + CREDIT)
                for j in range(TB):
                    pe.wait_ge(xn_ready, b * TB + j + 1)
                    for k in range(KB):
                        last = pe.transpose(bank[j][:, k * P:(k + 1) * P], work[:, j % 2, k * P:(k + 1) * P], ident[:, :])
                    last.then_inc(xT_psum, 1)
                pe.wait_ge(w_lo_made, NCH)
                pe.wait_ge(xT_lo_made, b * TB + TB)

                def qk(i, ks):
                    if i and ks[0] == 0:
                        pe.wait_ge(qk_lo_made, b * 2 * NG + i)
                    cols = slice((i % 2) * D + (i // 2) * P, (i % 2) * D + (i // 2 + 1) * P)
                    for k in ks:
                        last = matmul3(pe, bank[7][:, :], w_hi[:, k, cols], w_lo[:, k, cols], xT_hi[:, k, :], xT_lo[:, k, :],
                                       k == 0, k == KB - 1)
                    if ks[-1] == KB - 1:
                        last.then_inc(qk_psum, 1)

                qk(0, (0, 1, 2, 3))
                qk(1, (0, 1, 2, 3))
                for t in range(TB):
                    for k in range(KB):
                        last = matmul3(pe, bank[t][:, :], xT_hi[:, k, t * P:(t + 1) * P], xT_lo[:, k, t * P:(t + 1) * P],
                                       w_hi[:, k, 2 * D:], w_lo[:, k, 2 * D:], k == 0, k == KB - 1)
                    last.then_inc(v_psum, 1)
                pe.wait_ge(ones_set, 2)
                pe.wait_ge(v_made, b * TB + TB)

                last_m = [None]

                def scores(n):
                    p, t = divmod(n, 2 * TB)
                    hh, qb = divmod(t, TB)
                    if t == 0:
                        pe.wait_ge(stack_in[p % SLOTS], stacks_ready(b, p))
                    if n >= 2:
                        pe.wait_ge(max_made, b * NSTEP + n - 1)
                    pe.matmul(bank[n % 2][:, :], q_stack[0:STACK, p % SLOTS, hh, qb * P:(qb + 1) * P],
                              k_stack[0:STACK, p % SLOTS, hh, :], start=True, stop=True).then_inc(s_psum, 1)

                def turn_shifts(p):
                    pe.wait_ge(shift_made, b * NPAIR + p + 1)
                    free_m()
                    pe.transpose(bank[6][0:TB * 2 * TB, 0:P], neg_shift[:, p % 2, :, :].rearrange("q k x -> q (k x)"), ident[:, :])\
                        .then_inc(shiftT_psum, 1)
                    last_m[0] = (shift_rows_made, b * NPAIR + p + 1)

                def free_m():
                    if last_m[0]:
                        pe.wait_ge(*last_m[0])

                for n in range(2 * TB):
                    scores(n)
                turn_shifts(0)
                for n in range(LAST):
                    p, t = divmod(n, 2 * TB)
                    if n < NSTEP:
                        if t < TB and p + 1 < NPAIR:
                            scores((p + 1) * 2 * TB + 2 * t)
                            scores((p + 1) * 2 * TB + 2 * t + 1)
                        hh, kb = divmod(t, TB)
                        if t == 0:
                            pe.wait_ge(shift_in[p % 2], shift_ready(b, p))
                        if n >= 2:
                            pe.wait_ge(exp_made, b * NSTEP + n - 1)
                        pe.matmul(bank[2 + n % 2][:, :], k_stack[0:STACK + SHIFT, p % SLOTS, hh, kb * P:(kb + 1) * P],
                                  q_stack[0:STACK + SHIFT, p % SLOTS, hh, :], start=True, stop=True).then_inc(st_psum, 1)
                        if p % 2 == 0 and p // 2 + 1 < NG and t in (0, 1, 3, 4):
                            qk(p + 2 + (t >= 3), (0, 1) if t in (0, 3) else (2, 3))
                    m = n - LAG
                    if 0 <= m < NSTEP:
                        h, kb = divmod(m, TB)
                        pe.wait_ge(exp_made, b * NSTEP + m + 1)
                        if m >= 2:
                            pe.wait_ge(pv_made, b * NSTEP + m - 1)
                        for qb in range(TB):
                            last = pe.matmul(bank[4 + m % 2][:, qb * VW:(qb + 1) * VW], work[:, m % PRING, qb * P:(qb + 1) * P],
                                             v_ones[:, kb, h, :], start=True, stop=True)
                        last.then_inc(pv_psum, 1)
                    if n < NSTEP and t == TB and p + 1 < NPAIR:
                        turn_shifts(p + 1)
                    g = (n - 22) // 16
                    if n >= 22 and (n - 22) % 16 == 0 and g < NG:
                        pe.wait_ge(combine_chain, o_done(b, (g + 1) * HG - 1))
                        free_m()
                        for t4 in range(TB):
                            last = pe.transpose(bank[6][:, t4 * P:(t4 + 1) * P], o_group[:, t4, :], ident[:, :])
                        last.then_inc(OT_psum, 1)
                        last_m[0] = (OT_lo_made, b * NG + g + 1)
                pe.wait_ge(OT_lo_made, b * NG + NG)
                pe.wait_ge(wo_lo_made, KB)
                for j in range(TB):
                    for g in range(NG):
                        last = matmul3(pe, bank[j][:, :], OT_hi[:, g, j * P:(j + 1) * P], OT_lo[:, g, j * P:(j + 1) * P],
                                       wo_hi[:, g, :], wo_lo[:, g, :], g == 0, g == NG - 1)
                    last.then_inc(y_psum, 1)


def cross_attention(nc, xres, ident, bank, ctxT, wqT, bq, wkT, bk, Wg, Wu, Wd, GaT, Gb, UaT, Ub, DaT, Db, w_fix):
    with ExitStack() as ctx:
        def sb(name, shape, dt=F32):
            return ctx.enter_context(nc.sbuf_tensor("c_" + name, shape, dt))

        def sem(name):
            return ctx.enter_context(nc.semaphore("c_" + name))

        ctx_raw = sb("ctx_raw", [P, CB, B, S])
        w_raw = sb("w_raw", [P, 2, CB, P])
        w_hi, w_lo = sb("w_hi", [P, 2, CB, P], F32R), sb("w_lo", [P, 2, CB, P], F32R)
        bias = sb("bias", [P, 2])
        c_hi, c_lo = sb("c_hi", [P, CB, S], F32R), sb("c_lo", [P, CB, S], F32R)
        qk = sb("qk", [P, 2, S])
        qk_hi, qk_lo = sb("qk_hi", [P, 2, S], F32R), sb("qk_lo", [P, 2, S], F32R)
        att = sb("att", [P, 2, S])
        neg_max, row_sum, rec_sum = sb("neg_max", [P, TB]), sb("row_sum", [P, TB]), sb("rec_sum", [P, TB])
        aT_hi, aT_lo = sb("aT_hi", [P, KB, S], F32R), sb("aT_lo", [P, KB, S], F32R)
        xn = sb("xn", [P, 2, D])
        xT_hi, xT_lo = sb("xT_hi", [P, KB, S], F32R), sb("xT_lo", [P, KB, S], F32R)
        stats, mean = sb("stats", [P, TB, 6]), sb("mean", [P, TB])
        var, rstd, tmp = sb("var", [P, TB]), sb("rstd", [P, TB]), sb("tmp", [P, TB])
        down = sb("down", [R, NL, 3, D])
        up = sb("up", [R, NL, 3, FF])
        w_full = sb("w_full", [P, NL, 3, KB, FF])

        w_in, ctx_in, lora_in, w_fixed, fix_stored = sem("w_in"), sem("ctx_in"), sem("lora_in"), sem("w_fixed"), sem("fix_stored")
        w_hi_made, w_lo_made, c_hi_made, c_lo_made = sem("w_hi_made"), sem("w_lo_made"), sem("c_hi_made"), sem("c_lo_made")
        qk_psum, qk_made, qk_hi_made, qk_lo_made = sem("qk_psum"), sem("qk_made"), sem("qk_hi_made"), sem("qk_lo_made")
        e_psum, max_made, exp_made, rec_made, att_made = (
            sem("e_psum"), sem("max_made"), sem("exp_made"), sem("rec_made"), sem("att_made"))
        aT_psum, aT_hi_made, aT_lo_made, y_psum, x2_made = (
            sem("aT_psum"), sem("aT_hi_made"), sem("aT_lo_made"), sem("y_psum"), sem("x2_made"))
        ln_chain, xn_ready, xT_psum, xT_hi_made, xT_lo_made, fix_psum = (
            sem("ln_chain"), sem("xn_ready"), sem("xT_psum"), sem("xT_hi_made"), sem("xT_lo_made"), sem("fix_psum"))
        NFIX = NL * 3 * KB

        block = ctx.enter_context(nc.Block())

        @block.sync
        def _(sp):
            for i, w in enumerate((wqT, wkT)):
                sp.dma_start(w_raw[:, i, :, :], w.rearrange("(c p) d -> p c d", p=P)).then_inc(w_in, 16)
            for i, v in enumerate((bq, bk)):
                sp.dma_start(bias[:, i:i + 1], v.rearrange("(d a) -> d a", a=1)).then_inc(w_in, 16)
            for c in range(CB):
                sp.dma_start(ctx_raw[:, c, :, :], ctxT[:, c * P:(c + 1) * P, :].rearrange("b p s -> p b s")).then_inc(ctx_in, 16)
            for m, (a, v, w) in enumerate(((GaT, Gb, Wg), (UaT, Ub, Wu), (DaT, Db, Wd))):
                sp.dma_start(down[:, :, m, :], a.rearrange("e r d -> r e d")).then_inc(lora_in, 16)
                sp.dma_start(up[:, :, m, :], v.rearrange("e r d -> r e d")).then_inc(lora_in, 16)
                for e in range(NL):
                    sp.dma_start(w_full[:, e, m, :, :], w[e, :, :].rearrange("(k p) f -> p k f", p=P)).then_inc(lora_in, 16)
            for i in range(NL * 3):
                e, m = divmod(i, 3)
                sp.wait_ge(w_fixed, (i + 1) * KB)
                sp.dma_start(w_fix[e, m, :, :].rearrange("(k p) f -> p k f", p=P), w_full[:, e, m, :, :]).then_inc(fix_stored, 16)
            sp.wait_ge(fix_stored, 16 * NL * 3)

        @block.gpsimd
        def _(pool):
            pool.wait_ge(w_hi_made, 1)
            pool.tensor_tensor(w_lo[:, :, :, :], w_raw[:, :, :, :], w_hi[:, :, :, :].bitcast(F32), ALU.subtract)\
                .then_inc(w_lo_made, 1)

        def att_high(act, b, j):
            act.wait_ge(aT_psum, b * TB + j + 1)
            act.activation(aT_hi[:, :, j * P:(j + 1) * P], bank[4 + j % 2][:, :].rearrange("p (k t) -> p k t", k=KB), ACT.Copy)\
                .then_inc(aT_hi_made, 1)

        @block.scalar
        def _(act):
            act.wait_ge(w_in, 64)
            act.activation(w_hi[:, :, :, :], w_raw[:, :, :, :], ACT.Copy).then_inc(w_hi_made, 1)
            act.wait_ge(ctx_in, 16 * CB)
            with act.Fori(0, B) as b:
                act.wait_ge(x2_made, b * TB + CREDIT)
                act.activation(c_hi[:, :, :], ctx_raw[:, :, bass.ds(b, 1), :].rearrange("p c o s -> p c (o s)"), ACT.Copy)\
                    .then_inc(c_hi_made, 1)
                for i in range(2):
                    act.wait_ge(qk_psum, b * 2 + i + 1)
                    act.activation(qk[:, i, :], bank[4 + i][:, :], ACT.Identity, bias=bias[:, i:i + 1]).then_inc(qk_made, 1)
                    act.wait_ge(qk_made, b * 2 + i + 1)
                    act.activation(qk_hi[:, i, :], qk[:, i, :], ACT.Copy).then_inc(qk_hi_made, 1)
                for j in range(TB):
                    act.wait_ge(max_made, b * TB + j + 1)
                    if j >= 2:
                        act.wait_ge(aT_psum, b * TB + j - 1)
                    act.activation(att[:, j % 2, :], bank[6 + j % 2][:, :], ACT.Exp, bias=neg_max[:, j:j + 1],
                                   accum_out=row_sum[:, j:j + 1]).then_inc(exp_made, 1)
                    if j >= 1:
                        att_high(act, b, j - 1)
                att_high(act, b, TB - 1)
                for j in range(TB):
                    act.wait_ge(xT_psum, b * TB + j + 1)
                    act.activation(xT_hi[:, :, j * P:(j + 1) * P], bank[j][:, :].rearrange("p (k t) -> p k t", k=KB), ACT.Copy)\
                        .then_inc(xT_hi_made, 1)

        def att_scale(dve, b, j):
            dve.wait_ge(exp_made, b * TB + j + 1)
            dve.reciprocal(rec_sum[:, j:j + 1], row_sum[:, j:j + 1]).then_inc(rec_made, 1)
            dve.wait_ge(rec_made, b * TB + j + 1)
            dve.tensor_scalar(att[:, j % 2, :], att[:, j % 2, :], rec_sum[:, j:j + 1], None, ALU.mult).then_inc(att_made, 1)

        def xT_low(dve, b, j):
            dve.wait_ge(xT_hi_made, b * TB + j + 1)
            dve.tensor_tensor(xT_lo[:, :, j * P:(j + 1) * P], bank[j][:, :].rearrange("p (k t) -> p k t", k=KB),
                              xT_hi[:, :, j * P:(j + 1) * P].bitcast(F32), ALU.subtract).then_inc(xT_lo_made, 1)

        @block.vector
        def _(dve):
            dve.sem_inc(x2_made, CREDIT)
            with dve.Fori(0, B) as b:
                dve.wait_ge(c_hi_made, b + 1)
                dve.tensor_tensor(c_lo[:, :, :], ctx_raw[:, :, bass.ds(b, 1), :].rearrange("p c o s -> p c (o s)"),
                                  c_hi[:, :, :].bitcast(F32), ALU.subtract).then_inc(c_lo_made, 1)
                for i in range(2):
                    dve.wait_ge(qk_hi_made, b * 2 + i + 1)
                    dve.tensor_tensor(qk_lo[:, i, :], qk[:, i, :], qk_hi[:, i, :].bitcast(F32), ALU.subtract).then_inc(qk_lo_made, 1)

                def att_low(j):
                    dve.wait_ge(aT_hi_made, b * TB + j + 1)
                    dve.tensor_tensor(aT_lo[:, :, j * P:(j + 1) * P], bank[4 + j % 2][:, :].rearrange("p (k t) -> p k t", k=KB),
                                      aT_hi[:, :, j * P:(j + 1) * P].bitcast(F32), ALU.subtract).then_inc(aT_lo_made, 1)

                for j in range(TB):
                    dve.wait_ge(e_psum, b * TB + j + 1)
                    dve.tensor_reduce(neg_max[:, j:j + 1], bank[6 + j % 2][:, :], AX.X, ALU.max, negate=True).then_inc(max_made, 1)
                    if j >= 1:
                        att_scale(dve, b, j - 1)
                    if j >= 2:
                        att_low(j - 2)
                att_scale(dve, b, TB - 1)
                att_low(TB - 2)
                att_low(TB - 1)

                def row(j):
                    return xres[:, bass.ds(b * TB + j, 1), :].rearrange("p o d -> p (o d)")

                chain = Chain(dve, ln_chain, b * (TB + 9 + 3 * NEWTON))
                for j in range(TB):
                    chain.then(dve.bn_stats(stats[:, j, :], row(j)))
                moments(dve, stats, mean[:, :], var[:, :], tmp[:, :], chain)
                rsqrt_steps(dve, var[:, :], rstd[:, :], tmp[:, :], chain)
                for j in range(TB):
                    if j >= 2:
                        dve.wait_ge(xT_psum, b * TB + j - 1)
                    dve.tensor_scalar(xn[:, j % 2, :], row(j), mean[:, j:j + 1], rstd[:, j:j + 1], ALU.subtract, ALU.mult)\
                        .then_inc(xn_ready, 1)
                    if j >= 1:
                        xT_low(dve, b, j - 1)
                xT_low(dve, b, TB - 1)
                for j in range(TB):
                    dve.wait_ge(y_psum, b * TB + j + 1)
                    dve.tensor_tensor(row(j), bank[j][:, :], row(j), ALU.add).then_inc(x2_made, 1)
            dve.wait_ge(lora_in, 16 * 3 * (2 + NL))
            for i in range(NFIX):
                em, k = divmod(i, KB)
                e, m = divmod(em, 3)
                dve.wait_ge(fix_psum, i + 1)
                dve.tensor_tensor(w_full[:, e, m, k, :], bank[i % 4][:, :], w_full[:, e, m, k, :], ALU.add).then_inc(w_fixed, 1)

        @block.tensor
        def _(pe):
            pe.wait_ge(w_lo_made, 1)
            with pe.Fori(0, B) as b:
                pe.wait_ge(x2_made, b * TB + CREDIT)
                pe.wait_ge(c_lo_made, b + 1)
                for i in range(2):
                    for c in range(CB):
                        last = matmul3(pe, bank[4 + i][:, :], w_hi[:, i, c, :], w_lo[:, i, c, :], c_hi[:, c, :], c_lo[:, c, :],
                                       c == 0, c == CB - 1)
                    last.then_inc(qk_psum, 1)
                pe.wait_ge(qk_lo_made, b * 2 + 2)

                def turn(j):
                    pe.wait_ge(att_made, b * TB + j + 1)
                    if j >= 2:
                        pe.wait_ge(aT_lo_made, b * TB + j - 1)
                    for k in range(KB):
                        last = pe.transpose(bank[4 + j % 2][:, k * P:(k + 1) * P], att[:, j % 2, k * P:(k + 1) * P], ident[:, :])
                    last.then_inc(aT_psum, 1)

                for j in range(TB):
                    if j >= 2:
                        pe.wait_ge(exp_made, b * TB + j - 1)
                    matmul3(pe, bank[6 + j % 2][:, :], qk_hi[:, 0, j * P:(j + 1) * P], qk_lo[:, 0, j * P:(j + 1) * P],
                            qk_hi[:, 1, :], qk_lo[:, 1, :], True, True).then_inc(e_psum, 1)
                    if j >= 1:
                        turn(j - 1)
                turn(TB - 1)
                for j in range(TB):
                    pe.wait_ge(xn_ready, b * TB + j + 1)
                    for k in range(KB):
                        last = pe.transpose(bank[j][:, k * P:(k + 1) * P], xn[:, j % 2, k * P:(k + 1) * P], ident[:, :])
                    last.then_inc(xT_psum, 1)
                pe.wait_ge(aT_lo_made, b * TB + TB)
                pe.wait_ge(xT_lo_made, b * TB + TB)
                for j in range(TB):
                    for k in range(KB):
                        last = matmul3(pe, bank[j][:, :], xT_hi[:, k, j * P:(j + 1) * P], xT_lo[:, k, j * P:(j + 1) * P],
                                       aT_hi[:, k, :], aT_lo[:, k, :], k == 0, k == KB - 1)
                    last.then_inc(y_psum, 1)
            pe.wait_ge(x2_made, B * TB + CREDIT)
            pe.wait_ge(lora_in, 16 * 3 * (2 + NL))
            for i in range(NFIX):
                em, k = divmod(i, KB)
                e, m = divmod(em, 3)
                if i >= 4:
                    pe.wait_ge(w_fixed, i - 3)
                pe.matmul(bank[i % 4][:, :], down[:, e, m, k * P:(k + 1) * P], up[:, e, m, :], start=True, stop=True)\
                    .then_inc(fix_psum, 1)


def experts(nc, xres, ident, bank, Wg, Wu, Wd, w_fix, Wr, temperature):
    with ExitStack() as ctx:
        def sb(name, shape, dt=F32):
            return ctx.enter_context(nc.sbuf_tensor("e_" + name, shape, dt))

        def sem(name):
            return ctx.enter_context(nc.semaphore("e_" + name))

        xT_hi, xT_lo = sb("xT_hi", [P, KB, B * S], F32R), sb("xT_lo", [P, KB, B * S], F32R)
        raw = [sb("raw_gate", [P, KB, FH]), sb("raw_up", [P, KB, FH]), sb("raw_down", [P, FB, D])]
        w_hi = [[sb(f"{n}_hi{s}", [P, KB, FH] if n != "down" else [P, FB, D], F32R) for s in range(2)] for n in ("gate", "up", "down")]
        w_lo = [[sb(f"{n}_lo{s}", [P, KB, FH] if n != "down" else [P, FB, D], F32R) for s in range(2)] for n in ("gate", "up", "down")]
        silu = sb("silu", [P, FB, S])
        mid = sb("mid", [P, FB, S])
        mid_hi, mid_lo = sb("mid_hi", [P, 2, FB, S], F32R), sb("mid_lo", [P, 2, FB, S], F32R)
        xn = mid
        zero = sb("zero", [P, 1, 1])
        wr_raw = sb("wr_raw", [P, KB, P])
        wr_hi, wr_lo = sb("wr_hi", [P, KB, P], F32R), sb("wr_lo", [P, KB, P], F32R)
        logitsT = sb("logitsT", [P, S])
        stats, mean = sb("stats", [P, TB, 6]), sb("mean", [P, TB])
        var, rstd, tmp = sb("var", [P, TB]), sb("rstd", [P, TB]), sb("tmp", [P, TB])
        temp = sb("temp", [P, 2])
        E3 = [P, NT, NE]
        logits, inh, dist, zone, wts, fb, fbw, index, cand, mask = (
            sb(n, E3) for n in ("logits", "inh", "dist", "zone", "wts", "fb", "fbw", "index", "cand", "mask"))
        best, total = sb("best", [P, NT, 1]), sb("total", [P, NT, 1])
        none, some = sb("none", [P, NT, 1]), sb("some", [P, NT, 1])

        small_in, wr_zero, wr_hi_made, wr_lo_made = sem("small_in"), sem("wr_zero"), sem("wr_hi_made"), sem("wr_lo_made")
        index_set, temp_made, zero_set = sem("index_set"), sem("temp_made"), sem("zero_set")
        ln_chain, xn_ready, xT_psum, xT_hi_made, xT_lo_made = (
            sem("ln_chain"), sem("xn_ready"), sem("xT_psum"), sem("xT_hi_made"), sem("xT_lo_made"))
        lT_psum, lT_made, l_psum, l_made = sem("lT_psum"), sem("lT_made"), sem("l_psum"), sem("l_made")
        route_chain, inh_made, dist_made, exps_made = sem("route_chain"), sem("inh_made"), sem("dist_made"), sem("exps_made")
        raw_in = [sem(f"raw_in{m}") for m in range(3)]
        hi_made = [sem(f"hi_made{m}") for m in range(3)]
        lo_made = [sem(f"lo_made{m}") for m in range(3)]
        gate_psum, up_psum, silu_made, mid_made, mid_hi_made, mid_lo_made = (
            [sem(f"{n}{f}") for f in range(FB)] for n in ("gate_psum", "up_psum", "silu_made", "mid_made", "mid_hi_made", "mid_lo_made"))
        d_psum = [sem(f"d_psum{i}") for i in range(2)]
        acc_made = [sem(f"acc_made{j}") for j in range(TB)]

        UNITS = 2 * B

        block = ctx.enter_context(nc.Block())

        @block.sync
        def _(sp):
            sp.dma_start(temp[:, 0:1], temperature.rearrange("(a d) -> a d", a=1).broadcast_to([P, 1])).then_inc(small_in, 16)
            sp.wait_ge(wr_zero, 1)
            sp.dma_start(wr_raw[:, :, 0:NE], Wr.rearrange("(k p) e -> p k e", p=P)).then_inc(small_in, 16)

            def load(e, src):
                for h in range(2):
                    for m in range(3):
                        if e * 2 + h if isinstance(e, int) else True:
                            sp.wait_ge(lo_made[m], e * 2 + h)
                        w = src(m)
                        if m < 2:
                            w = w[:, h * FH:(h + 1) * FH].rearrange("(k p) f -> p k f", p=P)
                        else:
                            w = w[h * FH:(h + 1) * FH, :].rearrange("(k p) f -> p k f", p=P)
                        sp.dma_start(raw[m][:, :, :], w).then_inc(raw_in[m], 16)

            for e in range(NL):
                load(e, lambda m: w_fix[e, m, :, :])
            with sp.Fori(NL, NE) as e:
                sp.snap(e * (D * FF))
                load(e, lambda m: (Wg, Wu, Wd)[m][bass.ds(e, 1), :, :].rearrange("o a f -> (o a) f"))

        @block.gpsimd
        def _(pool):
            pool.memset(wr_raw[:, :, :], 0.0).then_inc(wr_zero, 1)
            for e in range(NE):
                pool.memset(index[:, :, e:e + 1], float(e)).then_inc(index_set, 1)

            def split(e, first):
                for h in range(2):
                    for m in range(3):
                        pool.wait_ge(raw_in[m], (e * 2 + h + 1) * 16)
                        if not first and m == 0:
                            pool.wait_ge(d_psum[1], (e - 1) * 16 + 8 * (h + 1) + CREDIT)
                        pool.tensor_tensor(w_hi[m][h][:, :, :], raw[m][:, :, :], zero[:, :, :].broadcast_to(raw[m].shape), ALU.add)\
                            .then_inc(hi_made[m], 1)
                        pool.wait_ge(hi_made[m], e * 2 + h + 1)
                        pool.tensor_tensor(w_lo[m][h][:, :, :], raw[m][:, :, :], w_hi[m][h][:, :, :].bitcast(F32), ALU.subtract)\
                            .then_inc(lo_made[m], 1)

            pool.memset(zero[:, :, :], 0.0).then_inc(zero_set, 1)
            pool.wait_ge(zero_set, 1)
            split(0, True)
            with pool.Fori(1, NE) as e:
                split(e, False)

        @block.scalar
        def _(act):
            for f in range(FB):
                act.sem_inc(silu_made[f], CREDIT)
                act.sem_inc(mid_hi_made[f], CREDIT)
            act.wait_ge(small_in, 32)
            act.activation(wr_hi[:, :, :], wr_raw[:, :, :], ACT.Copy).then_inc(wr_hi_made, 1)
            with act.Fori(0, B) as b:
                for j in range(TB):
                    act.wait_ge(xT_psum, b * TB + j + 1)
                    act.activation(xT_hi[:, :, bass.ds(b * S + j * P, P)], bank[j][:, :].rearrange("p (k t) -> p k t", k=KB), ACT.Copy)\
                        .then_inc(xT_hi_made, 1)
                act.wait_ge(lT_psum, b + 1)
                act.activation(logitsT[:, :], bank[4][:, :], ACT.Copy).then_inc(lT_made, 1)
            act.wait_ge(l_made, B + CREDIT)
            act.wait_ge(temp_made, 1)
            act.activation(inh[:, :, :], logits[:, :, :], ACT.Sigmoid, scale=temp[:, 1:2]).then_inc(inh_made, 1)
            act.wait_ge(dist_made, 1)
            act.activation(wts[:, :, :], dist[:, :, :], ACT.Exp, scale=-1.0 / 0.1).then_inc(exps_made, 1)
            act.activation(fb[:, :, :], dist[:, :, :], ACT.Exp, scale=-1.0 / 0.3).then_inc(exps_made, 1)
            with act.Fori(0, NE) as e:
                for u in range(UNITS):
                    n = e * UNITS + u
                    for f in range(FB):
                        act.wait_ge(gate_psum[f], n + 1)
                        act.wait_ge(mid_made[f], n + CREDIT)
                        act.activation(silu[:, f, :], bank[f][:, :], ACT.Silu).then_inc(silu_made[f], 1)
                        act.wait_ge(mid_made[f], n + 1 + CREDIT)
                        act.wait_ge(d_psum[u % 2], e * 16 + u // 2 * 4 + CREDIT)
                        act.activation(mid_hi[:, u % 2, f, :], mid[:, f, :], ACT.Copy).then_inc(mid_hi_made[f], 1)

        @block.vector
        def _(dve):
            for s in (*mid_made, *acc_made, xT_lo_made, l_made):
                dve.sem_inc(s, CREDIT)
            dve.wait_ge(small_in, 32)
            dve.reciprocal(temp[:, 1:2], temp[:, 0:1]).then_inc(temp_made, 1)
            dve.wait_ge(wr_hi_made, 1)
            dve.tensor_tensor(wr_lo[:, :, :], wr_raw[:, :, :], wr_hi[:, :, :].bitcast(F32), ALU.subtract).then_inc(wr_lo_made, 1)
            with dve.Fori(0, B) as b:
                def row(j):
                    return xres[:, bass.ds(b * TB + j, 1), :].rearrange("p o d -> p (o d)")

                def low(j):
                    dve.wait_ge(xT_hi_made, b * TB + j + 1)
                    cols = bass.ds(b * S + j * P, P)
                    dve.tensor_tensor(xT_lo[:, :, cols], bank[j][:, :].rearrange("p (k t) -> p k t", k=KB),
                                      xT_hi[:, :, cols].bitcast(F32), ALU.subtract).then_inc(xT_lo_made, 1)

                chain = Chain(dve, ln_chain, b * (TB + 9 + 3 * NEWTON))
                for j in range(TB):
                    chain.then(dve.bn_stats(stats[:, j, :], row(j)))
                moments(dve, stats, mean[:, :], var[:, :], tmp[:, :], chain)
                rsqrt_steps(dve, var[:, :], rstd[:, :], tmp[:, :], chain)
                for j in range(TB):
                    if j >= 2:
                        dve.wait_ge(xT_psum, b * TB + j - 1)
                    dve.tensor_scalar(xn[:, j % 2, :], row(j), mean[:, j:j + 1], rstd[:, j:j + 1], ALU.subtract, ALU.mult)\
                        .then_inc(xn_ready, 1)
                    if j >= 1:
                        low(j - 1)
                low(TB - 1)
                dve.wait_ge(l_psum, b + 1)
                dve.tensor_copy(logits[:, bass.ds(b * TB, TB), :], bank[5][:, :].rearrange("p (t e) -> p t e", t=TB)[:, :, 0:NE])\
                    .then_inc(l_made, 1)

            chain = Chain(dve, route_chain)

            def wide(v):
                return v[:, :, :].broadcast_to(E3)

            def all_(v):
                return v[:, :, :]

            def pick(values):
                chain.then(dve.tensor_reduce(all_(best), all_(values), AX.X, ALU.max))
                chain.then(dve.tensor_tensor(all_(cand), all_(values), wide(best), ALU.is_equal))
                chain.then(dve.scalar_tensor_tensor(out=all_(cand), in0=all_(cand), scalar=-float(NE), in1=all_(index),
                                                    op0=ALU.mult, op1=ALU.add))
                chain.then(dve.tensor_reduce(all_(best), all_(cand), AX.X, ALU.min))
                chain.then(dve.tensor_tensor(all_(cand), all_(cand), wide(best), ALU.is_equal))

            def normalise(values):
                chain.then(dve.tensor_reduce(all_(total), all_(values), AX.X, ALU.add))
                chain.then(dve.tensor_scalar(all_(total), all_(total), 1e-8, None, ALU.max))
                chain.then(dve.reciprocal(all_(total), all_(total)))
                chain.then(dve.tensor_tensor(all_(values), all_(values), wide(total), ALU.mult))

            dve.wait_ge(inh_made, 1)
            chain.then(dve.tensor_scalar(all_(dist), all_(inh), GOLDEN_CENTER, None, ALU.subtract))
            dve.scalar_tensor_tensor(out=all_(dist), in0=all_(dist), scalar=-1.0, in1=all_(dist), op0=ALU.mult, op1=ALU.max)\
                .then_inc(dist_made, 1)
            chain.then(dve.tensor_scalar(all_(zone), all_(inh), GOLDEN_LOWER, None, ALU.is_ge))
            chain.then(dve.scalar_tensor_tensor(out=all_(zone), in0=all_(inh), scalar=GOLDEN_UPPER, in1=all_(zone),
                                                op0=ALU.is_le, op1=ALU.mult))
            dve.wait_ge(exps_made, 2)
            chain.then(dve.tensor_tensor(all_(wts), all_(wts), all_(zone), ALU.mult))
            chain.then(dve.tensor_reduce(all_(total), all_(wts), AX.X, ALU.add))
            chain.then(dve.tensor_scalar(all_(none), all_(total), 1e-8, None, ALU.is_lt))
            chain.then(dve.tensor_scalar(all_(some), all_(none), -1.0, 1.0, ALU.mult, ALU.add))
            dve.wait_ge(index_set, NE)
            pick(fb)
            chain.then(dve.tensor_copy(all_(mask), all_(cand)))
            chain.then(dve.scalar_tensor_tensor(out=all_(fbw), in0=all_(mask), scalar=-2.0, in1=all_(fb), op0=ALU.mult, op1=ALU.add))
            pick(fbw)
            chain.then(dve.tensor_tensor(all_(mask), all_(mask), all_(cand), ALU.add))
            chain.then(dve.tensor_tensor(all_(fbw), all_(fb), all_(mask), ALU.mult))
            normalise(fbw)
            chain.then(dve.tensor_tensor(all_(fbw), all_(fbw), wide(none), ALU.mult))
            chain.then(dve.tensor_tensor(all_(wts), all_(wts), wide(some), ALU.mult))
            chain.then(dve.tensor_tensor(all_(wts), all_(wts), all_(fbw), ALU.add))
            normalise(wts)

            with dve.Fori(0, NE) as e:
                for u in range(UNITS):
                    n = e * UNITS + u
                    b = u % B
                    for f in range(FB):
                        dve.wait_ge(silu_made[f], n + 1 + CREDIT)
                        dve.wait_ge(up_psum[f], n + 1)
                        dve.wait_ge(mid_hi_made[f], n + CREDIT)
                        dve.tensor_tensor(mid[:, f, :], bank[2 + f][:, :], silu[:, f, :], ALU.mult).then_inc(mid_made[f], 1)
                        dve.wait_ge(mid_hi_made[f], n + 1 + CREDIT)
                        dve.tensor_tensor(mid_lo[:, u % 2, f, :], mid[:, f, :], mid_hi[:, u % 2, f, :].bitcast(F32), ALU.subtract)\
                            .then_inc(mid_lo_made[f], 1)
                    for j in range(TB):
                        dve.wait_ge(d_psum[u % 2], e * 16 + u // 2 * 4 + j + 1 + CREDIT)
                        blk = b * TB + j
                        dve.scalar_tensor_tensor(out=xres[:, blk, :], in0=bank[4 + j][:, :],
                                                 scalar=wts[:, blk:blk + 1, bass.ds(e, 1)].rearrange("p a o -> p (a o)"),
                                                 in1=xres[:, blk, :], op0=ALU.mult, op1=ALU.add).then_inc(acc_made[j], 1)

        @block.tensor
        def _(pe):
            for s in d_psum:
                pe.sem_inc(s, CREDIT)
            pe.wait_ge(wr_lo_made, 1)
            with pe.Fori(0, B) as b:
                for j in range(TB):
                    pe.wait_ge(xn_ready, b * TB + j + 1)
                    pe.wait_ge(xT_lo_made, b * TB + CREDIT)
                    for k in range(KB):
                        last = pe.transpose(bank[j][:, k * P:(k + 1) * P], xn[:, j % 2, k * P:(k + 1) * P], ident[:, :])
                    last.then_inc(xT_psum, 1)
                pe.wait_ge(xT_lo_made, b * TB + TB + CREDIT)
                for k in range(KB):
                    cols = bass.ds(b * S, S)
                    last = matmul3(pe, bank[4][:, :], wr_hi[:, k, :], wr_lo[:, k, :], xT_hi[:, k, cols], xT_lo[:, k, cols],
                                   k == 0, k == KB - 1)
                last.then_inc(lT_psum, 1)
                pe.wait_ge(lT_made, b + 1)
                pe.wait_ge(l_made, b + CREDIT)
                for j in range(TB):
                    last = pe.transpose(bank[5][:, j * P:(j + 1) * P], logitsT[:, j * P:(j + 1) * P], ident[:, :])
                last.then_inc(l_psum, 1)
            pe.wait_ge(l_made, B + CREDIT)
            with pe.Fori(0, NE) as e:
                for u in range(UNITS):
                    n = e * UNITS + u
                    h, b = divmod(u, B)
                    if b == 0:
                        for m in range(3):
                            pe.wait_ge(lo_made[m], e * 2 + h + 1)
                    for f in range(FB):
                        for m, psum, free in ((0, gate_psum, silu_made), (1, up_psum, mid_made)):
                            pe.wait_ge(free[f], n + CREDIT)
                            for k in range(KB):
                                last = matmul3(pe, bank[2 * m + f][:, :], w_hi[m][h][:, k, f * P:(f + 1) * P],
                                               w_lo[m][h][:, k, f * P:(f + 1) * P], xT_hi[:, k, b * S:(b + 1) * S],
                                               xT_lo[:, k, b * S:(b + 1) * S], k == 0, k == KB - 1)
                            last.then_inc(psum[f], 1)
                    for f in range(FB):
                        pe.wait_ge(mid_lo_made[f], n + 1)
                        for j in range(TB):
                            if f == 0:
                                pe.wait_ge(acc_made[j], n + CREDIT)
                            last = matmul3(pe, bank[4 + j][:, :], mid_hi[:, u % 2, f, j * P:(j + 1) * P],
                                           mid_lo[:, u % 2, f, j * P:(j + 1) * P], w_hi[2][h][:, f, :], w_lo[2][h][:, f, :],
                                           f == 0, f == FB - 1)
                            if f == FB - 1:
                                last.then_inc(d_psum[u % 2], 1)



def kernel(**inputs):
    from concourse import bacc, mybir as mb
    from concourse.bass_utils import run_bass_kernel_spmd as run

    def turned(a, axes):
        return np.ascontiguousarray(np.transpose(np.asarray(a), axes))

    i = {k.removeprefix("L0_"): v for k, v in inputs.items()}
    laid = {
        "x": np.asarray(i["x"]),
        "ctxT": turned(i["ctx_1024"], (0, 2, 1)),
        "w_qkvT": turned(i["attn_w_qkv"], (1, 0)),
        "w_outT": turned(i["attn_w_out"], (1, 0)),
        "b_out": np.asarray(i["attn_b_out"]),
        "wqT": turned(i["xattn_Wq"], (1, 0)), "bq": np.asarray(i["xattn_bq"]),
        "wkT": turned(i["xattn_Wk"], (1, 0)), "bk": np.asarray(i["xattn_bk"]),
        "Wg": np.asarray(i["ffn_Wg"]), "Wu": np.asarray(i["ffn_Wu"]), "Wd": np.asarray(i["ffn_Wd"]),
        "GaT": turned(i["ffn_Ga"], (0, 2, 1)), "Gb": np.asarray(i["ffn_Gb"]),
        "UaT": turned(i["ffn_Ua"], (0, 2, 1)), "Ub": np.asarray(i["ffn_Ub"]),
        "DaT": turned(i["ffn_Da"], (0, 2, 1)), "Db": np.asarray(i["ffn_Db"]),
        "Wr": np.asarray(i["ffn_Wr"]), "temperature": np.asarray(i["ffn_temperature"]),
        "ident_in": np.eye(P, dtype=np.float32),
    }
    nc = bacc.Bacc("TRN2", target_bir_lowering=False, num_devices=1)
    arrays, aps = {}, {}
    for name, a in laid.items():
        a = np.ascontiguousarray(a)
        arrays[name] = a
        aps[name] = nc.dram_tensor(name, a.shape, mb.dt.from_np(a.dtype), kind="ExternalInput").ap()
    out = nc.dram_tensor("out", (B, S, D), F32, kind="ExternalOutput").ap()
    build(nc, **aps, out=out)
    r = run(nc, [arrays], core_ids=[0])
    return r.results[0]["out"]
```

```python
import math
from contextlib import ExitStack

import numpy as np

import concourse.bass as bass
from concourse import mybir

F32 = mybir.dt.float32
F32R = mybir.dt.float32r
I32 = mybir.dt.int32
U32 = mybir.dt.uint32
ALU = mybir.AluOpType
ACT = mybir.ActivationFunctionType
AX = mybir.AxisListType

P = 128
B, S, D = 4, 512, 512
KB = D // P
TB = S // P
NT = B * TB
H, HD = 16, 32
HG = P // HD
NG = H // HG
NPAIR = H // 2
C = 256
CB = C // P
NE, FF, NL, R = 8, 512, 2, 64
FH = FF // 2
FB = FH // P
CREDIT = 1
LN_EPS = 1e-5
ATT_SCALE = 1.0 / math.sqrt(HD)
GOLDEN_CENTER = 1.0 / math.e
GOLDEN_LOWER = 0.5 - math.log(4.0 / 3.0)
GOLDEN_UPPER = 0.5

SLOTS = 4
STACK = 3 * HD
SHIFT = 2 * TB
PRING = 4
LAG = 3
VW = HD + 1
NSTEP = H * TB
NEWTON = 4


def matmul3(pe, out, w_hi, w_lo, x_hi, x_lo, first, last):
    pe.matmul(out, w_hi, x_hi, start=first, stop=False)
    pe.matmul(out, w_hi, x_lo, start=False, stop=False)
    return pe.matmul(out, w_lo, x_hi, start=False, stop=last)


def moments(dve, stats, mean, var, tmp, chain):
    even, odd, sq_even, sq_odd = (stats[:, :, i] for i in (1, 4, 2, 5))
    chain.then(dve.tensor_tensor(mean, even, odd, ALU.add))
    chain.then(dve.tensor_scalar(mean, mean, 0.5, None, ALU.mult))
    chain.then(dve.tensor_tensor(tmp, even, odd, ALU.subtract))
    chain.then(dve.scalar_tensor_tensor(out=tmp, in0=tmp, scalar=0.25, in1=tmp, op0=ALU.mult, op1=ALU.mult))
    chain.then(dve.tensor_tensor(var, sq_even, sq_odd, ALU.add))
    chain.then(dve.scalar_tensor_tensor(out=var, in0=var, scalar=1.0 / D, in1=tmp, op0=ALU.mult, op1=ALU.add))


def rsqrt_guess(dve, var, y, tmp, chain):
    chain.then(dve.tensor_scalar(var, var, LN_EPS, None, ALU.add))
    chain.then(dve.tensor_scalar(tmp.bitcast(U32), var.bitcast(U32), 1, None, ALU.logical_shift_right))
    chain.then(dve.tensor_scalar(y.bitcast(I32), tmp.bitcast(I32), -1.0, float(0x5F3759DF), ALU.mult, ALU.add))


def newton_step(dve, var, y, tmp, chain):
    chain.then(dve.scalar_tensor_tensor(out=tmp, in0=y, scalar=-0.5, in1=y, op0=ALU.mult, op1=ALU.mult))
    chain.then(dve.tensor_tensor(tmp, tmp, var, ALU.mult))
    chain.then(dve.scalar_tensor_tensor(out=y, in0=tmp, scalar=1.5, in1=y, op0=ALU.add, op1=ALU.mult))


def rsqrt_steps(dve, var, y, tmp, chain):
    rsqrt_guess(dve, var, y, tmp, chain)
    for _ in range(NEWTON):
        newton_step(dve, var, y, tmp, chain)


class Chain:

    def __init__(self, eng, sem, base=0):
        self.eng, self.sem, self.base, self.n = eng, sem, base, 0

    def then(self, instruction):
        self.n += 1
        instruction.then_inc(self.sem, 1)
        self.eng.wait_ge(self.sem, self.base + self.n)


def build(nc, x, ctxT, w_qkvT, w_outT, b_out, wqT, bq, wkT, bk, Wg, Wu, Wd, GaT, Gb, UaT, Ub, DaT, Db, Wr,
          temperature, ident_in, out, stop=3):
    xt = x.rearrange("b (t p) d -> p (b t) d", p=P)
    outt = out.rearrange("b (t p) d -> p (b t) d", p=P)
    w_fix = nc.dram_tensor("w_fix", [NL, 3, D, FF], F32, kind="Internal").ap()
    with ExitStack() as whole:
        xres = whole.enter_context(nc.sbuf_tensor("xres", [P, NT, D], F32))
        ident = whole.enter_context(nc.sbuf_tensor("ident", [P, P], F32))
        bank = [whole.enter_context(nc.psum_tensor(f"bank{i}", [P, 512], F32)) for i in range(8)]
        self_attention(nc, xres, ident, bank, xt, w_qkvT, w_outT, b_out, ident_in)
        if stop >= 2:
            cross_attention(nc, xres, ident, bank, ctxT, wqT, bq, wkT, bk, Wg, Wu, Wd, GaT, Gb, UaT, Ub, DaT, Db, w_fix)
        if stop >= 3:
            experts(nc, xres, ident, bank, Wg, Wu, Wd, w_fix, Wr, temperature)
        with nc.semaphore("out_stored") as out_stored, nc.Block() as block:
            @block.sync
            def _(sp):
                for b in range(B):
                    sp.dma_start(outt[:, b * TB:(b + 1) * TB, :], xres[:, b * TB:(b + 1) * TB, :]).then_inc(out_stored, 16)
                sp.wait_ge(out_stored, 16 * B)


def self_attention(nc, xres, ident, bank, xt, w_qkvT, w_outT, b_out, ident_in):
    with ExitStack() as ctx:
        def sb(name, shape, dt=F32):
            return ctx.enter_context(nc.sbuf_tensor("a_" + name, shape, dt))

        def sem(name):
            return ctx.enter_context(nc.semaphore("a_" + name))

        w_hi, w_lo = sb("w_hi", [P, KB, 3 * D], F32R), sb("w_lo", [P, KB, 3 * D], F32R)
        wo_hi, wo_lo = sb("wo_hi", [P, KB, D], F32R), sb("wo_lo", [P, KB, D], F32R)
        xT_hi, xT_lo = sb("xT_hi", [P, KB, S], F32R), sb("xT_lo", [P, KB, S], F32R)
        stack = sb("stack", [P, SLOTS, 2, 2, S], F32R)
        qk_parts = sb("qk_parts", [P, 4, S], F32R)
        v_ones = sb("v_ones", [P, TB, H, VW])
        probs = sb("probs", [P, PRING, S])
        xn = sb("xn", [P, 2, D])
        pv = sb("pv", [P, 2, TB, TB, VW])
        weighed = sb("weighed", [P, TB, TB, HD])
        half_sum, o_sum = sb("half_sum", [P, 2, TB, HD]), sb("o_sum", [P, TB, HD])
        l_part = sb("l_part", [P, TB, TB])
        l_sum, l_rec = sb("l_sum", [P, TB, 1]), sb("l_rec", [P, 2, TB, 1])
        o_group = sb("o_group", [P, TB, P])
        OT_hi, OT_lo = sb("OT_hi", [P, NG, S], F32R), sb("OT_lo", [P, NG, S], F32R)
        bo = sb("bo", [P, D])
        stats, mean = sb("stats", [P, TB, 6]), sb("mean", [P, TB])
        var, rstd, tmp = sb("var", [P, TB]), sb("rstd", [P, TB]), sb("tmp", [P, TB])
        row_max, gap, gain = (sb(n, [P, 2, TB, 2 * TB]) for n in ("row_max", "gap", "gain"))
        whole_max = sb("whole_max", [P, 2 * TB])
        neg_shift = sb("neg_shift", [P, 2 * TB, TB])
        shift_parts = sb("shift_parts", [P, 2 * TB, 2, TB], F32R)
        block_one = sb("block_one", [P, TB])

        x_in, w_raw, wo_raw, small_in = sem("x_in"), sem("w_raw"), sem("wo_raw"), sem("small_in")
        w_hi_made, w_lo_made, wo_hi_made, wo_lo_made = sem("w_hi_made"), sem("w_lo_made"), sem("wo_hi_made"), sem("wo_lo_made")
        ones_set = sem("ones_set")
        ln_chain, xn_ready, xT_psum, xT_hi_made, xT_lo_made = (
            sem("ln_chain"), sem("xn_ready"), sem("xT_psum"), sem("xT_hi_made"), sem("xT_lo_made"))
        qk_psum, qk_hi_made, qk_lo_made = sem("qk_psum"), sem("qk_hi_made"), sem("qk_lo_made")
        v_psum, v_made = sem("v_psum"), sem("v_made")
        stack_in = [sem(f"stack_in{i}") for i in range(SLOTS)]
        s_psum, max_made, whole_made, gap_made, shift_made, shift_hi_made, shift_lo_made, gain_made = (
            sem("s_psum"), sem("max_made"), sem("whole_made"), sem("gap_made"), sem("shift_made"),
            sem("shift_hi_made"), sem("shift_lo_made"), sem("gain_made"))
        shiftT_psum, shift_rows_made = sem("shiftT_psum"), sem("shift_rows_made")
        st_psum, exp_made, pv_psum, pv_made = sem("st_psum"), sem("exp_made"), sem("pv_psum"), sem("pv_made")
        l_part_made, l_sum_made, l_rec_made, combine_chain = (
            sem("l_part_made"), sem("l_sum_made"), sem("l_rec_made"), sem("combine_chain"))
        OT_psum, OT_hi_made, OT_lo_made, y_psum, bias_added, x1_made = (
            sem("OT_psum"), sem("OT_hi_made"), sem("OT_lo_made"), sem("y_psum"), sem("bias_added"), sem("x1_made"))

        NCH = KB * 3
        TP = 2 * TB
        ROWS = STACK + SHIFT
        Q_HI, K_LO, Q_LO, K_HI = range(4)
        LAST = NSTEP + 9
        Y_BANK = (7, 4, 5, 6)
        LN_SCALE_STEP = 16
        OT_STEPS = [24, 40, 56, LAST - 2]
        LN_ROW_STEPS = (22, 24, 27, 29)

        def staged(i):
            return xres[:, TB + i, :]

        def stacks_ready(b, p):
            return (b * (NPAIR // SLOTS) + p // SLOTS + 1) * 96

        def o_done(b, h):
            return (b * H + h + 1) * 4

        def wrap(b, p, more):
            if p < NPAIR:
                return b, p
            return (b + 1, p - NPAIR) if more else None

        def over_batches(eng, batch):
            with eng.Fori(0, B - 1) as b:
                batch(b, True)
            batch(B - 1, False)

        def row(b, j):
            if isinstance(b, int):
                return xres[:, b * TB + j, :]
            return xres[:, bass.ds(b * TB + j, 1), :].rearrange("p o d -> p (o d)")

        block = ctx.enter_context(nc.Block())

        @block.sync
        def _(sp):
            sp.dma_start(ident[:, :], ident_in).then_inc(small_in, 16)
            sp.dma_start(bo[:, :], b_out.rearrange("(a d) -> a d", a=1).broadcast_to([P, D])).then_inc(small_in, 16)
            for part in range(2):
                r0 = STACK + part * TB
                sp.dma_start(block_one[r0:r0 + TB, :], ident_in[0:TB, 0:TB]).then_inc(small_in, 16)
            sp.dma_start(xres[:, 0:TB, :], xt[:, 0:TB, :]).then_inc(x_in, 16)
            for k in range(KB):
                if k:
                    sp.wait_ge(w_raw, 16 * k)
                sp.dma_start(xres[:, TB + 3 * k:TB + 3 * k + 3, :],
                             w_qkvT[k * P:(k + 1) * P, :].rearrange("p (c n) -> p c n", n=D)).then_inc(w_raw, 16)

            def load_stacks(b, p, at_start=False):
                s, g, r0 = p % SLOTS, p // 2, (p % 2) * 2 * HD
                split = b * 2 * NG + 2 * g + 2
                free = b * NSTEP + (p - SLOTS + 1) * TP
                if not isinstance(b, int):
                    split, free = sp.to_reg(split), sp.to_reg(free)
                sp.wait_ge(qk_lo_made, split)
                if not at_start:
                    sp.wait_ge(st_psum, free)
                for hh in range(2):
                    rows = slice(r0 + hh * HD, r0 + (hh + 1) * HD)
                    for r, parts in enumerate((slice(Q_HI, K_HI + 1, K_HI - Q_HI), slice(Q_HI, K_LO + 1), slice(Q_LO, K_HI + 1))):
                        sp.dma_start(stack[r * HD:(r + 1) * HD, s, hh, :, :].bitcast(F32),
                                     qk_parts[rows, parts, :].bitcast(F32)).then_inc(stack_in[s], 16)

            load_stacks(0, 0, True)
            load_stacks(0, 1, True)
            load_stacks(0, 2, True)
            sp.wait_ge(w_lo_made, NCH)
            sp.dma_start(xres[:, TB:2 * TB, :], w_outT.rearrange("(k p) n -> p k n", p=P)).then_inc(wo_raw, 16)
            sp.wait_ge(wo_lo_made, KB)
            sp.wait_ge(x_in, 16)
            sp.dma_start(xres[:, TB:NT, :], xt[:, TB:NT, :]).then_inc(x_in, 16)

            def batch(b, more):
                for p in range(NPAIR):
                    ahead = wrap(b, p + 3, more)
                    if ahead:
                        load_stacks(*ahead)

            over_batches(sp, batch)

        @block.gpsimd
        def _(pool):
            pool.memset(v_ones[:, :, :, HD:VW], 1.0).then_inc(ones_set, 1)
            for i in range(NCH):
                pool.wait_ge(w_hi_made, i + 1)
                k, c = divmod(i, 3)
                pool.tensor_tensor(w_lo[:, k, c * D:(c + 1) * D], staged(i), w_hi[:, k, c * D:(c + 1) * D].bitcast(F32),
                                   ALU.subtract).then_inc(w_lo_made, 1)
            for k in range(KB):
                pool.wait_ge(wo_hi_made, k + 1)
                pool.tensor_tensor(wo_lo[:, k, :], xres[:, TB + k, :], wo_hi[:, k, :].bitcast(F32), ALU.subtract)\
                    .then_inc(wo_lo_made, 1)
            pool.wait_ge(small_in, 64)

            def add_bias(b):
                for j in range(TB):
                    pool.wait_ge(xn_ready, b * TB + j + 1)
                    pool.tensor_tensor(row(b, j), row(b, j), bo[:, :], ALU.add).then_inc(bias_added, 1)

            def batch(b, more):
                for h in range(H):
                    chain = Chain(pool, combine_chain, (b * H + h) * 4)
                    pool.wait_ge(pv_made, b * NSTEP + TB * (h + 1))
                    chain.then(pool.tensor_tensor(weighed[:, :, :, :], pv[:, h % 2, :, :, 0:HD],
                                                  pv[:, h % 2, :, :, HD:VW].broadcast_to([P, TB, TB, HD]), ALU.mult))
                    chain.then(pool.tensor_tensor(half_sum[:, :, :, :], weighed[:, 0:2, :, :], weighed[:, 2:4, :, :], ALU.add))
                    chain.then(pool.tensor_tensor(o_sum[:, :, :], half_sum[:, 0, :, :], half_sum[:, 1, :, :], ALU.add))
                    pool.wait_ge(l_rec_made, b * H + h + 1)
                    if h % HG == 0 and h:
                        pool.wait_ge(OT_psum, b * NG + h // HG)
                    chain.then(pool.tensor_tensor(o_group[:, :, (h % HG) * HD:(h % HG + 1) * HD], o_sum[:, :, :],
                                                  l_rec[:, h % 2, :, :].broadcast_to([P, TB, HD]), ALU.mult))
                    if h == 9 and more:
                        add_bias(b + 1)

            add_bias(0)
            over_batches(pool, batch)

        @block.scalar
        def _(act):
            def xT_high(b, j):
                act.wait_ge(xT_psum, b * TB + j + 1)
                act.activation(xT_hi[:, :, j * P:(j + 1) * P], bank[7][:, :].rearrange("p (k t) -> p k t", k=KB), ACT.Copy)\
                    .then_inc(xT_hi_made, 1)

            def qk_high(b, g, which, at_start=False):
                act.wait_ge(qk_psum, b * 2 * NG + 2 * g + which + 1)
                if which == 0 and not at_start:
                    for p in (2 * g - 2, 2 * g - 1):
                        bb, pp = (b, p) if p >= 0 else (b - 1, p + NPAIR)
                        act.wait_ge(stack_in[pp % SLOTS], stacks_ready(bb, pp))
                act.activation(qk_parts[:, K_HI if which else Q_HI, :], bank[7][:, :], ACT.Copy).then_inc(qk_hi_made, 1)

            def v_copy(b, t):
                act.wait_ge(v_psum, b * TB + t + 1)
                act.activation(v_ones[:, t, :, 0:HD], bank[4 + t % 2][:, :].rearrange("p (h d) -> p h d", h=H), ACT.Copy)\
                    .then_inc(v_made, 1)

            def gains(b, p, used=None):
                act.wait_ge(gap_made, b * NPAIR + p + 1)
                if used is not None:
                    act.wait_ge(l_part_made, used)
                act.activation(gain[:, p % 2, :, :], gap[:, p % 2, :, :], ACT.Exp, scale=0.5 * ATT_SCALE).then_inc(gain_made, 1)

            def shift_rows(b, p, hh):
                act.wait_ge(shiftT_psum, b * H + 2 * p + hh + 1)
                act.activation(stack[STACK:ROWS, p % SLOTS, hh, 0, :], bank[6][0:SHIFT, :], ACT.Copy).then_inc(shift_rows_made, 1)

            def batch(b, more):
                for n in range(LAST):
                    p, t = divmod(n, TP)
                    if n < NSTEP:
                        act.wait_ge(st_psum, b * NSTEP + n + 1)
                        if n >= PRING:
                            act.wait_ge(pv_psum, b * NSTEP + n - PRING + 1)
                        act.activation(probs[:, n % PRING, :], bank[2 + n % 2][:, :], ACT.Exp, scale=ATT_SCALE).then_inc(exp_made, 1)
                        ahead = wrap(b, p + 4, more)
                        if p % 2 == 0 and t in (3, 7) and ahead:
                            qk_high(ahead[0], ahead[1] // 2, t // 4)
                        if p == 3 and t % 2 and more:
                            xT_high(b + 1, t // 2)
                        ahead = wrap(b, p + 1, more)
                        if t in (4, 6) and ahead:
                            shift_rows(*ahead, t // 6)
                        if t == 5 and ahead:
                            gains(*ahead, used=b * H + 2 * p if p else None)
                    m = n - LAG - 1
                    if 0 <= m < NSTEP:
                        h, kb = divmod(m, TB)
                        act.wait_ge(pv_psum, b * NSTEP + m + 1)
                        if kb == 0 and h >= 2:
                            act.wait_ge(combine_chain, o_done(b, h - 2))
                            act.wait_ge(l_part_made, b * H + h - 1)
                        act.activation(pv[:, h % 2, kb, :, :], bank[4 + m % 2][:, 0:TB * VW].rearrange("p (t w) -> p t w", w=VW), ACT.Copy)\
                            .then_inc(pv_made, 1)
                    if more and NSTEP + LAG <= n < NSTEP + LAG + TB:
                        v_copy(b + 1, n - NSTEP - LAG)
                    if n in OT_STEPS:
                        g = OT_STEPS.index(n)
                        act.wait_ge(OT_psum, b * NG + g + 1)
                        act.activation(OT_hi[:, g, :], bank[6][:, :], ACT.Copy).then_inc(OT_hi_made, 1)

            for i in range(NCH):
                k, c = divmod(i, 3)
                act.wait_ge(w_raw, 16 * (k + 1))
                act.activation(w_hi[:, k, c * D:(c + 1) * D], staged(i), ACT.Copy).then_inc(w_hi_made, 1)
                if i % 3 == 2:
                    xT_high(0, k)
            qk_high(0, 0, 0, True)
            qk_high(0, 0, 1, True)
            for t in range(TB):
                v_copy(0, t)
            qk_high(0, 1, 0)
            qk_high(0, 1, 1)
            shift_rows(0, 0, 0)
            shift_rows(0, 0, 1)
            gains(0, 0)
            for k in range(KB):
                act.wait_ge(wo_raw, 16)
                act.activation(wo_hi[:, k, :], xres[:, TB + k, :], ACT.Copy).then_inc(wo_hi_made, 1)
            over_batches(act, batch)

        @block.vector
        def _(dve):
            def ln_stats(b, j):
                if j == 0:
                    dve.wait_ge(x_in, 16 if isinstance(b, int) and b == 0 else 32)
                dve.bn_stats(stats[:, j, :], row(b, j)).then_inc(ln_chain, 1)

            def ln_scale(b, part):
                base = b * (TB + 9 + 3 * NEWTON)
                before = TB + (0, 6)[part > 0] + 3 * max(part - 1, 0)
                if part == 0:
                    dve.wait_ge(ln_chain, base + TB)
                chain = Chain(dve, ln_chain, base + before)
                if part == 0:
                    moments(dve, stats, mean[:, :], var[:, :], tmp[:, :], chain)
                elif part == 1:
                    rsqrt_guess(dve, var[:, :], rstd[:, :], tmp[:, :], chain)
                else:
                    newton_step(dve, var[:, :], rstd[:, :], tmp[:, :], chain)

            def ln_row(b, j):
                if j >= 2:
                    dve.wait_ge(xT_psum, b * TB + j - 1)
                dve.tensor_scalar(xn[:, j % 2, :], row(b, j), mean[:, j:j + 1], rstd[:, j:j + 1], ALU.subtract, ALU.mult)\
                    .then_inc(xn_ready, 1)

            def xT_low(b, j):
                dve.wait_ge(xT_hi_made, b * TB + j + 1)
                dve.tensor_tensor(xT_lo[:, :, j * P:(j + 1) * P], bank[7][:, :].rearrange("p (k t) -> p k t", k=KB),
                                  xT_hi[:, :, j * P:(j + 1) * P].bitcast(F32), ALU.subtract).then_inc(xT_lo_made, 1)

            def qk_low(b, g, which):
                dve.wait_ge(qk_hi_made, b * 2 * NG + 2 * g + which + 1)
                dve.tensor_tensor(qk_parts[:, K_LO if which else Q_LO, :], bank[7][:, :],
                                  qk_parts[:, K_HI if which else Q_HI, :].bitcast(F32), ALU.subtract).then_inc(qk_lo_made, 1)

            def tile_max(b, p, t):
                dve.wait_ge(s_psum, b * NSTEP + p * TP + t + 1)
                dve.reduce_max(row_max[:, p % 2, :, t:t + 1], bank[t % 2][:, :].rearrange("q (k n) -> q k n", k=TB), AX.X)\
                    .then_inc(max_made, 1)

            def shifts(b, p):
                i = b * NPAIR + p + 1
                dve.wait_ge(max_made, i * TP)
                dve.tensor_reduce(whole_max[:, :], row_max[:, p % 2, :, :].rearrange("q k x -> q x k"), AX.X, ALU.max)\
                    .then_inc(whole_made, 1)
                dve.wait_ge(whole_made, i)
                dve.tensor_tensor(gap[:, p % 2, :, :], row_max[:, p % 2, :, :],
                                  whole_max[:, :].rearrange("q (o x) -> q o x", o=1).broadcast_to([P, TB, 2 * TB]), ALU.subtract)\
                    .then_inc(gap_made, 1)
                dve.wait_ge(gap_made, i)
                dve.scalar_tensor_tensor(out=neg_shift[:, :, :].rearrange("q x k -> q k x"), in0=gap[:, p % 2, :, :], scalar=0.5,
                                         in1=row_max[:, p % 2, :, :], op0=ALU.mult, op1=ALU.subtract).then_inc(shift_made, 1)
                dve.wait_ge(shift_made, i)
                dve.tensor_copy(shift_parts[:, :, 0, :], neg_shift[:, :, :]).then_inc(shift_hi_made, 1)
                dve.wait_ge(shift_hi_made, i)
                dve.tensor_tensor(shift_parts[:, :, 1, :], neg_shift[:, :, :], shift_parts[:, :, 0, :].bitcast(F32), ALU.subtract)\
                    .then_inc(shift_lo_made, 1)

            def batch(b, more):
                for n in range(LAST):
                    p, t = divmod(n, TP)
                    if n < NSTEP:
                        ahead = wrap(b, p + 2, more)
                        if ahead:
                            tile_max(*ahead, t)
                        ahead = wrap(b, p + 1, more)
                        if t == 1 and ahead:
                            shifts(*ahead)
                        ahead = wrap(b, p + 4, more)
                        if p % 2 == 0 and t in (3, 7) and ahead:
                            qk_low(ahead[0], ahead[1] // 2, t // 4)
                    if more and p == 1 and t % 2:
                        ln_stats(b + 1, t // 2)
                    if more and 0 <= n - LN_SCALE_STEP < 2 + NEWTON:
                        ln_scale(b + 1, n - LN_SCALE_STEP)
                    if more and n in LN_ROW_STEPS:
                        ln_row(b + 1, LN_ROW_STEPS.index(n))
                    if more and n in (26, 28, 30, 32):
                        xT_low(b + 1, (n - 26) // 2)
                    h = (n - LAG - 5) // TB
                    if h >= 0 and (n - LAG - 5) % TB == 0 and h < H:
                        i = b * H + h + 1
                        hh = h % 2
                        dve.wait_ge(pv_made, b * NSTEP + TB * (h + 1))
                        dve.wait_ge(gain_made, b * NPAIR + h // 2 + 1)
                        dve.tensor_tensor(l_part[:, :, :], pv[:, h % 2, :, :, HD:VW].rearrange("p k t o -> p k (t o)"),
                                          gain[:, h // 2 % 2, :, hh * TB:(hh + 1) * TB], ALU.mult).then_inc(l_part_made, 1)
                        dve.wait_ge(l_part_made, i)
                        dve.tensor_reduce(l_sum[:, :, 0], l_part[:, :, :].rearrange("p k t -> p t k"), AX.X, ALU.add)\
                            .then_inc(l_sum_made, 1)
                        dve.wait_ge(l_sum_made, i)
                        if h >= 2:
                            dve.wait_ge(combine_chain, o_done(b, h - 2))
                        dve.reciprocal(l_rec[:, h % 2, :, :], l_sum[:, :, :]).then_inc(l_rec_made, 1)
                    if n - 1 in OT_STEPS:
                        g = OT_STEPS.index(n - 1)
                        dve.wait_ge(OT_hi_made, b * NG + g + 1)
                        dve.tensor_tensor(OT_lo[:, g, :], bank[6][:, :], OT_hi[:, g, :].bitcast(F32), ALU.subtract)\
                            .then_inc(OT_lo_made, 1)
                for j in range(TB):
                    dve.wait_ge(y_psum, b * TB + j + 1)
                    dve.wait_ge(bias_added, b * TB + j + 1)
                    dve.tensor_tensor(row(b, j), bank[Y_BANK[j]][:, :], row(b, j), ALU.add).then_inc(x1_made, 1)

            for j in range(TB):
                ln_stats(0, j)
            for part in range(2 + NEWTON):
                ln_scale(0, part)
            for j in range(TB):
                ln_row(0, j)
                if j:
                    xT_low(0, j - 1)
            xT_low(0, TB - 1)
            dve.wait_ge(small_in, 64)
            for s in range(SLOTS):
                dve.tensor_copy(stack[STACK:ROWS, s, :, 1, :].rearrange("r h (k n) -> r h k n", k=TB),
                                block_one[STACK:ROWS, :].rearrange("r (a k b) -> r a k b", a=1, b=1)
                                .broadcast_to([SHIFT, 2, TB, P])).then_inc(ones_set, 1)
            dve.sem_inc(x1_made, TB)
            qk_low(0, 0, 0)
            qk_low(0, 0, 1)
            qk_low(0, 1, 0)
            qk_low(0, 1, 1)
            for p in range(2):
                for t in range(TP):
                    tile_max(0, p, t)
                if p == 0:
                    shifts(0, 0)
            over_batches(dve, batch)

        @block.tensor
        def _(pe):
            def turn_row(b, j):
                pe.wait_ge(xn_ready, b * TB + j + 1)
                if j:
                    pe.wait_ge(xT_lo_made, b * TB + j)
                for k in range(KB):
                    last = pe.transpose(bank[7][:, k * P:(k + 1) * P], xn[:, j % 2, k * P:(k + 1) * P], ident[:, :])
                last.then_inc(xT_psum, 1)

            def qk(b, g, which, ks):
                cols = slice(which * D + g * P, which * D + (g + 1) * P)
                for k in ks:
                    last = matmul3(pe, bank[7][:, :], w_hi[:, k, cols], w_lo[:, k, cols], xT_hi[:, k, :], xT_lo[:, k, :],
                                   k == 0, k == KB - 1)
                if ks[-1] == KB - 1:
                    last.then_inc(qk_psum, 1)

            def values(b, t):
                for k in range(KB):
                    last = matmul3(pe, bank[4 + t % 2][:, :], xT_hi[:, k, t * P:(t + 1) * P], xT_lo[:, k, t * P:(t + 1) * P],
                                   w_hi[:, k, 2 * D:], w_lo[:, k, 2 * D:], k == 0, k == KB - 1)
                last.then_inc(v_psum, 1)

            def scores(b, p, t, first=False):
                hh, qb = divmod(t, TB)
                if t == 0:
                    pe.wait_ge(stack_in[p % SLOTS], stacks_ready(b, p))
                if not first:
                    pe.wait_ge(max_made, b * NSTEP + p * TP + t - 1)
                pe.matmul(bank[t % 2][:, :], stack[0:STACK, p % SLOTS, hh, 0, qb * P:(qb + 1) * P],
                          stack[0:STACK, p % SLOTS, hh, 1, :], start=True, stop=True).then_inc(s_psum, 1)

            def turn_shifts(b, p, hh):
                pe.wait_ge(shift_lo_made, b * NPAIR + p + 1)
                for qb in range(TB):
                    last = pe.transpose(bank[6][0:SHIFT, qb * P:(qb + 1) * P],
                                        shift_parts[:, hh * TB + qb, :, :].bitcast(F32).rearrange("q a k -> q (a k)"), ident[:, :])
                last.then_inc(shiftT_psum, 1)

            def batch(b, more):
                for n in range(LAST):
                    p, t = divmod(n, TP)
                    if n < NSTEP:
                        ahead = wrap(b, p + 2, more)
                        if ahead:
                            scores(*ahead, t)
                        hh, kb = divmod(t, TB)
                        if kb == 0:
                            pe.wait_ge(shift_rows_made, b * H + 2 * p + hh + 1)
                        if n >= 2:
                            pe.wait_ge(exp_made, b * NSTEP + n - 1)
                        pe.matmul(bank[2 + n % 2][:, :], stack[0:ROWS, p % SLOTS, hh, 1, kb * P:(kb + 1) * P],
                                  stack[0:ROWS, p % SLOTS, hh, 0, :], start=True, stop=True).then_inc(st_psum, 1)
                        ahead = wrap(b, p + 4, more)
                        if p % 2 == 0 and ahead:
                            bb, g = ahead[0], ahead[1] // 2
                            if p == 0 and t == 1:
                                pe.wait_ge(x1_made, b * TB + 1)
                            if p == 4 and t == 1:
                                pe.wait_ge(xT_lo_made, bb * TB + TB)
                            if t == 5 or (t == 1 and p == 6):
                                pe.wait_ge(qk_lo_made, bb * 2 * NG + 2 * g + t // 4)
                            if t in (1, 2, 5, 6):
                                qk(bb, g, t // 4, (0, 1) if t % 4 == 1 else (2, 3))
                        if p == 3 and t % 2 and more:
                            if t == 1:
                                pe.wait_ge(qk_lo_made, b * 2 * NG + 2 * NG)
                            turn_row(b + 1, t // 2)
                        ahead = wrap(b, p + 1, more)
                        if t in (3, 5) and ahead:
                            pe.wait_ge(shift_rows_made, ahead[0] * H + 2 * ahead[1] + t // 5)
                            if p == 0 and t == 3:
                                pe.wait_ge(x1_made, b * TB + TB)
                            if p % 2 and p > 1 and t == 3:
                                pe.wait_ge(OT_lo_made, b * NG + p // 2)
                            turn_shifts(*ahead, t // 5)
                    m = n - LAG
                    if 0 <= m < NSTEP:
                        h, kb = divmod(m, TB)
                        pe.wait_ge(exp_made, b * NSTEP + m + 1)
                        if m >= 2:
                            pe.wait_ge(pv_made, b * NSTEP + m - 1)
                        else:
                            pe.wait_ge(x1_made, b * TB + m + 2)
                        if m == 0:
                            pe.wait_ge(v_made, b * TB + TB)
                        for qb in range(TB):
                            last = pe.matmul(bank[4 + m % 2][:, qb * VW:(qb + 1) * VW], probs[:, m % PRING, qb * P:(qb + 1) * P],
                                             v_ones[:, kb, h, :], start=True, stop=True)
                        last.then_inc(pv_psum, 1)
                    if more and NSTEP + LAG <= n < NSTEP + LAG + TB:
                        v = n - NSTEP - LAG
                        if v < 2:
                            pe.wait_ge(pv_made, (b + 1) * NSTEP - 1 + v)
                        else:
                            pe.wait_ge(v_made, (b + 1) * TB + v - 1)
                        values(b + 1, v)
                    if n in OT_STEPS:
                        g = OT_STEPS.index(n)
                        pe.wait_ge(combine_chain, o_done(b, (g + 1) * HG - 1))
                        if n < NSTEP:
                            pe.wait_ge(shift_rows_made, b * H + 2 * p + 2)
                        elif more:
                            pe.wait_ge(shift_rows_made, (b + 1) * H + 2)
                        else:
                            pe.wait_ge(OT_lo_made, b * NG + g)
                        for t4 in range(TB):
                            last = pe.transpose(bank[6][:, t4 * P:(t4 + 1) * P], o_group[:, t4, :], ident[:, :])
                        last.then_inc(OT_psum, 1)
                for j in range(TB):
                    if j == 0:
                        pe.wait_ge(wo_lo_made, KB)
                        pe.wait_ge(qk_lo_made, b * 2 * NG + 2 * NG + (4 if more else 0))
                    elif j < 3:
                        if more:
                            pe.wait_ge(v_made, (b + 1) * TB + j + 2)
                        else:
                            pe.wait_ge(pv_made, (b + 1) * NSTEP - 2 + j)
                    for g in range(NG):
                        if j == 0 and g == NG - 1:
                            pe.wait_ge(OT_lo_made, b * NG + NG)
                        last = matmul3(pe, bank[Y_BANK[j]][:, :], OT_hi[:, g, j * P:(j + 1) * P], OT_lo[:, g, j * P:(j + 1) * P],
                                       wo_hi[:, g, :], wo_lo[:, g, :], g == 0, g == NG - 1)
                    last.then_inc(y_psum, 1)

            pe.wait_ge(small_in, 64)
            for j in range(TB):
                turn_row(0, j)
            pe.wait_ge(w_lo_made, NCH)
            pe.wait_ge(xT_lo_made, TB)
            qk(0, 0, 0, (0, 1, 2, 3))
            pe.wait_ge(qk_lo_made, 1)
            qk(0, 0, 1, (0, 1, 2, 3))
            for t in range(TB):
                if t >= 2:
                    pe.wait_ge(v_made, t - 1)
                values(0, t)
            pe.wait_ge(qk_lo_made, 2)
            qk(0, 1, 0, (0, 1, 2, 3))
            pe.wait_ge(qk_lo_made, 3)
            qk(0, 1, 1, (0, 1, 2, 3))
            pe.wait_ge(v_made, TB)
            pe.wait_ge(ones_set, 1 + SLOTS)
            for p in range(2):
                for t in range(TP):
                    scores(0, p, t, first=p == 0 and t < 2)
                if p == 0:
                    turn_shifts(0, 0, 0)
                    pe.wait_ge(shift_rows_made, 1)
                    turn_shifts(0, 0, 1)
            over_batches(pe, batch)


def cross_attention(nc, xres, ident, bank, ctxT, wqT, bq, wkT, bk, Wg, Wu, Wd, GaT, Gb, UaT, Ub, DaT, Db, w_fix):
    with ExitStack() as ctx:
        def sb(name, shape, dt=F32):
            return ctx.enter_context(nc.sbuf_tensor("c_" + name, shape, dt))

        def sem(name):
            return ctx.enter_context(nc.semaphore("c_" + name))

        ctx_raw = sb("ctx_raw", [P, CB, B, S])
        w_raw = sb("w_raw", [P, 2, CB, P])
        w_hi, w_lo = sb("w_hi", [P, 2, CB, P], F32R), sb("w_lo", [P, 2, CB, P], F32R)
        bias = sb("bias", [P, 2])
        c_hi, c_lo = sb("c_hi", [P, CB, S], F32R), sb("c_lo", [P, CB, S], F32R)
        qk = sb("qk", [P, 2, S])
        qk_hi, qk_lo = sb("qk_hi", [P, 2, S], F32R), sb("qk_lo", [P, 2, S], F32R)
        att = sb("att", [P, 2, S])
        neg_max, row_sum, rec_sum = sb("neg_max", [P, TB]), sb("row_sum", [P, TB]), sb("rec_sum", [P, TB])
        aT_hi, aT_lo = sb("aT_hi", [P, KB, S], F32R), sb("aT_lo", [P, KB, S], F32R)
        xn = sb("xn", [P, 2, D])
        xT_hi, xT_lo = sb("xT_hi", [P, KB, S], F32R), sb("xT_lo", [P, KB, S], F32R)
        stats, mean = sb("stats", [P, TB, 6]), sb("mean", [P, TB])
        var, rstd, tmp = sb("var", [P, TB]), sb("rstd", [P, TB]), sb("tmp", [P, TB])
        down = sb("down", [R, NL, 3, D])
        up = sb("up", [R, NL, 3, FF])
        w_full = sb("w_full", [P, NL, 3, KB, FF])

        w_in, ctx_in, lora_in, w_fixed, fix_stored = sem("w_in"), sem("ctx_in"), sem("lora_in"), sem("w_fixed"), sem("fix_stored")
        w_hi_made, w_lo_made, c_hi_made, c_lo_made = sem("w_hi_made"), sem("w_lo_made"), sem("c_hi_made"), sem("c_lo_made")
        qk_psum, qk_made, qk_hi_made, qk_lo_made = sem("qk_psum"), sem("qk_made"), sem("qk_hi_made"), sem("qk_lo_made")
        e_psum, max_made, exp_made, rec_made, att_made = (
            sem("e_psum"), sem("max_made"), sem("exp_made"), sem("rec_made"), sem("att_made"))
        aT_psum, aT_hi_made, aT_lo_made, y_psum, x2_made = (
            sem("aT_psum"), sem("aT_hi_made"), sem("aT_lo_made"), sem("y_psum"), sem("x2_made"))
        ln_chain, xn_ready, xT_psum, xT_hi_made, xT_lo_made, fix_psum = (
            sem("ln_chain"), sem("xn_ready"), sem("xT_psum"), sem("xT_hi_made"), sem("xT_lo_made"), sem("fix_psum"))
        NFIX = NL * 3 * KB

        block = ctx.enter_context(nc.Block())

        @block.sync
        def _(sp):
            for i, w in enumerate((wqT, wkT)):
                sp.dma_start(w_raw[:, i, :, :], w.rearrange("(c p) d -> p c d", p=P)).then_inc(w_in, 16)
            for i, v in enumerate((bq, bk)):
                sp.dma_start(bias[:, i:i + 1], v.rearrange("(d a) -> d a", a=1)).then_inc(w_in, 16)
            for c in range(CB):
                sp.dma_start(ctx_raw[:, c, :, :], ctxT[:, c * P:(c + 1) * P, :].rearrange("b p s -> p b s")).then_inc(ctx_in, 16)
            for m, (a, v, w) in enumerate(((GaT, Gb, Wg), (UaT, Ub, Wu), (DaT, Db, Wd))):
                sp.dma_start(down[:, :, m, :], a.rearrange("e r d -> r e d")).then_inc(lora_in, 16)
                sp.dma_start(up[:, :, m, :], v.rearrange("e r d -> r e d")).then_inc(lora_in, 16)
                for e in range(NL):
                    sp.dma_start(w_full[:, e, m, :, :], w[e, :, :].rearrange("(k p) f -> p k f", p=P)).then_inc(lora_in, 16)
            for i in range(NL * 3):
                e, m = divmod(i, 3)
                sp.wait_ge(w_fixed, (i + 1) * KB)
                sp.dma_start(w_fix[e, m, :, :].rearrange("(k p) f -> p k f", p=P), w_full[:, e, m, :, :]).then_inc(fix_stored, 16)
            sp.wait_ge(fix_stored, 16 * NL * 3)

        @block.gpsimd
        def _(pool):
            pool.wait_ge(w_hi_made, 1)
            pool.tensor_tensor(w_lo[:, :, :, :], w_raw[:, :, :, :], w_hi[:, :, :, :].bitcast(F32), ALU.subtract)\
                .then_inc(w_lo_made, 1)

        def att_high(act, b, j):
            act.wait_ge(aT_psum, b * TB + j + 1)
            act.activation(aT_hi[:, :, j * P:(j + 1) * P], bank[4 + j % 2][:, :].rearrange("p (k t) -> p k t", k=KB), ACT.Copy)\
                .then_inc(aT_hi_made, 1)

        @block.scalar
        def _(act):
            act.wait_ge(w_in, 64)
            act.activation(w_hi[:, :, :, :], w_raw[:, :, :, :], ACT.Copy).then_inc(w_hi_made, 1)
            act.wait_ge(ctx_in, 16 * CB)
            with act.Fori(0, B) as b:
                act.wait_ge(x2_made, b * TB + CREDIT)
                act.activation(c_hi[:, :, :], ctx_raw[:, :, bass.ds(b, 1), :].rearrange("p c o s -> p c (o s)"), ACT.Copy)\
                    .then_inc(c_hi_made, 1)
                for i in range(2):
                    act.wait_ge(qk_psum, b * 2 + i + 1)
                    act.activation(qk[:, i, :], bank[4 + i][:, :], ACT.Identity, bias=bias[:, i:i + 1]).then_inc(qk_made, 1)
                    act.wait_ge(qk_made, b * 2 + i + 1)
                    act.activation(qk_hi[:, i, :], qk[:, i, :], ACT.Copy).then_inc(qk_hi_made, 1)
                for j in range(TB):
                    act.wait_ge(max_made, b * TB + j + 1)
                    if j >= 2:
                        act.wait_ge(aT_psum, b * TB + j - 1)
                    act.activation(att[:, j % 2, :], bank[6 + j % 2][:, :], ACT.Exp, bias=neg_max[:, j:j + 1],
                                   accum_out=row_sum[:, j:j + 1]).then_inc(exp_made, 1)
                    if j >= 1:
                        att_high(act, b, j - 1)
                att_high(act, b, TB - 1)
                for j in range(TB):
                    act.wait_ge(xT_psum, b * TB + j + 1)
                    act.activation(xT_hi[:, :, j * P:(j + 1) * P], bank[j][:, :].rearrange("p (k t) -> p k t", k=KB), ACT.Copy)\
                        .then_inc(xT_hi_made, 1)

        def att_scale(dve, b, j):
            dve.wait_ge(exp_made, b * TB + j + 1)
            dve.reciprocal(rec_sum[:, j:j + 1], row_sum[:, j:j + 1]).then_inc(rec_made, 1)
            dve.wait_ge(rec_made, b * TB + j + 1)
            dve.tensor_scalar(att[:, j % 2, :], att[:, j % 2, :], rec_sum[:, j:j + 1], None, ALU.mult).then_inc(att_made, 1)

        def xT_low(dve, b, j):
            dve.wait_ge(xT_hi_made, b * TB + j + 1)
            dve.tensor_tensor(xT_lo[:, :, j * P:(j + 1) * P], bank[j][:, :].rearrange("p (k t) -> p k t", k=KB),
                              xT_hi[:, :, j * P:(j + 1) * P].bitcast(F32), ALU.subtract).then_inc(xT_lo_made, 1)

        @block.vector
        def _(dve):
            dve.sem_inc(x2_made, CREDIT)
            with dve.Fori(0, B) as b:
                dve.wait_ge(c_hi_made, b + 1)
                dve.tensor_tensor(c_lo[:, :, :], ctx_raw[:, :, bass.ds(b, 1), :].rearrange("p c o s -> p c (o s)"),
                                  c_hi[:, :, :].bitcast(F32), ALU.subtract).then_inc(c_lo_made, 1)
                for i in range(2):
                    dve.wait_ge(qk_hi_made, b * 2 + i + 1)
                    dve.tensor_tensor(qk_lo[:, i, :], qk[:, i, :], qk_hi[:, i, :].bitcast(F32), ALU.subtract).then_inc(qk_lo_made, 1)

                def att_low(j):
                    dve.wait_ge(aT_hi_made, b * TB + j + 1)
                    dve.tensor_tensor(aT_lo[:, :, j * P:(j + 1) * P], bank[4 + j % 2][:, :].rearrange("p (k t) -> p k t", k=KB),
                                      aT_hi[:, :, j * P:(j + 1) * P].bitcast(F32), ALU.subtract).then_inc(aT_lo_made, 1)

                for j in range(TB):
                    dve.wait_ge(e_psum, b * TB + j + 1)
                    dve.tensor_reduce(neg_max[:, j:j + 1], bank[6 + j % 2][:, :], AX.X, ALU.max, negate=True).then_inc(max_made, 1)
                    if j >= 1:
                        att_scale(dve, b, j - 1)
                    if j >= 2:
                        att_low(j - 2)
                att_scale(dve, b, TB - 1)
                att_low(TB - 2)
                att_low(TB - 1)

                def row(j):
                    return xres[:, bass.ds(b * TB + j, 1), :].rearrange("p o d -> p (o d)")

                chain = Chain(dve, ln_chain, b * (TB + 9 + 3 * NEWTON))
                for j in range(TB):
                    chain.then(dve.bn_stats(stats[:, j, :], row(j)))
                moments(dve, stats, mean[:, :], var[:, :], tmp[:, :], chain)
                rsqrt_steps(dve, var[:, :], rstd[:, :], tmp[:, :], chain)
                for j in range(TB):
                    if j >= 2:
                        dve.wait_ge(xT_psum, b * TB + j - 1)
                    dve.tensor_scalar(xn[:, j % 2, :], row(j), mean[:, j:j + 1], rstd[:, j:j + 1], ALU.subtract, ALU.mult)\
                        .then_inc(xn_ready, 1)
                    if j >= 1:
                        xT_low(dve, b, j - 1)
                xT_low(dve, b, TB - 1)
                for j in range(TB):
                    dve.wait_ge(y_psum, b * TB + j + 1)
                    dve.tensor_tensor(row(j), bank[j][:, :], row(j), ALU.add).then_inc(x2_made, 1)
            dve.wait_ge(lora_in, 16 * 3 * (2 + NL))
            for i in range(NFIX):
                em, k = divmod(i, KB)
                e, m = divmod(em, 3)
                dve.wait_ge(fix_psum, i + 1)
                dve.tensor_tensor(w_full[:, e, m, k, :], bank[i % 4][:, :], w_full[:, e, m, k, :], ALU.add).then_inc(w_fixed, 1)

        @block.tensor
        def _(pe):
            pe.wait_ge(w_lo_made, 1)
            with pe.Fori(0, B) as b:
                pe.wait_ge(x2_made, b * TB + CREDIT)
                pe.wait_ge(c_lo_made, b + 1)
                for i in range(2):
                    for c in range(CB):
                        last = matmul3(pe, bank[4 + i][:, :], w_hi[:, i, c, :], w_lo[:, i, c, :], c_hi[:, c, :], c_lo[:, c, :],
                                       c == 0, c == CB - 1)
                    last.then_inc(qk_psum, 1)
                pe.wait_ge(qk_lo_made, b * 2 + 2)

                def turn(j):
                    pe.wait_ge(att_made, b * TB + j + 1)
                    if j >= 2:
                        pe.wait_ge(aT_lo_made, b * TB + j - 1)
                    for k in range(KB):
                        last = pe.transpose(bank[4 + j % 2][:, k * P:(k + 1) * P], att[:, j % 2, k * P:(k + 1) * P], ident[:, :])
                    last.then_inc(aT_psum, 1)

                for j in range(TB):
                    if j >= 2:
                        pe.wait_ge(exp_made, b * TB + j - 1)
                    matmul3(pe, bank[6 + j % 2][:, :], qk_hi[:, 0, j * P:(j + 1) * P], qk_lo[:, 0, j * P:(j + 1) * P],
                            qk_hi[:, 1, :], qk_lo[:, 1, :], True, True).then_inc(e_psum, 1)
                    if j >= 1:
                        turn(j - 1)
                turn(TB - 1)
                for j in range(TB):
                    pe.wait_ge(xn_ready, b * TB + j + 1)
                    for k in range(KB):
                        last = pe.transpose(bank[j][:, k * P:(k + 1) * P], xn[:, j % 2, k * P:(k + 1) * P], ident[:, :])
                    last.then_inc(xT_psum, 1)
                pe.wait_ge(aT_lo_made, b * TB + TB)
                pe.wait_ge(xT_lo_made, b * TB + TB)
                for j in range(TB):
                    for k in range(KB):
                        last = matmul3(pe, bank[j][:, :], xT_hi[:, k, j * P:(j + 1) * P], xT_lo[:, k, j * P:(j + 1) * P],
                                       aT_hi[:, k, :], aT_lo[:, k, :], k == 0, k == KB - 1)
                    last.then_inc(y_psum, 1)
            pe.wait_ge(x2_made, B * TB + CREDIT)
            pe.wait_ge(lora_in, 16 * 3 * (2 + NL))
            for i in range(NFIX):
                em, k = divmod(i, KB)
                e, m = divmod(em, 3)
                if i >= 4:
                    pe.wait_ge(w_fixed, i - 3)
                pe.matmul(bank[i % 4][:, :], down[:, e, m, k * P:(k + 1) * P], up[:, e, m, :], start=True, stop=True)\
                    .then_inc(fix_psum, 1)


def experts(nc, xres, ident, bank, Wg, Wu, Wd, w_fix, Wr, temperature):
    with ExitStack() as ctx:
        def sb(name, shape, dt=F32):
            return ctx.enter_context(nc.sbuf_tensor("e_" + name, shape, dt))

        def sem(name):
            return ctx.enter_context(nc.semaphore("e_" + name))

        xT_hi, xT_lo = sb("xT_hi", [P, KB, B * S], F32R), sb("xT_lo", [P, KB, B * S], F32R)
        raw = [sb("raw_gate", [P, KB, FH]), sb("raw_up", [P, KB, FH]), sb("raw_down", [P, FB, D])]
        w_hi = [[sb(f"{n}_hi{s}", [P, KB, FH] if n != "down" else [P, FB, D], F32R) for s in range(2)] for n in ("gate", "up", "down")]
        w_lo = [[sb(f"{n}_lo{s}", [P, KB, FH] if n != "down" else [P, FB, D], F32R) for s in range(2)] for n in ("gate", "up", "down")]
        silu = sb("silu", [P, FB, S])
        mid = sb("mid", [P, FB, S])
        mid_hi, mid_lo = sb("mid_hi", [P, 2, FB, S], F32R), sb("mid_lo", [P, 2, FB, S], F32R)
        xn = mid
        zero = sb("zero", [P, 1, 1])
        wr_raw = sb("wr_raw", [P, KB, P])
        wr_hi, wr_lo = sb("wr_hi", [P, KB, P], F32R), sb("wr_lo", [P, KB, P], F32R)
        logitsT = sb("logitsT", [P, S])
        stats, mean = sb("stats", [P, TB, 6]), sb("mean", [P, TB])
        var, rstd, tmp = sb("var", [P, TB]), sb("rstd", [P, TB]), sb("tmp", [P, TB])
        temp = sb("temp", [P, 2])
        E3 = [P, NT, NE]
        logits, inh, dist, zone, wts, fb, fbw, index, cand, mask = (
            sb(n, E3) for n in ("logits", "inh", "dist", "zone", "wts", "fb", "fbw", "index", "cand", "mask"))
        best, total = sb("best", [P, NT, 1]), sb("total", [P, NT, 1])
        none, some = sb("none", [P, NT, 1]), sb("some", [P, NT, 1])

        small_in, wr_zero, wr_hi_made, wr_lo_made = sem("small_in"), sem("wr_zero"), sem("wr_hi_made"), sem("wr_lo_made")
        index_set, temp_made, zero_set = sem("index_set"), sem("temp_made"), sem("zero_set")
        ln_chain, xn_ready, xT_psum, xT_hi_made, xT_lo_made = (
            sem("ln_chain"), sem("xn_ready"), sem("xT_psum"), sem("xT_hi_made"), sem("xT_lo_made"))
        lT_psum, lT_made, l_psum, l_made = sem("lT_psum"), sem("lT_made"), sem("l_psum"), sem("l_made")
        route_chain, inh_made, dist_made, exps_made = sem("route_chain"), sem("inh_made"), sem("dist_made"), sem("exps_made")
        raw_in = [sem(f"raw_in{m}") for m in range(3)]
        hi_made = [sem(f"hi_made{m}") for m in range(3)]
        lo_made = [sem(f"lo_made{m}") for m in range(3)]
        gate_psum, up_psum, silu_made, mid_made, mid_hi_made, mid_lo_made = (
            [sem(f"{n}{f}") for f in range(FB)] for n in ("gate_psum", "up_psum", "silu_made", "mid_made", "mid_hi_made", "mid_lo_made"))
        d_psum = [sem(f"d_psum{i}") for i in range(2)]
        acc_made = [sem(f"acc_made{j}") for j in range(TB)]

        UNITS = 2 * B

        block = ctx.enter_context(nc.Block())

        @block.sync
        def _(sp):
            sp.dma_start(temp[:, 0:1], temperature.rearrange("(a d) -> a d", a=1).broadcast_to([P, 1])).then_inc(small_in, 16)
            sp.wait_ge(wr_zero, 1)
            sp.dma_start(wr_raw[:, :, 0:NE], Wr.rearrange("(k p) e -> p k e", p=P)).then_inc(small_in, 16)

            def load(e, src):
                for h in range(2):
                    for m in range(3):
                        if e * 2 + h if isinstance(e, int) else True:
                            sp.wait_ge(lo_made[m], e * 2 + h)
                        w = src(m)
                        if m < 2:
                            w = w[:, h * FH:(h + 1) * FH].rearrange("(k p) f -> p k f", p=P)
                        else:
                            w = w[h * FH:(h + 1) * FH, :].rearrange("(k p) f -> p k f", p=P)
                        sp.dma_start(raw[m][:, :, :], w).then_inc(raw_in[m], 16)

            for e in range(NL):
                load(e, lambda m: w_fix[e, m, :, :])
            with sp.Fori(NL, NE) as e:
                sp.snap(e * (D * FF))
                load(e, lambda m: (Wg, Wu, Wd)[m][bass.ds(e, 1), :, :].rearrange("o a f -> (o a) f"))

        @block.gpsimd
        def _(pool):
            pool.memset(wr_raw[:, :, :], 0.0).then_inc(wr_zero, 1)
            for e in range(NE):
                pool.memset(index[:, :, e:e + 1], float(e)).then_inc(index_set, 1)

            def split(e, first):
                for h in range(2):
                    for m in range(3):
                        pool.wait_ge(raw_in[m], (e * 2 + h + 1) * 16)
                        if not first and m == 0:
                            pool.wait_ge(d_psum[1], (e - 1) * 16 + 8 * (h + 1) + CREDIT)
                        pool.tensor_tensor(w_hi[m][h][:, :, :], raw[m][:, :, :], zero[:, :, :].broadcast_to(raw[m].shape), ALU.add)\
                            .then_inc(hi_made[m], 1)
                        pool.wait_ge(hi_made[m], e * 2 + h + 1)
                        pool.tensor_tensor(w_lo[m][h][:, :, :], raw[m][:, :, :], w_hi[m][h][:, :, :].bitcast(F32), ALU.subtract)\
                            .then_inc(lo_made[m], 1)

            pool.memset(zero[:, :, :], 0.0).then_inc(zero_set, 1)
            pool.wait_ge(zero_set, 1)
            split(0, True)
            with pool.Fori(1, NE) as e:
                split(e, False)

        @block.scalar
        def _(act):
            for f in range(FB):
                act.sem_inc(silu_made[f], CREDIT)
                act.sem_inc(mid_hi_made[f], CREDIT)
            act.wait_ge(small_in, 32)
            act.activation(wr_hi[:, :, :], wr_raw[:, :, :], ACT.Copy).then_inc(wr_hi_made, 1)
            with act.Fori(0, B) as b:
                for j in range(TB):
                    act.wait_ge(xT_psum, b * TB + j + 1)
                    act.activation(xT_hi[:, :, bass.ds(b * S + j * P, P)], bank[j][:, :].rearrange("p (k t) -> p k t", k=KB), ACT.Copy)\
                        .then_inc(xT_hi_made, 1)
                act.wait_ge(lT_psum, b + 1)
                act.activation(logitsT[:, :], bank[4][:, :], ACT.Copy).then_inc(lT_made, 1)
            act.wait_ge(l_made, B + CREDIT)
            act.wait_ge(temp_made, 1)
            act.activation(inh[:, :, :], logits[:, :, :], ACT.Sigmoid, scale=temp[:, 1:2]).then_inc(inh_made, 1)
            act.wait_ge(dist_made, 1)
            act.activation(wts[:, :, :], dist[:, :, :], ACT.Exp, scale=-1.0 / 0.1).then_inc(exps_made, 1)
            act.activation(fb[:, :, :], dist[:, :, :], ACT.Exp, scale=-1.0 / 0.3).then_inc(exps_made, 1)
            with act.Fori(0, NE) as e:
                for u in range(UNITS):
                    n = e * UNITS + u
                    for f in range(FB):
                        act.wait_ge(gate_psum[f], n + 1)
                        act.wait_ge(mid_made[f], n + CREDIT)
                        act.activation(silu[:, f, :], bank[f][:, :], ACT.Silu).then_inc(silu_made[f], 1)
                        act.wait_ge(mid_made[f], n + 1 + CREDIT)
                        act.wait_ge(d_psum[u % 2], e * 16 + u // 2 * 4 + CREDIT)
                        act.activation(mid_hi[:, u % 2, f, :], mid[:, f, :], ACT.Copy).then_inc(mid_hi_made[f], 1)

        @block.vector
        def _(dve):
            for s in (*mid_made, *acc_made, xT_lo_made, l_made):
                dve.sem_inc(s, CREDIT)
            dve.wait_ge(small_in, 32)
            dve.reciprocal(temp[:, 1:2], temp[:, 0:1]).then_inc(temp_made, 1)
            dve.wait_ge(wr_hi_made, 1)
            dve.tensor_tensor(wr_lo[:, :, :], wr_raw[:, :, :], wr_hi[:, :, :].bitcast(F32), ALU.subtract).then_inc(wr_lo_made, 1)
            with dve.Fori(0, B) as b:
                def row(j):
                    return xres[:, bass.ds(b * TB + j, 1), :].rearrange("p o d -> p (o d)")

                def low(j):
                    dve.wait_ge(xT_hi_made, b * TB + j + 1)
                    cols = bass.ds(b * S + j * P, P)
                    dve.tensor_tensor(xT_lo[:, :, cols], bank[j][:, :].rearrange("p (k t) -> p k t", k=KB),
                                      xT_hi[:, :, cols].bitcast(F32), ALU.subtract).then_inc(xT_lo_made, 1)

                chain = Chain(dve, ln_chain, b * (TB + 9 + 3 * NEWTON))
                for j in range(TB):
                    chain.then(dve.bn_stats(stats[:, j, :], row(j)))
                moments(dve, stats, mean[:, :], var[:, :], tmp[:, :], chain)
                rsqrt_steps(dve, var[:, :], rstd[:, :], tmp[:, :], chain)
                for j in range(TB):
                    if j >= 2:
                        dve.wait_ge(xT_psum, b * TB + j - 1)
                    dve.tensor_scalar(xn[:, j % 2, :], row(j), mean[:, j:j + 1], rstd[:, j:j + 1], ALU.subtract, ALU.mult)\
                        .then_inc(xn_ready, 1)
                    if j >= 1:
                        low(j - 1)
                low(TB - 1)
                dve.wait_ge(l_psum, b + 1)
                dve.tensor_copy(logits[:, bass.ds(b * TB, TB), :], bank[5][:, :].rearrange("p (t e) -> p t e", t=TB)[:, :, 0:NE])\
                    .then_inc(l_made, 1)

            chain = Chain(dve, route_chain)

            def wide(v):
                return v[:, :, :].broadcast_to(E3)

            def all_(v):
                return v[:, :, :]

            def pick(values):
                chain.then(dve.tensor_reduce(all_(best), all_(values), AX.X, ALU.max))
                chain.then(dve.tensor_tensor(all_(cand), all_(values), wide(best), ALU.is_equal))
                chain.then(dve.scalar_tensor_tensor(out=all_(cand), in0=all_(cand), scalar=-float(NE), in1=all_(index),
                                                    op0=ALU.mult, op1=ALU.add))
                chain.then(dve.tensor_reduce(all_(best), all_(cand), AX.X, ALU.min))
                chain.then(dve.tensor_tensor(all_(cand), all_(cand), wide(best), ALU.is_equal))

            def normalise(values):
                chain.then(dve.tensor_reduce(all_(total), all_(values), AX.X, ALU.add))
                chain.then(dve.tensor_scalar(all_(total), all_(total), 1e-8, None, ALU.max))
                chain.then(dve.reciprocal(all_(total), all_(total)))
                chain.then(dve.tensor_tensor(all_(values), all_(values), wide(total), ALU.mult))

            dve.wait_ge(inh_made, 1)
            chain.then(dve.tensor_scalar(all_(dist), all_(inh), GOLDEN_CENTER, None, ALU.subtract))
            dve.scalar_tensor_tensor(out=all_(dist), in0=all_(dist), scalar=-1.0, in1=all_(dist), op0=ALU.mult, op1=ALU.max)\
                .then_inc(dist_made, 1)
            chain.then(dve.tensor_scalar(all_(zone), all_(inh), GOLDEN_LOWER, None, ALU.is_ge))
            chain.then(dve.scalar_tensor_tensor(out=all_(zone), in0=all_(inh), scalar=GOLDEN_UPPER, in1=all_(zone),
                                                op0=ALU.is_le, op1=ALU.mult))
            dve.wait_ge(exps_made, 2)
            chain.then(dve.tensor_tensor(all_(wts), all_(wts), all_(zone), ALU.mult))
            chain.then(dve.tensor_reduce(all_(total), all_(wts), AX.X, ALU.add))
            chain.then(dve.tensor_scalar(all_(none), all_(total), 1e-8, None, ALU.is_lt))
            chain.then(dve.tensor_scalar(all_(some), all_(none), -1.0, 1.0, ALU.mult, ALU.add))
            dve.wait_ge(index_set, NE)
            pick(fb)
            chain.then(dve.tensor_copy(all_(mask), all_(cand)))
            chain.then(dve.scalar_tensor_tensor(out=all_(fbw), in0=all_(mask), scalar=-2.0, in1=all_(fb), op0=ALU.mult, op1=ALU.add))
            pick(fbw)
            chain.then(dve.tensor_tensor(all_(mask), all_(mask), all_(cand), ALU.add))
            chain.then(dve.tensor_tensor(all_(fbw), all_(fb), all_(mask), ALU.mult))
            normalise(fbw)
            chain.then(dve.tensor_tensor(all_(fbw), all_(fbw), wide(none), ALU.mult))
            chain.then(dve.tensor_tensor(all_(wts), all_(wts), wide(some), ALU.mult))
            chain.then(dve.tensor_tensor(all_(wts), all_(wts), all_(fbw), ALU.add))
            normalise(wts)

            with dve.Fori(0, NE) as e:
                for u in range(UNITS):
                    n = e * UNITS + u
                    b = u % B
                    for f in range(FB):
                        dve.wait_ge(silu_made[f], n + 1 + CREDIT)
                        dve.wait_ge(up_psum[f], n + 1)
                        dve.wait_ge(mid_hi_made[f], n + CREDIT)
                        dve.tensor_tensor(mid[:, f, :], bank[2 + f][:, :], silu[:, f, :], ALU.mult).then_inc(mid_made[f], 1)
                        dve.wait_ge(mid_hi_made[f], n + 1 + CREDIT)
                        dve.tensor_tensor(mid_lo[:, u % 2, f, :], mid[:, f, :], mid_hi[:, u % 2, f, :].bitcast(F32), ALU.subtract)\
                            .then_inc(mid_lo_made[f], 1)
                    for j in range(TB):
                        dve.wait_ge(d_psum[u % 2], e * 16 + u // 2 * 4 + j + 1 + CREDIT)
                        blk = b * TB + j
                        dve.scalar_tensor_tensor(out=xres[:, blk, :], in0=bank[4 + j][:, :],
                                                 scalar=wts[:, blk:blk + 1, bass.ds(e, 1)].rearrange("p a o -> p (a o)"),
                                                 in1=xres[:, blk, :], op0=ALU.mult, op1=ALU.add).then_inc(acc_made[j], 1)

        @block.tensor
        def _(pe):
            for s in d_psum:
                pe.sem_inc(s, CREDIT)
            pe.wait_ge(wr_lo_made, 1)
            with pe.Fori(0, B) as b:
                for j in range(TB):
                    pe.wait_ge(xn_ready, b * TB + j + 1)
                    pe.wait_ge(xT_lo_made, b * TB + CREDIT)
                    for k in range(KB):
                        last = pe.transpose(bank[j][:, k * P:(k + 1) * P], xn[:, j % 2, k * P:(k + 1) * P], ident[:, :])
                    last.then_inc(xT_psum, 1)
                pe.wait_ge(xT_lo_made, b * TB + TB + CREDIT)
                for k in range(KB):
                    cols = bass.ds(b * S, S)
                    last = matmul3(pe, bank[4][:, :], wr_hi[:, k, :], wr_lo[:, k, :], xT_hi[:, k, cols], xT_lo[:, k, cols],
                                   k == 0, k == KB - 1)
                last.then_inc(lT_psum, 1)
                pe.wait_ge(lT_made, b + 1)
                pe.wait_ge(l_made, b + CREDIT)
                for j in range(TB):
                    last = pe.transpose(bank[5][:, j * P:(j + 1) * P], logitsT[:, j * P:(j + 1) * P], ident[:, :])
                last.then_inc(l_psum, 1)
            pe.wait_ge(l_made, B + CREDIT)
            with pe.Fori(0, NE) as e:
                for u in range(UNITS):
                    n = e * UNITS + u
                    h, b = divmod(u, B)
                    if b == 0:
                        for m in range(3):
                            pe.wait_ge(lo_made[m], e * 2 + h + 1)
                    for f in range(FB):
                        for m, psum, free in ((0, gate_psum, silu_made), (1, up_psum, mid_made)):
                            pe.wait_ge(free[f], n + CREDIT)
                            for k in range(KB):
                                last = matmul3(pe, bank[2 * m + f][:, :], w_hi[m][h][:, k, f * P:(f + 1) * P],
                                               w_lo[m][h][:, k, f * P:(f + 1) * P], xT_hi[:, k, b * S:(b + 1) * S],
                                               xT_lo[:, k, b * S:(b + 1) * S], k == 0, k == KB - 1)
                            last.then_inc(psum[f], 1)
                    for f in range(FB):
                        pe.wait_ge(mid_lo_made[f], n + 1)
                        for j in range(TB):
                            if f == 0:
                                pe.wait_ge(acc_made[j], n + CREDIT)
                            last = matmul3(pe, bank[4 + j][:, :], mid_hi[:, u % 2, f, j * P:(j + 1) * P],
                                           mid_lo[:, u % 2, f, j * P:(j + 1) * P], w_hi[2][h][:, f, :], w_lo[2][h][:, f, :],
                                           f == 0, f == FB - 1)
                            if f == FB - 1:
                                last.then_inc(d_psum[u % 2], 1)



def kernel(**inputs):
    from concourse import bacc, mybir as mb
    from concourse.bass_utils import run_bass_kernel_spmd as run

    def turned(a, axes):
        return np.ascontiguousarray(np.transpose(np.asarray(a), axes))

    i = {k.removeprefix("L0_"): v for k, v in inputs.items()}
    laid = {
        "x": np.asarray(i["x"]),
        "ctxT": turned(i["ctx_1024"], (0, 2, 1)),
        "w_qkvT": turned(i["attn_w_qkv"], (1, 0)),
        "w_outT": turned(i["attn_w_out"], (1, 0)),
        "b_out": np.asarray(i["attn_b_out"]),
        "wqT": turned(i["xattn_Wq"], (1, 0)), "bq": np.asarray(i["xattn_bq"]),
        "wkT": turned(i["xattn_Wk"], (1, 0)), "bk": np.asarray(i["xattn_bk"]),
        "Wg": np.asarray(i["ffn_Wg"]), "Wu": np.asarray(i["ffn_Wu"]), "Wd": np.asarray(i["ffn_Wd"]),
        "GaT": turned(i["ffn_Ga"], (0, 2, 1)), "Gb": np.asarray(i["ffn_Gb"]),
        "UaT": turned(i["ffn_Ua"], (0, 2, 1)), "Ub": np.asarray(i["ffn_Ub"]),
        "DaT": turned(i["ffn_Da"], (0, 2, 1)), "Db": np.asarray(i["ffn_Db"]),
        "Wr": np.asarray(i["ffn_Wr"]), "temperature": np.asarray(i["ffn_temperature"]),
        "ident_in": np.eye(P, dtype=np.float32),
    }
    nc = bacc.Bacc("TRN2", target_bir_lowering=False, num_devices=1)
    arrays, aps = {}, {}
    for name, a in laid.items():
        a = np.ascontiguousarray(a)
        arrays[name] = a
        aps[name] = nc.dram_tensor(name, a.shape, mb.dt.from_np(a.dtype), kind="ExternalInput").ap()
    out = nc.dram_tensor("out", (B, S, D), F32, kind="ExternalOutput").ap()
    build(nc, **aps, out=out)
    r = run(nc, [arrays], core_ids=[0])
    return r.results[0]["out"]
```

```python
import math
from contextlib import ExitStack

import numpy as np

import concourse.bass as bass
from concourse import mybir

F32 = mybir.dt.float32
F32R = mybir.dt.float32r
I32 = mybir.dt.int32
U32 = mybir.dt.uint32
ALU = mybir.AluOpType
ACT = mybir.ActivationFunctionType
AX = mybir.AxisListType

P = 128
B, S, D = 4, 512, 512
KB = D // P
TB = S // P
NT = B * TB
H, HD = 16, 32
HG = P // HD
NG = H // HG
NPAIR = H // 2
C = 256
CB = C // P
NE, FF, NL, R = 8, 512, 2, 64
FH = FF // 2
FB = FH // P
CREDIT = 1
LN_EPS = 1e-5
ATT_SCALE = 1.0 / math.sqrt(HD)
GOLDEN_CENTER = 1.0 / math.e
GOLDEN_LOWER = 0.5 - math.log(4.0 / 3.0)
GOLDEN_UPPER = 0.5

SLOTS = 4
STACK = 3 * HD
SHIFT = 2 * TB
PRING = 4
LAG = 3
VW = HD + 1
NSTEP = H * TB
NEWTON = 3


def matmul3(pe, out, w_hi, w_lo, x_hi, x_lo, first, last):
    pe.matmul(out, w_hi, x_hi, start=first, stop=False)
    pe.matmul(out, w_hi, x_lo, start=False, stop=False)
    return pe.matmul(out, w_lo, x_hi, start=False, stop=last)


def moments(dve, stats, mean, var, tmp, chain):
    even, odd, sq_even, sq_odd = (stats[:, :, i] for i in (1, 4, 2, 5))
    chain.then(dve.tensor_tensor(mean, even, odd, ALU.add))
    chain.then(dve.tensor_scalar(mean, mean, 0.5, None, ALU.mult))
    chain.then(dve.tensor_tensor(tmp, even, odd, ALU.subtract))
    chain.then(dve.scalar_tensor_tensor(out=tmp, in0=tmp, scalar=0.25, in1=tmp, op0=ALU.mult, op1=ALU.mult))
    chain.then(dve.tensor_tensor(var, sq_even, sq_odd, ALU.add))
    chain.then(dve.scalar_tensor_tensor(out=var, in0=var, scalar=1.0 / D, in1=tmp, op0=ALU.mult, op1=ALU.add))


def rsqrt_guess(dve, var, y, tmp, chain):
    chain.then(dve.tensor_scalar(var, var, LN_EPS, None, ALU.add))
    chain.then(dve.tensor_scalar(tmp.bitcast(U32), var.bitcast(U32), 1, None, ALU.logical_shift_right))
    chain.then(dve.tensor_scalar(y.bitcast(I32), tmp.bitcast(I32), -1.0, float(0x5F3759DF), ALU.mult, ALU.add))


def newton_step(dve, var, y, tmp, chain):
    chain.then(dve.scalar_tensor_tensor(out=tmp, in0=y, scalar=-0.5, in1=y, op0=ALU.mult, op1=ALU.mult))
    chain.then(dve.tensor_tensor(tmp, tmp, var, ALU.mult))
    chain.then(dve.scalar_tensor_tensor(out=y, in0=tmp, scalar=1.5, in1=y, op0=ALU.add, op1=ALU.mult))


def rsqrt_steps(dve, var, y, tmp, chain):
    rsqrt_guess(dve, var, y, tmp, chain)
    for _ in range(NEWTON):
        newton_step(dve, var, y, tmp, chain)


class Chain:

    def __init__(self, eng, sem, base=0):
        self.eng, self.sem, self.base, self.n = eng, sem, base, 0

    def then(self, instruction):
        self.n += 1
        instruction.then_inc(self.sem, 1)
        self.eng.wait_ge(self.sem, self.base + self.n)


def ln_scale(chain, stats, norm, lo, hi):
    mean, var, rstd, tmp = (t[:, lo:hi] for t in norm)
    moments(chain.eng, stats[:, lo:hi, :], mean, var, tmp, chain)
    rsqrt_steps(chain.eng, var, rstd, tmp, chain)


def build(nc, x, ctxT, w_qkvT, w_outT, b_out, wqT, bq, wkT, bk, Wg, Wu, Wd, GaT, Gb, UaT, Ub, DaT, Db, Wr,
          temperature, ident_in, out):
    xt = x.rearrange("b (t p) d -> p (b t) d", p=P)
    outt = out.rearrange("b (t p) d -> p (b t) d", p=P)
    w_fix = nc.dram_tensor("w_fix", [NL, 3, D, FF], F32, kind="Internal").ap()
    with ExitStack() as whole:
        xres = whole.enter_context(nc.sbuf_tensor("xres", [P, NT, D], F32))
        ident = whole.enter_context(nc.sbuf_tensor("ident", [P, P], F32))
        wr_raw = whole.enter_context(nc.sbuf_tensor("wr_raw", [P, KB, P], F32))
        norm = [whole.enter_context(nc.sbuf_tensor(n, [P, NT], F32)) for n in ("mean", "var", "rstd", "norm_tmp")]
        temp = whole.enter_context(nc.sbuf_tensor("temp", [P, 2], F32))
        stats = whole.enter_context(nc.sbuf_tensor("stats", [P, NT, 6], F32))
        bank = [whole.enter_context(nc.psum_tensor(f"bank{i}", [P, 512], F32)) for i in range(8)]
        self_attention(nc, xres, ident, bank, xt, w_qkvT, w_outT, b_out, ident_in)
        cross_attention(nc, xres, stats, norm, wr_raw, temp, ident, bank, Wr, temperature, ctxT, wqT, bq, wkT, bk,
                        Wg, Wu, Wd, GaT, Gb, UaT, Ub, DaT, Db, w_fix)
        experts(nc, xres, stats, norm, wr_raw, temp, ident, bank, outt, Wg, Wu, Wd, w_fix)


def self_attention(nc, xres, ident, bank, xt, w_qkvT, w_outT, b_out, ident_in):
    with ExitStack() as ctx:
        def sb(name, shape, dt=F32):
            return ctx.enter_context(nc.sbuf_tensor("a_" + name, shape, dt))

        def sem(name):
            return ctx.enter_context(nc.semaphore("a_" + name))

        w_hi, w_lo = sb("w_hi", [P, KB, 3 * D], F32R), sb("w_lo", [P, KB, 3 * D], F32R)
        wo_hi, wo_lo = sb("wo_hi", [P, KB, D], F32R), sb("wo_lo", [P, KB, D], F32R)
        xT_hi, xT_lo = sb("xT_hi", [P, KB, S], F32R), sb("xT_lo", [P, KB, S], F32R)
        stack = sb("stack", [P, SLOTS, 2, 2, S], F32R)
        qk_parts = sb("qk_parts", [P, 4, S], F32R)
        v_ones = sb("v_ones", [P, TB, H, VW])
        probs = sb("probs", [P, PRING, S])
        xn = sb("xn", [P, 2, D])
        pv = sb("pv", [P, 2, TB, TB, VW])
        weighed = sb("weighed", [P, TB, TB, HD])
        half_sum, o_sum = sb("half_sum", [P, 2, TB, HD]), sb("o_sum", [P, TB, HD])
        l_part = sb("l_part", [P, TB, TB])
        l_sum, l_rec = sb("l_sum", [P, TB, 1]), sb("l_rec", [P, 2, TB, 1])
        o_group = sb("o_group", [P, TB, P])
        OT_hi, OT_lo = sb("OT_hi", [P, NG, S], F32R), sb("OT_lo", [P, NG, S], F32R)
        bo = sb("bo", [P, D])
        stats, mean = sb("stats", [P, TB, 6]), sb("mean", [P, TB])
        var, rstd, tmp = sb("var", [P, TB]), sb("rstd", [P, TB]), sb("tmp", [P, TB])
        row_max, gap, gain = (sb(n, [P, 2, TB, 2 * TB]) for n in ("row_max", "gap", "gain"))
        whole_max = sb("whole_max", [P, 2 * TB])
        neg_shift = sb("neg_shift", [P, 2 * TB, TB])
        shift_parts = sb("shift_parts", [P, 2 * TB, 2, TB], F32R)
        block_one = sb("block_one", [P, TB])

        x_in, w_raw, wo_raw, small_in = sem("x_in"), [sem(f"w_raw{k}") for k in range(KB)], sem("wo_raw"), sem("small_in")
        wv_lo_made = sem("wv_lo_made")
        w_hi_made, w_lo_made, wo_hi_made, wo_lo_made = sem("w_hi_made"), sem("w_lo_made"), sem("wo_hi_made"), sem("wo_lo_made")
        ones_set = sem("ones_set")
        ln_chain, xn_ready, xT_psum, xT_hi_made, xT_lo_made = (
            sem("ln_chain"), sem("xn_ready"), sem("xT_psum"), sem("xT_hi_made"), sem("xT_lo_made"))
        qk_psum, qk_hi_made, qk_lo_made = sem("qk_psum"), sem("qk_hi_made"), sem("qk_lo_made")
        v_psum, v_made = sem("v_psum"), sem("v_made")
        stack_in = [sem(f"stack_in{i}") for i in range(SLOTS)]
        s_psum, max_made, whole_made, gap_made, shift_made, shift_hi_made, shift_lo_made, gain_made = (
            sem("s_psum"), sem("max_made"), sem("whole_made"), sem("gap_made"), sem("shift_made"),
            sem("shift_hi_made"), sem("shift_lo_made"), sem("gain_made"))
        shiftT_psum, shift_rows_made = sem("shiftT_psum"), sem("shift_rows_made")
        st_psum, exp_made, pv_psum, pv_made = sem("st_psum"), sem("exp_made"), sem("pv_psum"), sem("pv_made")
        l_part_made, l_sum_made, l_rec_made, combine_chain = (
            sem("l_part_made"), sem("l_sum_made"), sem("l_rec_made"), sem("combine_chain"))
        OT_psum, OT_hi_made, OT_lo_made, y_psum, bias_added, x1_made = (
            sem("OT_psum"), sem("OT_hi_made"), sem("OT_lo_made"), sem("y_psum"), sem("bias_added"), sem("x1_made"))

        NCH = KB * 3
        TP = 2 * TB
        ROWS = STACK + SHIFT
        Q_HI, K_LO, Q_LO, K_HI = range(4)
        LAST = NSTEP + 9
        Y_BANK = (7, 4, 5, 6)
        LN_SCALE_STEP = 16
        OT_STEPS = [24, 40, 56, LAST - 2]
        LN_ROW_STEPS = (22, 24, 27, 29)

        def staged(i):
            return xres[:, TB + i, :]

        def stacks_ready(b, p):
            return (b * (NPAIR // SLOTS) + p // SLOTS + 1) * 96

        def o_done(b, h):
            return (b * H + h + 1) * 4

        def wrap(b, p, more):
            if p < NPAIR:
                return b, p
            return (b + 1, p - NPAIR) if more else None

        def over_batches(eng, batch):
            with eng.Fori(0, B - 1) as b:
                batch(b, True)
            batch(B - 1, False)

        def row(b, j):
            if isinstance(b, int):
                return xres[:, b * TB + j, :]
            return xres[:, bass.ds(b * TB + j, 1), :].rearrange("p o d -> p (o d)")

        block = ctx.enter_context(nc.Block())

        @block.sync
        def _(sp):
            sp.dma_start(xres[:, 0:TB, :], xt[:, 0:TB, :]).then_inc(x_in, 16)
            sp.dma_start(ident[:, :], ident_in).then_inc(small_in, 16)
            for k in range(KB):
                sp.dma_start(xres[:, TB + 3 * k:TB + 3 * k + 3, :],
                             w_qkvT[k * P:(k + 1) * P, :].rearrange("p (c n) -> p c n", n=D)).then_inc(w_raw[k], 16)
            for part in range(2):
                r0 = STACK + part * TB
                sp.dma_start(block_one[r0:r0 + TB, :], ident_in[0:TB, 0:TB]).then_inc(small_in, 16)
            sp.dma_start(bo[:, :], b_out.rearrange("(a d) -> a d", a=1).broadcast_to([P, D])).then_inc(small_in, 16)

            def load_stacks(b, p, at_start=False):
                s, g, r0 = p % SLOTS, p // 2, (p % 2) * 2 * HD
                split = b * 2 * NG + 2 * g + 2
                free = b * NSTEP + (p - SLOTS + 1) * TP
                if not isinstance(b, int):
                    split, free = sp.to_reg(split), sp.to_reg(free)
                sp.wait_ge(qk_lo_made, split)
                if not at_start:
                    sp.wait_ge(st_psum, free)
                for hh in range(2):
                    rows = slice(r0 + hh * HD, r0 + (hh + 1) * HD)
                    for r, parts in enumerate((slice(Q_HI, K_HI + 1, K_HI - Q_HI), slice(Q_HI, K_LO + 1), slice(Q_LO, K_HI + 1))):
                        sp.dma_start(stack[r * HD:(r + 1) * HD, s, hh, :, :].bitcast(F32),
                                     qk_parts[rows, parts, :].bitcast(F32)).then_inc(stack_in[s], 16)

            sp.wait_ge(w_lo_made, 2 * KB)
            sp.wait_ge(wv_lo_made, KB)
            sp.dma_start(xres[:, TB:2 * TB, :], w_outT.rearrange("(k p) n -> p k n", p=P)).then_inc(wo_raw, 16)
            load_stacks(0, 0, True)
            load_stacks(0, 1, True)
            load_stacks(0, 2, True)
            sp.wait_ge(wo_lo_made, KB)
            sp.wait_ge(x_in, 16)
            sp.dma_start(xres[:, TB:NT, :], xt[:, TB:NT, :]).then_inc(x_in, 16)

            def batch(b, more):
                for p in range(NPAIR):
                    ahead = wrap(b, p + 3, more)
                    if ahead:
                        load_stacks(*ahead)

            over_batches(sp, batch)

        @block.gpsimd
        def _(pool):
            pool.memset(v_ones[:, :, :, HD:VW], 1.0).then_inc(ones_set, 1)
            for k in range(KB):
                for c in range(2):
                    pool.wait_ge(w_hi_made, 3 * k + c + 1)
                    pool.tensor_tensor(w_lo[:, k, c * D:(c + 1) * D], staged(3 * k + c), w_hi[:, k, c * D:(c + 1) * D].bitcast(F32),
                                       ALU.subtract).then_inc(w_lo_made, 1)
            for k in range(KB):
                pool.wait_ge(wo_hi_made, k + 1)
                pool.tensor_tensor(wo_lo[:, k, :], xres[:, TB + k, :], wo_hi[:, k, :].bitcast(F32), ALU.subtract)\
                    .then_inc(wo_lo_made, 1)
            pool.wait_ge(small_in, 64)

            def add_bias(b):
                for j in range(TB):
                    pool.wait_ge(xn_ready, b * TB + j + 1)
                    pool.tensor_tensor(row(b, j), row(b, j), bo[:, :], ALU.add).then_inc(bias_added, 1)

            def batch(b, more):
                for h in range(H):
                    chain = Chain(pool, combine_chain, (b * H + h) * 4)
                    pool.wait_ge(pv_made, b * NSTEP + TB * (h + 1))
                    chain.then(pool.tensor_tensor(weighed[:, :, :, :], pv[:, h % 2, :, :, 0:HD],
                                                  pv[:, h % 2, :, :, HD:VW].broadcast_to([P, TB, TB, HD]), ALU.mult))
                    chain.then(pool.tensor_tensor(half_sum[:, :, :, :], weighed[:, 0:2, :, :], weighed[:, 2:4, :, :], ALU.add))
                    chain.then(pool.tensor_tensor(o_sum[:, :, :], half_sum[:, 0, :, :], half_sum[:, 1, :, :], ALU.add))
                    pool.wait_ge(l_rec_made, b * H + h + 1)
                    if h % HG == 0 and h:
                        pool.wait_ge(OT_psum, b * NG + h // HG)
                    chain.then(pool.tensor_tensor(o_group[:, :, (h % HG) * HD:(h % HG + 1) * HD], o_sum[:, :, :],
                                                  l_rec[:, h % 2, :, :].broadcast_to([P, TB, HD]), ALU.mult))
                    if h == 9 and more:
                        add_bias(b + 1)

            add_bias(0)
            over_batches(pool, batch)

        @block.scalar
        def _(act):
            def xT_high(b, j):
                act.wait_ge(xT_psum, b * TB + j + 1)
                act.activation(xT_hi[:, :, j * P:(j + 1) * P], bank[7][:, :].rearrange("p (k t) -> p k t", k=KB), ACT.Copy)\
                    .then_inc(xT_hi_made, 1)

            def qk_high(b, g, which, at_start=False, src=7):
                act.wait_ge(qk_psum, b * 2 * NG + 2 * g + which + 1)
                if which == 0 and not at_start:
                    for p in (2 * g - 2, 2 * g - 1):
                        bb, pp = (b, p) if p >= 0 else (b - 1, p + NPAIR)
                        act.wait_ge(stack_in[pp % SLOTS], stacks_ready(bb, pp))
                act.activation(qk_parts[:, K_HI if which else Q_HI, :], bank[src][:, :], ACT.Copy).then_inc(qk_hi_made, 1)

            def v_copy(b, t):
                act.wait_ge(v_psum, b * TB + t + 1)
                act.activation(v_ones[:, t, :, 0:HD], bank[4 + t % 2][:, :].rearrange("p (h d) -> p h d", h=H), ACT.Copy)\
                    .then_inc(v_made, 1)

            def gains(b, p, used=None):
                act.wait_ge(gap_made, b * NPAIR + p + 1)
                if used is not None:
                    act.wait_ge(l_part_made, used)
                act.activation(gain[:, p % 2, :, :], gap[:, p % 2, :, :], ACT.Exp, scale=0.5 * ATT_SCALE).then_inc(gain_made, 1)

            def shift_rows(b, p, hh):
                act.wait_ge(shiftT_psum, b * H + 2 * p + hh + 1)
                act.activation(stack[STACK:ROWS, p % SLOTS, hh, 0, :], bank[6][0:SHIFT, :], ACT.Copy).then_inc(shift_rows_made, 1)

            def batch(b, more):
                for n in range(LAST):
                    p, t = divmod(n, TP)
                    m = n - LAG - 1
                    if 0 <= m < NSTEP:
                        h, kb = divmod(m, TB)
                        act.wait_ge(pv_psum, b * NSTEP + m + 1)
                        if kb == 0 and h >= 2:
                            act.wait_ge(combine_chain, o_done(b, h - 2))
                            act.wait_ge(l_part_made, b * H + h - 1)
                        act.activation(pv[:, h % 2, kb, :, :], bank[4 + m % 2][:, 0:TB * VW].rearrange("p (t w) -> p t w", w=VW), ACT.Copy)\
                            .then_inc(pv_made, 1)
                    if n < NSTEP:
                        act.wait_ge(st_psum, b * NSTEP + n + 1)
                        if n >= PRING:
                            act.wait_ge(pv_psum, b * NSTEP + n - PRING + 1)
                        act.activation(probs[:, n % PRING, :], bank[2 + n % 2][:, :], ACT.Exp, scale=ATT_SCALE).then_inc(exp_made, 1)
                        ahead = wrap(b, p + 4, more)
                        if p % 2 == 0 and t in (3, 7) and ahead:
                            qk_high(ahead[0], ahead[1] // 2, t // 4)
                        if p == 3 and t % 2 and more:
                            xT_high(b + 1, t // 2)
                        ahead = wrap(b, p + 1, more)
                        if t in (4, 6) and ahead:
                            shift_rows(*ahead, t // 6)
                        if t == 5 and ahead:
                            gains(*ahead, used=b * H + 2 * p if p else None)
                    if more and NSTEP + LAG <= n < NSTEP + LAG + TB:
                        v_copy(b + 1, n - NSTEP - LAG)
                    if n in OT_STEPS:
                        g = OT_STEPS.index(n)
                        act.wait_ge(OT_psum, b * NG + g + 1)
                        act.activation(OT_hi[:, g, :], bank[6][:, :], ACT.Copy).then_inc(OT_hi_made, 1)

            for i in range(NCH):
                k, c = divmod(i, 3)
                act.wait_ge(w_raw[k], 16)
                act.activation(w_hi[:, k, c * D:(c + 1) * D], staged(i), ACT.Copy).then_inc(w_hi_made, 1)
                if i % 3 == 2:
                    xT_high(0, k)
            qk_high(0, 0, 0, True)
            qk_high(0, 0, 1, True, src=6)
            v_copy(0, 0)
            for k in range(KB):
                act.wait_ge(wo_raw, 16)
                act.activation(wo_hi[:, k, :], xres[:, TB + k, :], ACT.Copy).then_inc(wo_hi_made, 1)
            qk_high(0, 1, 0)
            v_copy(0, 1)
            qk_high(0, 1, 1, src=6)
            v_copy(0, 2)
            v_copy(0, 3)
            shift_rows(0, 0, 0)
            shift_rows(0, 0, 1)
            gains(0, 0)
            over_batches(act, batch)

        @block.vector
        def _(dve):
            def ln_stats(b, j):
                if j == 0:
                    dve.wait_ge(x_in, 16 if isinstance(b, int) and b == 0 else 32)
                dve.bn_stats(stats[:, j, :], row(b, j)).then_inc(ln_chain, 1)

            def ln_scale(b, part):
                base = b * (TB + 9 + 3 * NEWTON)
                before = TB + (0, 6)[part > 0] + 3 * max(part - 1, 0)
                if part == 0:
                    dve.wait_ge(ln_chain, base + TB)
                chain = Chain(dve, ln_chain, base + before)
                if part == 0:
                    moments(dve, stats, mean[:, :], var[:, :], tmp[:, :], chain)
                elif part == 1:
                    rsqrt_guess(dve, var[:, :], rstd[:, :], tmp[:, :], chain)
                else:
                    newton_step(dve, var[:, :], rstd[:, :], tmp[:, :], chain)

            def ln_row(b, j):
                if j >= 2:
                    dve.wait_ge(xT_psum, b * TB + j - 1)
                dve.tensor_scalar(xn[:, j % 2, :], row(b, j), mean[:, j:j + 1], rstd[:, j:j + 1], ALU.subtract, ALU.mult)\
                    .then_inc(xn_ready, 1)

            def xT_low(b, j):
                dve.wait_ge(xT_hi_made, b * TB + j + 1)
                dve.tensor_tensor(xT_lo[:, :, j * P:(j + 1) * P], bank[7][:, :].rearrange("p (k t) -> p k t", k=KB),
                                  xT_hi[:, :, j * P:(j + 1) * P].bitcast(F32), ALU.subtract).then_inc(xT_lo_made, 1)

            def qk_low(b, g, which, src=7):
                dve.wait_ge(qk_hi_made, b * 2 * NG + 2 * g + which + 1)
                dve.tensor_tensor(qk_parts[:, K_LO if which else Q_LO, :], bank[src][:, :],
                                  qk_parts[:, K_HI if which else Q_HI, :].bitcast(F32), ALU.subtract).then_inc(qk_lo_made, 1)

            def tile_max(b, p, t):
                dve.wait_ge(s_psum, b * NSTEP + p * TP + t + 1)
                dve.reduce_max(row_max[:, p % 2, :, t:t + 1], bank[t % 2][:, :].rearrange("q (k n) -> q k n", k=TB), AX.X)\
                    .then_inc(max_made, 1)

            def shifts(b, p):
                i = b * NPAIR + p + 1
                dve.wait_ge(max_made, i * TP)
                dve.tensor_reduce(whole_max[:, :], row_max[:, p % 2, :, :].rearrange("q k x -> q x k"), AX.X, ALU.max)\
                    .then_inc(whole_made, 1)
                dve.wait_ge(whole_made, i)
                dve.tensor_tensor(gap[:, p % 2, :, :], row_max[:, p % 2, :, :],
                                  whole_max[:, :].rearrange("q (o x) -> q o x", o=1).broadcast_to([P, TB, 2 * TB]), ALU.subtract)\
                    .then_inc(gap_made, 1)
                dve.wait_ge(gap_made, i)
                dve.scalar_tensor_tensor(out=neg_shift[:, :, :].rearrange("q x k -> q k x"), in0=gap[:, p % 2, :, :], scalar=0.5,
                                         in1=row_max[:, p % 2, :, :], op0=ALU.mult, op1=ALU.subtract).then_inc(shift_made, 1)
                dve.wait_ge(shift_made, i)
                dve.tensor_copy(shift_parts[:, :, 0, :], neg_shift[:, :, :]).then_inc(shift_hi_made, 1)
                dve.wait_ge(shift_hi_made, i)
                dve.tensor_tensor(shift_parts[:, :, 1, :], neg_shift[:, :, :], shift_parts[:, :, 0, :].bitcast(F32), ALU.subtract)\
                    .then_inc(shift_lo_made, 1)

            def batch(b, more):
                for n in range(LAST):
                    p, t = divmod(n, TP)
                    if n < NSTEP:
                        ahead = wrap(b, p + 2, more)
                        if ahead:
                            tile_max(*ahead, t)
                        ahead = wrap(b, p + 1, more)
                        if t == 1 and ahead:
                            shifts(*ahead)
                        ahead = wrap(b, p + 4, more)
                        if p % 2 == 0 and t in (3, 7) and ahead:
                            qk_low(ahead[0], ahead[1] // 2, t // 4)
                    if more and p == 1 and t % 2:
                        ln_stats(b + 1, t // 2)
                    if more and 0 <= n - LN_SCALE_STEP < 2 + NEWTON:
                        ln_scale(b + 1, n - LN_SCALE_STEP)
                    if more and n in LN_ROW_STEPS:
                        ln_row(b + 1, LN_ROW_STEPS.index(n))
                    if more and n in (26, 28, 30, 32):
                        xT_low(b + 1, (n - 26) // 2)
                    h = (n - LAG - 5) // TB
                    if h >= 0 and (n - LAG - 5) % TB == 0 and h < H:
                        i = b * H + h + 1
                        hh = h % 2
                        dve.wait_ge(pv_made, b * NSTEP + TB * (h + 1))
                        dve.wait_ge(gain_made, b * NPAIR + h // 2 + 1)
                        dve.tensor_tensor(l_part[:, :, :], pv[:, h % 2, :, :, HD:VW].rearrange("p k t o -> p k (t o)"),
                                          gain[:, h // 2 % 2, :, hh * TB:(hh + 1) * TB], ALU.mult).then_inc(l_part_made, 1)
                        dve.wait_ge(l_part_made, i)
                        dve.tensor_reduce(l_sum[:, :, 0], l_part[:, :, :].rearrange("p k t -> p t k"), AX.X, ALU.add)\
                            .then_inc(l_sum_made, 1)
                        dve.wait_ge(l_sum_made, i)
                        if h >= 2:
                            dve.wait_ge(combine_chain, o_done(b, h - 2))
                        dve.reciprocal(l_rec[:, h % 2, :, :], l_sum[:, :, :]).then_inc(l_rec_made, 1)
                    if n - 1 in OT_STEPS:
                        g = OT_STEPS.index(n - 1)
                        dve.wait_ge(OT_hi_made, b * NG + g + 1)
                        dve.tensor_tensor(OT_lo[:, g, :], bank[6][:, :], OT_hi[:, g, :].bitcast(F32), ALU.subtract)\
                            .then_inc(OT_lo_made, 1)
                for j in range(TB):
                    dve.wait_ge(y_psum, b * TB + j + 1)
                    dve.wait_ge(bias_added, b * TB + j + 1)
                    dve.tensor_tensor(row(b, j), bank[Y_BANK[j]][:, :], row(b, j), ALU.add).then_inc(x1_made, 1)

            for j in range(TB):
                ln_stats(0, j)
            for part in range(2 + NEWTON):
                ln_scale(0, part)
            for j in range(TB):
                ln_row(0, j)
                if j:
                    xT_low(0, j - 1)
            xT_low(0, TB - 1)
            for k in range(KB):
                dve.wait_ge(w_hi_made, 3 * k + 3)
                dve.tensor_tensor(w_lo[:, k, 2 * D:], staged(3 * k + 2), w_hi[:, k, 2 * D:].bitcast(F32), ALU.subtract)\
                    .then_inc(wv_lo_made, 1)
            dve.wait_ge(small_in, 64)
            for s in range(SLOTS):
                dve.tensor_copy(stack[STACK:ROWS, s, :, 1, :].rearrange("r h (k n) -> r h k n", k=TB),
                                block_one[STACK:ROWS, :].rearrange("r (a k b) -> r a k b", a=1, b=1)
                                .broadcast_to([SHIFT, 2, TB, P])).then_inc(ones_set, 1)
            dve.sem_inc(x1_made, TB)
            qk_low(0, 0, 0)
            qk_low(0, 0, 1, src=6)
            qk_low(0, 1, 0)
            qk_low(0, 1, 1, src=6)
            for p in range(2):
                for t in range(TP):
                    tile_max(0, p, t)
                if p == 0:
                    shifts(0, 0)
            over_batches(dve, batch)

        @block.tensor
        def _(pe):
            def turn_row(b, j):
                pe.wait_ge(xn_ready, b * TB + j + 1)
                if j:
                    pe.wait_ge(xT_lo_made, b * TB + j)
                for k in range(KB):
                    last = pe.transpose(bank[7][:, k * P:(k + 1) * P], xn[:, j % 2, k * P:(k + 1) * P], ident[:, :])
                last.then_inc(xT_psum, 1)

            def qk(b, g, which, ks, dst=7):
                cols = slice(which * D + g * P, which * D + (g + 1) * P)
                for k in ks:
                    last = matmul3(pe, bank[dst][:, :], w_hi[:, k, cols], w_lo[:, k, cols], xT_hi[:, k, :], xT_lo[:, k, :],
                                   k == 0, k == KB - 1)
                if ks[-1] == KB - 1:
                    last.then_inc(qk_psum, 1)

            def values(b, t, ks=(0, 1, 2, 3)):
                for k in ks:
                    last = matmul3(pe, bank[4 + t % 2][:, :], xT_hi[:, k, t * P:(t + 1) * P], xT_lo[:, k, t * P:(t + 1) * P],
                                   w_hi[:, k, 2 * D:], w_lo[:, k, 2 * D:], k == 0, k == KB - 1)
                if ks[-1] == KB - 1:
                    last.then_inc(v_psum, 1)

            def scores(b, p, t, first=False):
                hh, qb = divmod(t, TB)
                if t == 0:
                    pe.wait_ge(stack_in[p % SLOTS], stacks_ready(b, p))
                if not first:
                    pe.wait_ge(max_made, b * NSTEP + p * TP + t - 1)
                pe.matmul(bank[t % 2][:, :], stack[0:STACK, p % SLOTS, hh, 0, qb * P:(qb + 1) * P],
                          stack[0:STACK, p % SLOTS, hh, 1, :], start=True, stop=True).then_inc(s_psum, 1)

            def turn_shifts(b, p, hh):
                pe.wait_ge(shift_lo_made, b * NPAIR + p + 1)
                for qb in range(TB):
                    last = pe.transpose(bank[6][0:SHIFT, qb * P:(qb + 1) * P],
                                        shift_parts[:, hh * TB + qb, :, :].bitcast(F32).rearrange("q a k -> q (a k)"), ident[:, :])
                last.then_inc(shiftT_psum, 1)

            def batch(b, more):
                for n in range(LAST):
                    p, t = divmod(n, TP)
                    if n < NSTEP:
                        ahead = wrap(b, p + 2, more)
                        if ahead:
                            scores(*ahead, t)
                        hh, kb = divmod(t, TB)
                        if kb == 0:
                            pe.wait_ge(shift_rows_made, b * H + 2 * p + hh + 1)
                        if n >= 2:
                            pe.wait_ge(exp_made, b * NSTEP + n - 1)
                        pe.matmul(bank[2 + n % 2][:, :], stack[0:ROWS, p % SLOTS, hh, 1, kb * P:(kb + 1) * P],
                                  stack[0:ROWS, p % SLOTS, hh, 0, :], start=True, stop=True).then_inc(st_psum, 1)
                        ahead = wrap(b, p + 4, more)
                        if p % 2 == 0 and ahead:
                            bb, g = ahead[0], ahead[1] // 2
                            if p == 0 and t == 1:
                                pe.wait_ge(x1_made, b * TB + 1)
                            if p == 4 and t == 1:
                                pe.wait_ge(xT_lo_made, bb * TB + TB)
                            if t == 5 or (t == 1 and p == 6):
                                pe.wait_ge(qk_lo_made, bb * 2 * NG + 2 * g + t // 4)
                            if t in (1, 2, 5, 6):
                                qk(bb, g, t // 4, (0, 1) if t % 4 == 1 else (2, 3))
                        ahead = wrap(b, p + 1, more)
                        if t in (3, 5) and ahead:
                            pe.wait_ge(shift_rows_made, ahead[0] * H + 2 * ahead[1] + t // 5)
                            if p == 0 and t == 3:
                                pe.wait_ge(x1_made, b * TB + TB)
                            if p % 2 and p > 1 and t == 3:
                                pe.wait_ge(OT_lo_made, b * NG + p // 2)
                            turn_shifts(*ahead, t // 5)
                    m = n - LAG
                    if 0 <= m < NSTEP:
                        h, kb = divmod(m, TB)
                        pe.wait_ge(exp_made, b * NSTEP + m + 1)
                        if m >= 2:
                            pe.wait_ge(pv_made, b * NSTEP + m - 1)
                        else:
                            pe.wait_ge(x1_made, b * TB + m + 2)
                        if m == 0:
                            pe.wait_ge(v_made, b * TB + TB)
                        for qb in range(TB):
                            last = pe.matmul(bank[4 + m % 2][:, qb * VW:(qb + 1) * VW], probs[:, m % PRING, qb * P:(qb + 1) * P],
                                             v_ones[:, kb, h, :], start=True, stop=True)
                        last.then_inc(pv_psum, 1)
                    if p == 3 and t % 2 and more:
                        if t == 1:
                            pe.wait_ge(qk_lo_made, b * 2 * NG + 2 * NG)
                        turn_row(b + 1, t // 2)
                    if more and NSTEP + LAG <= n < NSTEP + LAG + TB:
                        v = n - NSTEP - LAG
                        if v < 2:
                            pe.wait_ge(pv_made, (b + 1) * NSTEP - 1 + v)
                        else:
                            pe.wait_ge(v_made, (b + 1) * TB + v - 1)
                        values(b + 1, v)
                    if n in OT_STEPS:
                        g = OT_STEPS.index(n)
                        pe.wait_ge(combine_chain, o_done(b, (g + 1) * HG - 1))
                        if n < NSTEP:
                            pe.wait_ge(shift_rows_made, b * H + 2 * p + 2)
                        elif more:
                            pe.wait_ge(shift_rows_made, (b + 1) * H + 2)
                        else:
                            pe.wait_ge(OT_lo_made, b * NG + g)
                        for t4 in range(TB):
                            last = pe.transpose(bank[6][:, t4 * P:(t4 + 1) * P], o_group[:, t4, :], ident[:, :])
                        last.then_inc(OT_psum, 1)
                for j in range(TB):
                    if j == 0:
                        pe.wait_ge(wo_lo_made, KB)
                        pe.wait_ge(qk_lo_made, b * 2 * NG + 2 * NG + (4 if more else 0))
                    elif j < 3:
                        if more:
                            pe.wait_ge(v_made, (b + 1) * TB + j + 2)
                        else:
                            pe.wait_ge(pv_made, (b + 1) * NSTEP - 2 + j)
                    for g in range(NG):
                        if j == 0 and g == NG - 1:
                            pe.wait_ge(OT_lo_made, b * NG + NG)
                        last = matmul3(pe, bank[Y_BANK[j]][:, :], OT_hi[:, g, j * P:(j + 1) * P], OT_lo[:, g, j * P:(j + 1) * P],
                                       wo_hi[:, g, :], wo_lo[:, g, :], g == 0, g == NG - 1)
                    last.then_inc(y_psum, 1)

            pe.wait_ge(small_in, 64)
            for j in range(TB):
                turn_row(0, j)
            pe.wait_ge(xT_lo_made, TB)
            for k in range(KB):
                pe.wait_ge(w_lo_made, 2 * k + 2)
                qk(0, 0, 0, (k,))
            qk(0, 0, 1, (0, 1, 2, 3), dst=6)
            pe.wait_ge(wv_lo_made, KB)
            values(0, 0)
            pe.wait_ge(qk_lo_made, 1)
            qk(0, 1, 0, (0, 1, 2, 3))
            values(0, 1)
            pe.wait_ge(qk_lo_made, 2)
            qk(0, 1, 1, (0, 1, 2, 3), dst=6)
            pe.wait_ge(ones_set, 1 + SLOTS)
            for t in range(TP):
                scores(0, 0, t, first=t < 2)
                v, k = 2 + t // KB, t % KB
                if k == 0:
                    pe.wait_ge(v_made, v - 1)
                values(0, v, (k,))
            pe.wait_ge(qk_lo_made, 4)
            turn_shifts(0, 0, 0)
            for t in range(TP):
                scores(0, 1, t)
                if t == TP // 2:
                    pe.wait_ge(shift_rows_made, 1)
                    turn_shifts(0, 0, 1)
            over_batches(pe, batch)


def cross_attention(nc, xres, stats, norm, wr_raw, temp, ident, bank, Wr, temperature, ctxT, wqT, bq, wkT, bk, Wg, Wu, Wd, GaT, Gb, UaT, Ub, DaT, Db, w_fix):
    with ExitStack() as ctx:
        def sb(name, shape, dt=F32):
            return ctx.enter_context(nc.sbuf_tensor("c_" + name, shape, dt))

        def sem(name):
            return ctx.enter_context(nc.semaphore("c_" + name))

        c_raw = sb("c_raw", [P, CB, B, S])
        c_hi, c_lo = sb("c_hi", [P, CB, B, S], F32R), sb("c_lo", [P, CB, B, S], F32R)
        w_raw = sb("w_raw", [P, 2, CB, P])
        w_hi, w_lo = sb("w_hi", [P, 2, CB, P], F32R), sb("w_lo", [P, 2, CB, P], F32R)
        bias = sb("bias", [P, 2])
        qk = sb("qk", [P, 2, S])
        qk_hi, qk_lo = sb("qk_hi", [P, 2, S], F32R), sb("qk_lo", [P, 2, S], F32R)
        att = sb("att", [P, 2, S])
        neg_max, row_sum, rec_sum = sb("neg_max", [P, TB]), sb("row_sum", [P, TB]), sb("rec_sum", [P, TB])
        aT_hi, aT_lo = sb("aT_hi", [P, 2, KB, S], F32R), sb("aT_lo", [P, 2, KB, S], F32R)
        xn = sb("xn", [P, 2, D])
        xT_hi, xT_lo = sb("xT_hi", [P, KB, S], F32R), sb("xT_lo", [P, KB, S], F32R)
        mean, var, rstd, tmp = norm
        down = sb("down", [R, NL, 3, D])
        up = sb("up", [R, NL, 3, FF])
        w_full = sb("w_full", [P, 3, KB, FF])

        w_in, ctx_in = sem("w_in"), [sem("ctx_in0"), sem("ctx_in_rest")]
        lora_in, w_full_in, w_fixed, fix_stored = sem("lora_in"), sem("w_full_in"), sem("w_fixed"), sem("fix_stored")
        w_hi_made, w_lo_made, c_hi_made, c_lo_made = sem("w_hi_made"), sem("w_lo_made"), sem("c_hi_made"), sem("c_lo_made")
        qk_psum, qk_made, qk_hi_made, qk_lo_made = sem("qk_psum"), sem("qk_made"), sem("qk_hi_made"), sem("qk_lo_made")
        e_psum, max_made, exp_made, rec_made, att_made = (
            sem("e_psum"), sem("max_made"), sem("exp_made"), sem("rec_made"), sem("att_made"))
        aT_psum, aT_hi_made, aT_lo_made, y_psum, x2_made = (
            sem("aT_psum"), sem("aT_hi_made"), sem("aT_lo_made"), sem("y_psum"), sem("x2_made"))
        ln_chain, xn_ready, xT_psum, xT_hi_made, xT_lo_made, fix_psum = (
            sem("ln_chain"), sem("xn_ready"), sem("xT_psum"), sem("xT_hi_made"), sem("xT_lo_made"), sem("fix_psum"))
        stats_made, router_in, wr_zero = sem("stats_made"), sem("router_in"), sem("wr_zero")
        NFIX = 3 * KB

        def over_batches(eng, front, body):
            front(0)
            with eng.Fori(0, B - 1) as b:
                body(b, b + 1)
            body(B - 1, None)

        def row(b, j):
            if isinstance(b, int):
                return xres[:, b * TB + j, :]
            return xres[:, bass.ds(b * TB + j, 1), :].rearrange("p o d -> p (o d)")

        def of_batch(t, b, n):
            if n == 2:
                return t[:, b % 2, :, :] if isinstance(b, int) else t[:, bass.ds(b & 1, 1), :, :].rearrange("p o k s -> p (o k) s")
            return t[:, :, b, :] if isinstance(b, int) else t[:, :, bass.ds(b, 1), :].rearrange("p c o s -> p c (o s)")

        block = ctx.enter_context(nc.Block())

        @block.sync
        def _(sp):
            for i, w in enumerate((wqT, wkT)):
                sp.dma_start(w_raw[:, i, :, :], w.rearrange("(c p) d -> p c d", p=P)).then_inc(w_in, 16)
            for b in range(B):
                sp.dma_start(c_raw[:, :, b, :], ctxT[b, :, :].rearrange("(c p) s -> p c s", p=P))\
                    .then_inc(ctx_in[b > 0], 16)
                if b == 0:
                    for i, v in enumerate((bq, bk)):
                        sp.dma_start(bias[:, i:i + 1], v.rearrange("(d a) -> d a", a=1)).then_inc(w_in, 16)
            sp.dma_start(temp[:, 0:1], temperature.rearrange("(a d) -> a d", a=1).broadcast_to([P, 1])).then_inc(router_in, 16)
            sp.wait_ge(wr_zero, 1)
            sp.dma_start(wr_raw[:, :, 0:NE], Wr.rearrange("(k p) e -> p k e", p=P)).then_inc(router_in, 16)
            for m, (a, v) in enumerate(((GaT, Gb), (UaT, Ub), (DaT, Db))):
                sp.dma_start(down[:, :, m, :], a.rearrange("e r d -> r e d")).then_inc(lora_in, 16)
                sp.dma_start(up[:, :, m, :], v.rearrange("e r d -> r e d")).then_inc(lora_in, 16)
            for e in range(NL):
                if e:
                    sp.wait_ge(fix_stored, 16 * 3 * e)
                for m, w in enumerate((Wg, Wu, Wd)):
                    sp.dma_start(w_full[:, m, :, :], w[e, :, :].rearrange("(k p) f -> p k f", p=P)).then_inc(w_full_in, 16)
                for m in range(3):
                    sp.wait_ge(w_fixed, e * NFIX + (m + 1) * KB)
                    sp.dma_start(w_fix[e, m, :, :].rearrange("(k p) f -> p k f", p=P), w_full[:, m, :, :]).then_inc(fix_stored, 16)
            sp.wait_ge(fix_stored, 16 * NL * 3)
            sp.wait_ge(router_in, 32)

        @block.gpsimd
        def _(pool):
            def c_low(b):
                pool.wait_ge(c_hi_made, b + 1)
                pool.tensor_tensor(c_lo[:, :, b, :], c_raw[:, :, b, :], c_hi[:, :, b, :].bitcast(F32), ALU.subtract)\
                    .then_inc(c_lo_made, 1)

            def front(b):
                for i in range(2):
                    pool.wait_ge(qk_hi_made, b * 2 + i + 1)
                    pool.tensor_tensor(qk_lo[:, i, :], qk[:, i, :], qk_hi[:, i, :].bitcast(F32), ALU.subtract).then_inc(qk_lo_made, 1)
                if isinstance(b, int):
                    for bb in range(1, B):
                        c_low(bb)

            def body(b, nb):
                if nb is not None:
                    front(nb)

            pool.memset(wr_raw[:, :, :], 0.0).then_inc(wr_zero, 1)
            pool.wait_ge(w_hi_made, 1)
            pool.tensor_tensor(w_lo[:, :, :, :], w_raw[:, :, :, :], w_hi[:, :, :, :].bitcast(F32), ALU.subtract)\
                .then_inc(w_lo_made, 1)
            c_low(0)
            over_batches(pool, front, body)

        @block.scalar
        def _(act):
            def c_high(b):
                act.wait_ge(ctx_in[b > 0], 16 if b == 0 else 16 * (B - 1))
                act.activation(c_hi[:, :, b, :], c_raw[:, :, b, :], ACT.Copy).then_inc(c_hi_made, 1)

            def front(b):
                for i in range(2):
                    act.wait_ge(qk_psum, b * 2 + i + 1)
                    act.activation(qk[:, i, :], bank[6 + i][:, :], ACT.Identity, bias=bias[:, i:i + 1]).then_inc(qk_made, 1)
                    act.wait_ge(qk_made, b * 2 + i + 1)
                    act.activation(qk_hi[:, i, :], qk[:, i, :], ACT.Copy).then_inc(qk_hi_made, 1)

                def att_high(j):
                    act.wait_ge(aT_psum, b * TB + j + 1)
                    act.activation(of_batch(aT_hi, b, 2)[:, :, j * P:(j + 1) * P],
                                   bank[4 + j % 2][:, :].rearrange("p (k t) -> p k t", k=KB), ACT.Copy).then_inc(aT_hi_made, 1)

                def row_high(j):
                    act.wait_ge(xT_psum, b * TB + j + 1)
                    act.activation(xT_hi[:, :, j * P:(j + 1) * P], bank[2 + j % 2][:, :].rearrange("p (k t) -> p k t", k=KB), ACT.Copy)\
                        .then_inc(xT_hi_made, 1)

                for j in range(TB):
                    act.wait_ge(max_made, b * TB + j + 1)
                    if j >= 2:
                        act.wait_ge(aT_psum, b * TB + j - 1)
                    act.activation(att[:, j % 2, :], bank[6 + j % 2][:, :], ACT.Exp, bias=neg_max[:, j:j + 1],
                                   accum_out=row_sum[:, j:j + 1]).then_inc(exp_made, 1)
                    if isinstance(b, int) and j:
                        c_high(j)
                    if j >= 1:
                        row_high(j - 1)
                    if j >= 2:
                        att_high(j - 2)
                att_high(2)
                row_high(3)
                att_high(3)

            def body(b, nb):
                if nb is not None:
                    front(nb)

            act.wait_ge(w_in, 64)
            act.activation(w_hi[:, :, :, :], w_raw[:, :, :, :], ACT.Copy).then_inc(w_hi_made, 1)
            c_high(0)
            over_batches(act, front, body)

        @block.vector
        def _(dve):
            def row_low(b, j):
                dve.wait_ge(xT_hi_made, b * TB + j + 1)
                dve.tensor_tensor(xT_lo[:, :, j * P:(j + 1) * P], bank[2 + j % 2][:, :].rearrange("p (k t) -> p k t", k=KB),
                                  xT_hi[:, :, j * P:(j + 1) * P].bitcast(F32), ALU.subtract).then_inc(xT_lo_made, 1)

            def ln_row(b, j):
                if j >= 2:
                    dve.wait_ge(xT_psum, b * TB + j - 1)
                of_row = bass.ds(b * TB + j, 1)
                dve.tensor_scalar(xn[:, j % 2, :], row(b, j), mean[:, of_row], rstd[:, of_row], ALU.subtract, ALU.mult)\
                    .then_inc(xn_ready, 1)

            def att_low(b, j):
                dve.wait_ge(aT_hi_made, b * TB + j + 1)
                dve.tensor_tensor(of_batch(aT_lo, b, 2)[:, :, j * P:(j + 1) * P],
                                  bank[4 + j % 2][:, :].rearrange("p (k t) -> p k t", k=KB),
                                  of_batch(aT_hi, b, 2)[:, :, j * P:(j + 1) * P].bitcast(F32), ALU.subtract).then_inc(aT_lo_made, 1)

            def row_max(b, j):
                dve.wait_ge(e_psum, b * TB + j + 1)
                dve.tensor_reduce(neg_max[:, j:j + 1], bank[6 + j % 2][:, :], AX.X, ALU.max, negate=True).then_inc(max_made, 1)

            def att_scale(b, j):
                dve.wait_ge(exp_made, b * TB + j + 1)
                dve.reciprocal(rec_sum[:, j:j + 1], row_sum[:, j:j + 1]).then_inc(rec_made, 1)
                dve.wait_ge(rec_made, b * TB + j + 1)
                dve.tensor_scalar(att[:, j % 2, :], att[:, j % 2, :], rec_sum[:, j:j + 1], None, ALU.mult).then_inc(att_made, 1)

            def add_y(b, j):
                dve.wait_ge(y_psum, b * TB + j + 1)
                dve.tensor_tensor(row(b, j), bank[j % 2][:, :], row(b, j), ALU.add).then_inc(x2_made, 1)

            def finished_stats(b, j):
                dve.wait_ge(x2_made, b * TB + TB + j + 1)
                dve.bn_stats(stats[:, bass.ds(b * TB + j, 1), :].rearrange("p o s -> p (o s)"), row(b, j)).then_inc(stats_made, 1)

            def add_fix(e, i):
                m, k = divmod(i, KB)
                dve.wait_ge(w_full_in, 16 * 3 * (e + 1))
                dve.wait_ge(fix_psum, e * NFIX + i + 1)
                dve.tensor_tensor(w_full[:, m, k, :], bank[4 * e + i % 2][:, :], w_full[:, m, k, :], ALU.add).then_inc(w_fixed, 1)

            def front(b, back=None):
                def behind(j):
                    if back is not None:
                        add_y(back, j)

                def fixes(lo, hi):
                    if back is None:
                        for i in range(lo, hi):
                            add_fix(0, i)

                behind(0)
                row_max(b, 0)
                ln_row(b, 0)
                row_max(b, 1)
                att_scale(b, 0)
                ln_row(b, 1)
                behind(1)
                att_scale(b, 1)
                fixes(0, 4)
                row_low(b, 0)
                ln_row(b, 2)
                row_max(b, 2)
                behind(2)
                att_low(b, 0)
                row_max(b, 3)
                att_scale(b, 2)
                row_low(b, 1)
                ln_row(b, 3)
                att_scale(b, 3)
                fixes(4, 8)
                att_low(b, 1)
                row_low(b, 2)
                behind(3)
                att_low(b, 2)
                row_low(b, 3)
                att_low(b, 3)
                fixes(8, NFIX)

            def body(b, nb):
                if nb is not None:
                    front(nb, b)
                    for j in range(TB):
                        finished_stats(b, j)
                else:
                    for j in range(TB):
                        for i in range(4 * j, min(4 * j + 4, NFIX)):
                            add_fix(1, i)
                        add_y(b, j)
                        if j == TB - 2:
                            dve.wait_ge(stats_made, NT - TB)
                            ln_scale(chain, stats, norm, 0, NT - TB)
                    for j in range(TB):
                        finished_stats(B - 1, j)

            dve.sem_inc(x2_made, TB)
            with dve.Fori(0, B) as b:
                for j in range(TB):
                    dve.bn_stats(stats[:, bass.ds(b * TB + j, 1), :].rearrange("p o s -> p (o s)"), row(b, j)).then_inc(ln_chain, 1)
            dve.wait_ge(ln_chain, NT)
            chain = Chain(dve, ln_chain, NT)
            ln_scale(chain, stats, norm, 0, NT)
            over_batches(dve, front, body)
            dve.wait_ge(stats_made, NT)

        @block.tensor
        def _(pe):
            def project(b, i):
                if i == 0:
                    pe.wait_ge(c_lo_made, b + 1)
                for c in range(CB):
                    last = matmul3(pe, bank[6 + i][:, :], w_hi[:, i, c, :], w_lo[:, i, c, :], of_batch(c_hi, b, B)[:, c, :],
                                   of_batch(c_lo, b, B)[:, c, :], c == 0, c == CB - 1)
                last.then_inc(qk_psum, 1)

            def energies(b, j):
                if j == 0:
                    pe.wait_ge(qk_lo_made, b * 2 + 2)
                if j >= 2:
                    pe.wait_ge(exp_made, b * TB + j - 1)
                matmul3(pe, bank[6 + j % 2][:, :], qk_hi[:, 0, j * P:(j + 1) * P], qk_lo[:, 0, j * P:(j + 1) * P],
                        qk_hi[:, 1, :], qk_lo[:, 1, :], True, True).then_inc(e_psum, 1)

            def turn_att(b, j):
                pe.wait_ge(att_made, b * TB + j + 1)
                if j >= 2:
                    pe.wait_ge(aT_lo_made, b * TB + j - 1)
                for k in range(KB):
                    last = pe.transpose(bank[4 + j % 2][:, k * P:(k + 1) * P], att[:, j % 2, k * P:(k + 1) * P], ident[:, :])
                last.then_inc(aT_psum, 1)

            def turn_row(b, j):
                pe.wait_ge(xn_ready, b * TB + j + 1)
                if j >= 2:
                    pe.wait_ge(xT_lo_made, b * TB + j - 1)
                for k in range(KB):
                    last = pe.transpose(bank[2 + j % 2][:, k * P:(k + 1) * P], xn[:, j % 2, k * P:(k + 1) * P], ident[:, :])
                last.then_inc(xT_psum, 1)

            def products(b, j):
                if j == 0:
                    pe.wait_ge(aT_lo_made, b * TB + TB)
                    pe.wait_ge(xT_lo_made, b * TB + TB)
                    pe.wait_ge(w_fixed, NFIX)
                    pe.wait_ge(x2_made, b * TB + TB)
                if j >= 2:
                    pe.wait_ge(x2_made, b * TB + TB + j - 1)
                for k in range(KB):
                    last = matmul3(pe, bank[j % 2][:, :], xT_hi[:, k, j * P:(j + 1) * P], xT_lo[:, k, j * P:(j + 1) * P],
                                   of_batch(aT_hi, b, 2)[:, k, :], of_batch(aT_lo, b, 2)[:, k, :], k == 0, k == KB - 1)
                last.then_inc(y_psum, 1)

            def fix(e, i):
                m, k = divmod(i, KB)
                pe.wait_ge(lora_in, 16 * 6)
                if e and i == 0:
                    pe.wait_ge(aT_lo_made, B * TB)
                if i >= 2:
                    pe.wait_ge(w_fixed, e * NFIX + i - 1)
                pe.matmul(bank[4 * e + i % 2][:, :], down[:, e, m, k * P:(k + 1) * P], up[:, e, m, :], start=True, stop=True)\
                    .then_inc(fix_psum, 1)

            def front(b, back=None):
                def behind(j):
                    if back is not None:
                        products(back, j)

                def fixes(lo, hi):
                    if back is None:
                        for i in range(lo, hi):
                            fix(0, i)

                project(b, 0)
                behind(0)
                project(b, 1)
                behind(1)
                energies(b, 0)
                energies(b, 1)
                fixes(0, 4)
                turn_row(b, 0)
                behind(2)
                turn_att(b, 0)
                energies(b, 2)
                turn_row(b, 1)
                turn_att(b, 1)
                energies(b, 3)
                fixes(4, 8)
                turn_row(b, 2)
                behind(3)
                turn_att(b, 2)
                turn_row(b, 3)
                turn_att(b, 3)
                fixes(8, NFIX)

            def body(b, nb):
                if nb is not None:
                    front(nb, b)
                else:
                    for j in range(TB):
                        for i in range(4 * j, min(4 * j + 4, NFIX)):
                            fix(1, i)
                        products(b, j)

            pe.wait_ge(w_lo_made, 1)
            over_batches(pe, front, body)


def experts(nc, xres, stats, norm, wr_raw, temp, ident, bank, outt, Wg, Wu, Wd, w_fix):
    with ExitStack() as ctx:
        def sb(name, shape, dt=F32):
            return ctx.enter_context(nc.sbuf_tensor("e_" + name, shape, dt))

        def sem(name):
            return ctx.enter_context(nc.semaphore("e_" + name))

        xT_hi, xT_lo = sb("xT_hi", [P, KB, B * S], F32R), sb("xT_lo", [P, KB, B * S], F32R)
        raw = [sb("raw_gate", [P, KB, FH]), sb("raw_up", [P, KB, FH]), sb("raw_down", [P, FB, D])]
        w_hi = [[sb(f"{n}_hi{s}", [P, KB, FH] if n != "down" else [P, FB, D], F32R) for s in range(2)] for n in ("gate", "up", "down")]
        w_lo = [[sb(f"{n}_lo{s}", [P, KB, FH] if n != "down" else [P, FB, D], F32R) for s in range(2)] for n in ("gate", "up", "down")]
        silu = sb("silu", [P, FB, S])
        mid = sb("mid", [P, FB, S])
        mid_hi, mid_lo = sb("mid_hi", [P, 2, FB, S], F32R), sb("mid_lo", [P, 2, FB, S], F32R)
        xn = [mid[:, 0, :], mid[:, 1, :], silu[:, 0, :], silu[:, 1, :]]
        zero = sb("zero", [P, 1, 1])
        wr_hi, wr_lo = sb("wr_hi", [P, KB, P], F32R), sb("wr_lo", [P, KB, P], F32R)
        logitsT = sb("logitsT", [P, S])
        mean, var, rstd, tmp = norm
        E3 = [P, NT, NE]
        logits, inh, dist, zone, wts, fb, fbw, index, cand, mask = (
            sb(n, E3) for n in ("logits", "inh", "dist", "zone", "wts", "fb", "fbw", "index", "cand", "mask"))
        best, total = sb("best", [P, NT, 1]), sb("total", [P, NT, 1])
        none, some = sb("none", [P, NT, 1]), sb("some", [P, NT, 1])

        wr_hi_made, wr_lo_made = sem("wr_hi_made"), sem("wr_lo_made")
        index_set, temp_made, zero_set = sem("index_set"), sem("temp_made"), sem("zero_set")
        ln_chain, xn_ready, xT_psum, xT_hi_made, xT_lo_made = (
            sem("ln_chain"), sem("xn_ready"), sem("xT_psum"), sem("xT_hi_made"), sem("xT_lo_made"))
        lT_psum, lT_made, l_psum, l_made = sem("lT_psum"), sem("lT_made"), sem("l_psum"), sem("l_made")
        route_chain, inh_made, dist_made, exps_made = sem("route_chain"), sem("inh_made"), sem("dist_made"), sem("exps_made")
        raw_in = [sem(f"raw_in{m}") for m in range(3)]
        hi_made = [sem(f"hi_made{m}") for m in range(3)]
        lo_made = [sem(f"lo_made{m}") for m in range(3)]
        gate_psum, up_psum, silu_made, mid_made, mid_hi_made, mid_lo_made = (
            [sem(f"{n}{f}") for f in range(FB)] for n in ("gate_psum", "up_psum", "silu_made", "mid_made", "mid_hi_made", "mid_lo_made"))
        d_psum = [sem(f"d_psum{i}") for i in range(2)]
        acc_made = [sem(f"acc_made{j}") for j in range(TB)]
        out_stored = sem("out_stored")

        UNITS = 2 * B

        def rows_then_router(eng, rows, router):
            rows(0)
            with eng.Fori(1, B) as b:
                rows(b)
                router(b - 1)
            router(B - 1)

        block = ctx.enter_context(nc.Block())

        @block.sync
        def _(sp):
            def load(e, src):
                for h in range(2):
                    for m in range(3):
                        if e * 2 + h if isinstance(e, int) else True:
                            sp.wait_ge(lo_made[m], e * 2 + h)
                        w = src(m)
                        if m < 2:
                            w = w[:, h * FH:(h + 1) * FH].rearrange("(k p) f -> p k f", p=P)
                        else:
                            w = w[h * FH:(h + 1) * FH, :].rearrange("(k p) f -> p k f", p=P)
                        sp.dma_start(raw[m][:, :, :], w).then_inc(raw_in[m], 16)

            for e in range(NL):
                load(e, lambda m: w_fix[e, m, :, :])
            with sp.Fori(NL, NE) as e:
                sp.snap(e * (D * FF))
                load(e, lambda m: (Wg, Wu, Wd)[m][bass.ds(e, 1), :, :].rearrange("o a f -> (o a) f"))
            for b in range(B):
                for j in range(TB):
                    sp.wait_ge(acc_made[j], NE * UNITS - (B - 1 - b) + CREDIT)
                sp.dma_start(outt[:, b * TB:(b + 1) * TB, :], xres[:, b * TB:(b + 1) * TB, :]).then_inc(out_stored, 16)
            sp.wait_ge(out_stored, 16 * B)

        @block.gpsimd
        def _(pool):
            for e in range(NE):
                pool.memset(index[:, :, e:e + 1], float(e)).then_inc(index_set, 1)

            def split(e, first):
                for h in range(2):
                    for m in range(3):
                        pool.wait_ge(raw_in[m], (e * 2 + h + 1) * 16)
                        if not first and m == 0:
                            pool.wait_ge(d_psum[1], (e - 1) * 16 + 8 * (h + 1) + CREDIT)
                        pool.tensor_tensor(w_hi[m][h][:, :, :], raw[m][:, :, :], zero[:, :, :].broadcast_to(raw[m].shape), ALU.add)\
                            .then_inc(hi_made[m], 1)
                        pool.wait_ge(hi_made[m], e * 2 + h + 1)
                        pool.tensor_tensor(w_lo[m][h][:, :, :], raw[m][:, :, :], w_hi[m][h][:, :, :].bitcast(F32), ALU.subtract)\
                            .then_inc(lo_made[m], 1)

            pool.memset(zero[:, :, :], 0.0).then_inc(zero_set, 1)
            pool.wait_ge(zero_set, 1)
            split(0, True)
            with pool.Fori(1, NE) as e:
                split(e, False)

        @block.scalar
        def _(act):
            for f in range(FB):
                act.sem_inc(silu_made[f], CREDIT)
                act.sem_inc(mid_hi_made[f], CREDIT)
            act.activation(wr_hi[:, :, :], wr_raw[:, :, :], ACT.Copy).then_inc(wr_hi_made, 1)

            def rows(b):
                for j in range(TB):
                    act.wait_ge(xT_psum, b * TB + j + 1)
                    act.activation(xT_hi[:, :, bass.ds(b * S + j * P, P)], bank[j][:, :].rearrange("p (k t) -> p k t", k=KB), ACT.Copy)\
                        .then_inc(xT_hi_made, 1)

            def router(b):
                act.wait_ge(lT_psum, b + 1)
                act.activation(logitsT[:, :], bank[4][:, :], ACT.Copy).then_inc(lT_made, 1)

            rows_then_router(act, rows, router)
            act.wait_ge(l_made, B + CREDIT)
            act.wait_ge(temp_made, 1)
            act.activation(inh[:, :, :], logits[:, :, :], ACT.Sigmoid, scale=temp[:, 1:2]).then_inc(inh_made, 1)
            act.wait_ge(dist_made, 1)
            act.activation(wts[:, :, :], dist[:, :, :], ACT.Exp, scale=-1.0 / 0.1).then_inc(exps_made, 1)
            act.activation(fb[:, :, :], dist[:, :, :], ACT.Exp, scale=-1.0 / 0.3).then_inc(exps_made, 1)
            with act.Fori(0, NE) as e:
                for u in range(UNITS):
                    n = e * UNITS + u
                    for f in range(FB):
                        act.wait_ge(gate_psum[f], n + 1)
                        act.wait_ge(mid_made[f], n + CREDIT)
                        act.activation(silu[:, f, :], bank[f][:, :], ACT.Silu).then_inc(silu_made[f], 1)
                        act.wait_ge(mid_made[f], n + 1 + CREDIT)
                        act.wait_ge(d_psum[u % 2], e * 16 + u // 2 * 4 + CREDIT)
                        act.activation(mid_hi[:, u % 2, f, :], mid[:, f, :], ACT.Copy).then_inc(mid_hi_made[f], 1)

        @block.vector
        def _(dve):
            for s in (*mid_made, *acc_made, l_made):
                dve.sem_inc(s, CREDIT)
            dve.sem_inc(xT_lo_made, TB)
            dve.reciprocal(temp[:, 1:2], temp[:, 0:1]).then_inc(temp_made, 1)
            dve.wait_ge(wr_hi_made, 1)
            dve.tensor_tensor(wr_lo[:, :, :], wr_raw[:, :, :], wr_hi[:, :, :].bitcast(F32), ALU.subtract).then_inc(wr_lo_made, 1)

            def row(b, j):
                return xres[:, bass.ds(b * TB + j, 1), :].rearrange("p o d -> p (o d)")


            def low(b, j):
                dve.wait_ge(xT_hi_made, b * TB + j + 1)
                cols = bass.ds(b * S + j * P, P)
                dve.tensor_tensor(xT_lo[:, :, cols], bank[j][:, :].rearrange("p (k t) -> p k t", k=KB),
                                  xT_hi[:, :, cols].bitcast(F32), ALU.subtract).then_inc(xT_lo_made, 1)

            def rows(b, behind=None):
                for j in range(TB):
                    if not (isinstance(b, int) and b == 0):
                        dve.wait_ge(xT_psum, b * TB - TB + j + 1)
                    of_row = bass.ds(b * TB + j, 1)
                    dve.tensor_scalar(xn[j], row(b, j), mean[:, of_row], rstd[:, of_row], ALU.subtract, ALU.mult)\
                        .then_inc(xn_ready, 1)
                for j in range(TB):
                    if j == 2 and behind is not None:
                        router(behind)
                    low(b, j)

            def router(b):
                dve.wait_ge(l_psum, b + 1)
                dve.tensor_copy(logits[:, bass.ds(b * TB, TB), :], bank[5][:, :].rearrange("p (t e) -> p t e", t=TB)[:, :, 0:NE])\
                    .then_inc(l_made, 1)

            rows(0)
            chain = Chain(dve, ln_chain)
            last_norm = [t[:, NT - TB:NT] for t in norm]
            moments(dve, stats[:, NT - TB:NT, :], last_norm[0], last_norm[1], last_norm[3], chain)
            rows(1)
            rsqrt_steps(dve, last_norm[1], last_norm[2], last_norm[3], chain)
            with dve.Fori(2, B) as b:
                rows(b, behind=b - 2)
            router(B - 2)
            router(B - 1)

            chain = Chain(dve, route_chain)

            def wide(v):
                return v[:, :, :].broadcast_to(E3)

            def all_(v):
                return v[:, :, :]

            def pick(values):
                chain.then(dve.tensor_reduce(all_(best), all_(values), AX.X, ALU.max))
                chain.then(dve.tensor_tensor(all_(cand), all_(values), wide(best), ALU.is_equal))
                chain.then(dve.scalar_tensor_tensor(out=all_(cand), in0=all_(cand), scalar=-float(NE), in1=all_(index),
                                                    op0=ALU.mult, op1=ALU.add))
                chain.then(dve.tensor_reduce(all_(best), all_(cand), AX.X, ALU.min))
                chain.then(dve.tensor_tensor(all_(cand), all_(cand), wide(best), ALU.is_equal))

            def normalise(values):
                chain.then(dve.tensor_reduce(all_(total), all_(values), AX.X, ALU.add))
                chain.then(dve.tensor_scalar(all_(total), all_(total), 1e-8, None, ALU.max))
                chain.then(dve.reciprocal(all_(total), all_(total)))
                chain.then(dve.tensor_tensor(all_(values), all_(values), wide(total), ALU.mult))

            dve.wait_ge(inh_made, 1)
            chain.then(dve.tensor_scalar(all_(dist), all_(inh), GOLDEN_CENTER, None, ALU.subtract))
            dve.scalar_tensor_tensor(out=all_(dist), in0=all_(dist), scalar=-1.0, in1=all_(dist), op0=ALU.mult, op1=ALU.max)\
                .then_inc(dist_made, 1)
            chain.then(dve.tensor_scalar(all_(zone), all_(inh), GOLDEN_LOWER, None, ALU.is_ge))
            chain.then(dve.scalar_tensor_tensor(out=all_(zone), in0=all_(inh), scalar=GOLDEN_UPPER, in1=all_(zone),
                                                op0=ALU.is_le, op1=ALU.mult))
            dve.wait_ge(exps_made, 2)
            chain.then(dve.tensor_tensor(all_(wts), all_(wts), all_(zone), ALU.mult))
            chain.then(dve.tensor_reduce(all_(total), all_(wts), AX.X, ALU.add))
            chain.then(dve.tensor_scalar(all_(none), all_(total), 1e-8, None, ALU.is_lt))
            chain.then(dve.tensor_scalar(all_(some), all_(none), -1.0, 1.0, ALU.mult, ALU.add))
            dve.wait_ge(index_set, NE)
            pick(fb)
            chain.then(dve.tensor_copy(all_(mask), all_(cand)))
            chain.then(dve.scalar_tensor_tensor(out=all_(fbw), in0=all_(mask), scalar=-2.0, in1=all_(fb), op0=ALU.mult, op1=ALU.add))
            pick(fbw)
            chain.then(dve.tensor_tensor(all_(mask), all_(mask), all_(cand), ALU.add))
            chain.then(dve.tensor_tensor(all_(fbw), all_(fb), all_(mask), ALU.mult))
            normalise(fbw)
            chain.then(dve.tensor_tensor(all_(fbw), all_(fbw), wide(none), ALU.mult))
            chain.then(dve.tensor_tensor(all_(wts), all_(wts), wide(some), ALU.mult))
            chain.then(dve.tensor_tensor(all_(wts), all_(wts), all_(fbw), ALU.add))
            normalise(wts)

            with dve.Fori(0, NE) as e:
                for u in range(UNITS):
                    n = e * UNITS + u
                    b = u % B
                    for f in range(FB):
                        dve.wait_ge(silu_made[f], n + 1 + CREDIT)
                        dve.wait_ge(up_psum[f], n + 1)
                        dve.wait_ge(mid_hi_made[f], n + CREDIT)
                        dve.tensor_tensor(mid[:, f, :], bank[2 + f][:, :], silu[:, f, :], ALU.mult).then_inc(mid_made[f], 1)
                        dve.wait_ge(mid_hi_made[f], n + 1 + CREDIT)
                        dve.tensor_tensor(mid_lo[:, u % 2, f, :], mid[:, f, :], mid_hi[:, u % 2, f, :].bitcast(F32), ALU.subtract)\
                            .then_inc(mid_lo_made[f], 1)
                    for j in range(TB):
                        dve.wait_ge(d_psum[u % 2], e * 16 + u // 2 * 4 + j + 1 + CREDIT)
                        blk = b * TB + j
                        dve.scalar_tensor_tensor(out=xres[:, blk, :], in0=bank[4 + j][:, :],
                                                 scalar=wts[:, blk:blk + 1, bass.ds(e, 1)].rearrange("p a o -> p (a o)"),
                                                 in1=xres[:, blk, :], op0=ALU.mult, op1=ALU.add).then_inc(acc_made[j], 1)

        @block.tensor
        def _(pe):
            for s in d_psum:
                pe.sem_inc(s, CREDIT)
            pe.wait_ge(wr_lo_made, 1)

            def rows(b):
                for j in range(TB):
                    pe.wait_ge(xn_ready, b * TB + j + 1)
                    pe.wait_ge(xT_lo_made, b * TB + j + 1)
                    for k in range(KB):
                        last = pe.transpose(bank[j][:, k * P:(k + 1) * P], xn[j][:, k * P:(k + 1) * P], ident[:, :])
                    last.then_inc(xT_psum, 1)

            def router(b):
                pe.wait_ge(xT_lo_made, b * TB + TB + TB)
                for k in range(KB):
                    cols = bass.ds(b * S, S)
                    last = matmul3(pe, bank[4][:, :], wr_hi[:, k, :], wr_lo[:, k, :], xT_hi[:, k, cols], xT_lo[:, k, cols],
                                   k == 0, k == KB - 1)
                last.then_inc(lT_psum, 1)
                pe.wait_ge(lT_made, b + 1)
                pe.wait_ge(l_made, b + CREDIT)
                for j in range(TB):
                    last = pe.transpose(bank[5][:, j * P:(j + 1) * P], logitsT[:, j * P:(j + 1) * P], ident[:, :])
                last.then_inc(l_psum, 1)

            rows_then_router(pe, rows, router)
            pe.wait_ge(l_made, B + CREDIT)
            with pe.Fori(0, NE) as e:
                for u in range(UNITS):
                    n = e * UNITS + u
                    h, b = divmod(u, B)
                    if b == 0:
                        for m in range(3):
                            pe.wait_ge(lo_made[m], e * 2 + h + 1)
                    for f in range(FB):
                        for m, psum, free in ((0, gate_psum, silu_made), (1, up_psum, mid_made)):
                            pe.wait_ge(free[f], n + CREDIT)
                            for k in range(KB):
                                last = matmul3(pe, bank[2 * m + f][:, :], w_hi[m][h][:, k, f * P:(f + 1) * P],
                                               w_lo[m][h][:, k, f * P:(f + 1) * P], xT_hi[:, k, b * S:(b + 1) * S],
                                               xT_lo[:, k, b * S:(b + 1) * S], k == 0, k == KB - 1)
                            last.then_inc(psum[f], 1)
                    for f in range(FB):
                        pe.wait_ge(mid_lo_made[f], n + 1)
                        for j in range(TB):
                            if f == 0:
                                pe.wait_ge(acc_made[j], n + CREDIT)
                            last = matmul3(pe, bank[4 + j][:, :], mid_hi[:, u % 2, f, j * P:(j + 1) * P],
                                           mid_lo[:, u % 2, f, j * P:(j + 1) * P], w_hi[2][h][:, f, :], w_lo[2][h][:, f, :],
                                           f == 0, f == FB - 1)
                            if f == FB - 1:
                                last.then_inc(d_psum[u % 2], 1)



def kernel(**inputs):
    from concourse import bacc, mybir as mb
    from concourse.bass_utils import run_bass_kernel_spmd as run

    def turned(a, axes):
        return np.ascontiguousarray(np.transpose(np.asarray(a), axes))

    i = {k.removeprefix("L0_"): v for k, v in inputs.items()}
    laid = {
        "x": np.asarray(i["x"]),
        "ctxT": turned(i["ctx_1024"], (0, 2, 1)),
        "w_qkvT": turned(i["attn_w_qkv"], (1, 0)),
        "w_outT": turned(i["attn_w_out"], (1, 0)),
        "b_out": np.asarray(i["attn_b_out"]),
        "wqT": turned(i["xattn_Wq"], (1, 0)), "bq": np.asarray(i["xattn_bq"]),
        "wkT": turned(i["xattn_Wk"], (1, 0)), "bk": np.asarray(i["xattn_bk"]),
        "Wg": np.asarray(i["ffn_Wg"]), "Wu": np.asarray(i["ffn_Wu"]), "Wd": np.asarray(i["ffn_Wd"]),
        "GaT": turned(i["ffn_Ga"], (0, 2, 1)), "Gb": np.asarray(i["ffn_Gb"]),
        "UaT": turned(i["ffn_Ua"], (0, 2, 1)), "Ub": np.asarray(i["ffn_Ub"]),
        "DaT": turned(i["ffn_Da"], (0, 2, 1)), "Db": np.asarray(i["ffn_Db"]),
        "Wr": np.asarray(i["ffn_Wr"]), "temperature": np.asarray(i["ffn_temperature"]),
        "ident_in": np.eye(P, dtype=np.float32),
    }
    nc = bacc.Bacc("TRN2", target_bir_lowering=False, num_devices=1)
    arrays, aps = {}, {}
    for name, a in laid.items():
        a = np.ascontiguousarray(a)
        arrays[name] = a
        aps[name] = nc.dram_tensor(name, a.shape, mb.dt.from_np(a.dtype), kind="ExternalInput").ap()
    out = nc.dram_tensor("out", (B, S, D), F32, kind="ExternalOutput").ap()
    build(nc, **aps, out=out)
    r = run(nc, [arrays], core_ids=[0])
    return r.results[0]["out"]
```
